# Optimizing a Trainium2 kernel written in Bass

```python
import numpy as np
import jax
import jax.numpy as jnp

def _softmax(x, axis=-1):
    return jax.nn.softmax(x, axis=axis)

def _gelu(x):
    return jax.nn.gelu(x, approximate=True)

def _silu(x):
    return jax.nn.silu(x)

def _sigmoid(x):
    return jax.nn.sigmoid(x)

def _layernorm(x, axis=-1, eps=1e-05):
    m = jnp.mean(x, axis=axis, keepdims=True)
    v = jnp.var(x, axis=axis, keepdims=True)
    return (x - m) / jnp.sqrt(v + eps)

def _scatter_add(tgt, idx, src, axis=0):
    return tgt.at[idx].add(src)

def _segment_sum(src, seg, n):
    return jax.ops.segment_sum(src, seg, n)
kernel_name = 'mk_adaln_d1_jaxref_r8_616be5'

def setup_inputs(seed: int=0):
    np.random.seed(seed)
    _w = jnp.asarray

    def _L0_attn_setup():
        import math
        import jax, jax.numpy as jnp
        import numpy as np
        DIM = 128
        N_HEADS = 16
        HEAD_DIM = DIM // N_HEADS
        MAX_SEQ_LEN = 512
        ROPE_BASE = 10000.0

        def _rope_tables(seq_len):
            inv_freq = 1.0 / ROPE_BASE ** (jnp.arange(0, HEAD_DIM, 2, dtype=jnp.float32) / HEAD_DIM)
            t = jnp.arange(seq_len, dtype=jnp.float32)
            freqs = jnp.outer(t, inv_freq)
            return (jnp.cos(freqs), jnp.sin(freqs))

        def _rotate_half(x):
            x1 = x[..., 0::2]
            x2 = x[..., 1::2]
            return jnp.stack([-x2, x1], axis=-1).reshape(x.shape)

        def _apply_rope(xq, xk, cos, sin):
            cos = jnp.repeat(cos, 2, axis=-1)[None, None]
            sin = jnp.repeat(sin, 2, axis=-1)[None, None]
            xq_out = xq * cos + _rotate_half(xq) * sin
            xk_out = xk * cos + _rotate_half(xk) * sin
            return (xq_out, xk_out)
        key = jax.random.key(seed)
        kx, kq, kk, kv, ko = jax.random.split(key, 5)
        B, S = (1, 512)
        x = jax.random.normal(kx, (B, S, DIM), dtype=jnp.float32)
        scale = 0.02
        Wq = jax.random.normal(kq, (DIM, DIM), dtype=jnp.float32) * scale
        Wk = jax.random.normal(kk, (DIM, DIM), dtype=jnp.float32) * scale
        Wv = jax.random.normal(kv, (DIM, DIM), dtype=jnp.float32) * scale
        Wo = jax.random.normal(ko, (DIM, DIM), dtype=jnp.float32) * scale
        return {'x': x, 'Wq': Wq, 'Wk': Wk, 'Wv': Wv, 'Wo': Wo}
    _L0_attn_in = _L0_attn_setup()

    def _L0_ffn_setup():
        import jax, jax.numpy as jnp
        import numpy as np
        DIM = 128
        DEPTH = 6
        HEADS = 16
        DIM_HEAD = 64
        WINDOW = 32
        INNER = HEADS * DIM_HEAD
        DIM_INNER = int(DIM * 4 * 2 / 3)
        QK_SCALE = 8.0

        def shift_tokens(t):
            a, s = jnp.split(t, 2, -1)
            s = jnp.pad(s, ((0, 0), (1, 0), (0, 0)))[:, :-1]
            return jnp.concatenate([a, s], -1)

        def l2norm(t):
            return t / jnp.maximum(jnp.linalg.norm(t, axis=-1, keepdims=True), 1e-12)

        def rotate_half(x):
            x1, x2 = jnp.split(x, 2, -1)
            return jnp.concatenate([-x2, x1], -1)

        def rotary_tables(n):
            half = jnp.arange(0, DIM_HEAD, 2, dtype=jnp.float32)
            inv_freq = 1.0 / 10000.0 ** (half / DIM_HEAD)
            t = jnp.arange(n, dtype=jnp.float32)
            freqs = t[:, None] * inv_freq[None, :]
            freqs = jnp.concatenate([freqs, freqs], -1)
            base_scale = (half + 0.4 * DIM_HEAD) / (1.4 * DIM_HEAD)
            power = (t - n // 2) / (WINDOW // 2)
            scale = base_scale[None, :] ** power[:, None]
            scale = jnp.concatenate([scale, scale], -1)
            return (freqs, scale)

        def local_attention(q, k, v):
            b, h, n, d = q.shape
            w = WINDOW
            nw = n // w
            bq = q.reshape(b, h, nw, w, d)
            bk = k.reshape(b, h, nw, w, d)
            bv = v.reshape(b, h, nw, w, d)

            def look(t):
                p = jnp.pad(t, ((0, 0), (0, 0), (1, 0), (0, 0), (0, 0)))
                return jnp.concatenate([p[:, :, :nw], p[:, :, 1:]], axis=3)
            bk2, bv2 = (look(bk), look(bv))
            seq = jnp.arange(n).reshape(nw, w)
            seq_p = jnp.pad(seq, ((1, 0), (0, 0)), constant_values=-1)
            jt = jnp.concatenate([seq_p[:nw], seq_p[1:]], axis=1)
            it = seq[:, :, None]
            jb = jt[:, None, :]
            mask = (it < jb) | (it > jb + w) | (jb == -1)
            sim = jnp.einsum('bhwie,bhwje->bhwij', bq, bk2) * QK_SCALE
            sim = jnp.where(mask, -jnp.finfo(sim.dtype).max, sim)
            attn = jax.nn.softmax(sim, -1)
            out = jnp.einsum('bhwij,bhwje->bhwie', attn, bv2)
            return out.reshape(b, h, n, d)

        def attn_layer(x, Wqkv, qs, ksc, Wo):
            b, n, _ = x.shape
            qkv = x @ Wqkv
            q, k, v = jnp.split(qkv, 3, -1)
            sh = lambda t: t.reshape(b, n, HEADS, DIM_HEAD).transpose(0, 2, 1, 3)
            q, k, v = (sh(q), sh(k), sh(v))
            q = l2norm(q) * qs
            k = l2norm(k) * ksc
            freqs, scale = rotary_tables(n)
            cos, sin = (jnp.cos(freqs), jnp.sin(freqs))
            q = q * cos * scale + rotate_half(q) * sin * scale
            inv = 1.0 / scale
            k = k * cos * inv + rotate_half(k) * sin * inv
            out = local_attention(q, k, v)
            out = out.transpose(0, 2, 1, 3).reshape(b, n, INNER)
            return out @ Wo

        def ffn_layer(x, g, bln, W1, b1, W2, b2):
            mu = x.mean(-1, keepdims=True)
            var = ((x - mu) ** 2).mean(-1, keepdims=True)
            xn = (x - mu) / jnp.sqrt(var + 1e-05) * g + bln
            hg = xn @ W1 + b1
            a, gate = jnp.split(hg, 2, -1)
            return a * jax.nn.gelu(gate, approximate=False) @ W2 + b2
        key = jax.random.key(seed)
        ks = jax.random.split(key, 8)
        B, N = (2, 256)
        init = lambda k, shape: jax.random.normal(k, shape, jnp.float32) * 0.02
        return {'x': jax.random.normal(ks[0], (B, N, DIM), jnp.float32), 'Wqkv': init(ks[1], (DEPTH, DIM, 3 * INNER)), 'q_scale': jnp.ones((DEPTH, DIM_HEAD), jnp.float32), 'k_scale': jnp.ones((DEPTH, DIM_HEAD), jnp.float32), 'Wo': init(ks[2], (DEPTH, INNER, DIM)), 'ln_g': jnp.ones((DEPTH, DIM), jnp.float32), 'ln_b': jnp.zeros((DEPTH, DIM), jnp.float32), 'W1': init(ks[3], (DEPTH, DIM, 2 * DIM_INNER)), 'b1': jnp.zeros((DEPTH, 2 * DIM_INNER), jnp.float32), 'W2': init(ks[4], (DEPTH, DIM_INNER, DIM)), 'b2': jnp.zeros((DEPTH, DIM), jnp.float32)}
    _L0_ffn_in = _L0_ffn_setup()
    _L0_c = _w((lambda *s: np.random.randn(*s).astype(np.float32) * 0.05)(8, 128))
    _L0_wmod = _w((lambda *s: np.random.randn(*s).astype(np.float32) * 0.05)(128, 6 * 128) * 128 ** (-0.5))
    _d = {'L0_attn_x': _L0_attn_in['x'], 'L0_attn_Wq': _L0_attn_in['Wq'], 'L0_attn_Wk': _L0_attn_in['Wk'], 'L0_attn_Wv': _L0_attn_in['Wv'], 'L0_attn_Wo': _L0_attn_in['Wo'], 'L0_ffn_Wqkv': _L0_ffn_in['Wqkv'], 'L0_ffn_q_scale': _L0_ffn_in['q_scale'], 'L0_ffn_k_scale': _L0_ffn_in['k_scale'], 'L0_ffn_Wo': _L0_ffn_in['Wo'], 'L0_ffn_ln_g': _L0_ffn_in['ln_g'], 'L0_ffn_ln_b': _L0_ffn_in['ln_b'], 'L0_ffn_W1': _L0_ffn_in['W1'], 'L0_ffn_b1': _L0_ffn_in['b1'], 'L0_ffn_W2': _L0_ffn_in['W2'], 'L0_ffn_b2': _L0_ffn_in['b2'], 'L0_c': _L0_c, 'L0_wmod': _L0_wmod}
    _x0 = _d['L0_attn_x']
    _d['L0_attn_x'] = jax.random.normal(jax.random.fold_in(jax.random.key(seed), 1), (8, 512, 128), dtype=_x0.dtype)
    del _x0
    return _d

def reference(L0_attn_x, L0_attn_Wq, L0_attn_Wk, L0_attn_Wv, L0_attn_Wo, L0_ffn_Wqkv, L0_ffn_q_scale, L0_ffn_k_scale, L0_ffn_Wo, L0_ffn_ln_g, L0_ffn_ln_b, L0_ffn_W1, L0_ffn_b1, L0_ffn_W2, L0_ffn_b2, L0_c, L0_wmod):

    def _L0_attn_ref(x, Wq, Wk, Wv, Wo):
        import math
        import jax, jax.numpy as jnp
        import numpy as np
        DIM = 128
        N_HEADS = 16
        HEAD_DIM = DIM // N_HEADS
        MAX_SEQ_LEN = 512
        ROPE_BASE = 10000.0

        def _rope_tables(seq_len):
            inv_freq = 1.0 / ROPE_BASE ** (jnp.arange(0, HEAD_DIM, 2, dtype=jnp.float32) / HEAD_DIM)
            t = jnp.arange(seq_len, dtype=jnp.float32)
            freqs = jnp.outer(t, inv_freq)
            return (jnp.cos(freqs), jnp.sin(freqs))

        def _rotate_half(x):
            x1 = x[..., 0::2]
            x2 = x[..., 1::2]
            return jnp.stack([-x2, x1], axis=-1).reshape(x.shape)

        def _apply_rope(xq, xk, cos, sin):
            cos = jnp.repeat(cos, 2, axis=-1)[None, None]
            sin = jnp.repeat(sin, 2, axis=-1)[None, None]
            xq_out = xq * cos + _rotate_half(xq) * sin
            xk_out = xk * cos + _rotate_half(xk) * sin
            return (xq_out, xk_out)
        B, S, _ = x.shape
        q = (x @ Wq.T).reshape(B, S, N_HEADS, HEAD_DIM).transpose(0, 2, 1, 3)
        k = (x @ Wk.T).reshape(B, S, N_HEADS, HEAD_DIM).transpose(0, 2, 1, 3)
        v = (x @ Wv.T).reshape(B, S, N_HEADS, HEAD_DIM).transpose(0, 2, 1, 3)
        cos, sin = _rope_tables(S)
        q, k = _apply_rope(q, k, cos, sin)
        scores = jnp.einsum('bhqd,bhkd->bhqk', q, k) / math.sqrt(HEAD_DIM)
        mask = jnp.triu(jnp.full((S, S), -jnp.inf, dtype=scores.dtype), k=1)
        scores = scores + mask[None, None]
        probs = jax.nn.softmax(scores, axis=-1)
        out = jnp.einsum('bhqk,bhkd->bhqd', probs, v)
        out = out.transpose(0, 2, 1, 3).reshape(B, S, DIM)
        return out @ Wo.T

    def _L0_ffn_ref(x, Wqkv, q_scale, k_scale, Wo, ln_g, ln_b, W1, b1, W2, b2):
        import jax, jax.numpy as jnp
        import numpy as np
        DIM = 128
        DEPTH = 6
        HEADS = 16
        DIM_HEAD = 64
        WINDOW = 32
        INNER = HEADS * DIM_HEAD
        DIM_INNER = int(DIM * 4 * 2 / 3)
        QK_SCALE = 8.0

        def shift_tokens(t):
            a, s = jnp.split(t, 2, -1)
            s = jnp.pad(s, ((0, 0), (1, 0), (0, 0)))[:, :-1]
            return jnp.concatenate([a, s], -1)

        def l2norm(t):
            return t / jnp.maximum(jnp.linalg.norm(t, axis=-1, keepdims=True), 1e-12)

        def rotate_half(x):
            x1, x2 = jnp.split(x, 2, -1)
            return jnp.concatenate([-x2, x1], -1)

        def rotary_tables(n):
            half = jnp.arange(0, DIM_HEAD, 2, dtype=jnp.float32)
            inv_freq = 1.0 / 10000.0 ** (half / DIM_HEAD)
            t = jnp.arange(n, dtype=jnp.float32)
            freqs = t[:, None] * inv_freq[None, :]
            freqs = jnp.concatenate([freqs, freqs], -1)
            base_scale = (half + 0.4 * DIM_HEAD) / (1.4 * DIM_HEAD)
            power = (t - n // 2) / (WINDOW // 2)
            scale = base_scale[None, :] ** power[:, None]
            scale = jnp.concatenate([scale, scale], -1)
            return (freqs, scale)

        def local_attention(q, k, v):
            b, h, n, d = q.shape
            w = WINDOW
            nw = n // w
            bq = q.reshape(b, h, nw, w, d)
            bk = k.reshape(b, h, nw, w, d)
            bv = v.reshape(b, h, nw, w, d)

            def look(t):
                p = jnp.pad(t, ((0, 0), (0, 0), (1, 0), (0, 0), (0, 0)))
                return jnp.concatenate([p[:, :, :nw], p[:, :, 1:]], axis=3)
            bk2, bv2 = (look(bk), look(bv))
            seq = jnp.arange(n).reshape(nw, w)
            seq_p = jnp.pad(seq, ((1, 0), (0, 0)), constant_values=-1)
            jt = jnp.concatenate([seq_p[:nw], seq_p[1:]], axis=1)
            it = seq[:, :, None]
            jb = jt[:, None, :]
            mask = (it < jb) | (it > jb + w) | (jb == -1)
            sim = jnp.einsum('bhwie,bhwje->bhwij', bq, bk2) * QK_SCALE
            sim = jnp.where(mask, -jnp.finfo(sim.dtype).max, sim)
            attn = jax.nn.softmax(sim, -1)
            out = jnp.einsum('bhwij,bhwje->bhwie', attn, bv2)
            return out.reshape(b, h, n, d)

        def attn_layer(x, Wqkv, qs, ksc, Wo):
            b, n, _ = x.shape
            qkv = x @ Wqkv
            q, k, v = jnp.split(qkv, 3, -1)
            sh = lambda t: t.reshape(b, n, HEADS, DIM_HEAD).transpose(0, 2, 1, 3)
            q, k, v = (sh(q), sh(k), sh(v))
            q = l2norm(q) * qs
            k = l2norm(k) * ksc
            freqs, scale = rotary_tables(n)
            cos, sin = (jnp.cos(freqs), jnp.sin(freqs))
            q = q * cos * scale + rotate_half(q) * sin * scale
            inv = 1.0 / scale
            k = k * cos * inv + rotate_half(k) * sin * inv
            out = local_attention(q, k, v)
            out = out.transpose(0, 2, 1, 3).reshape(b, n, INNER)
            return out @ Wo

        def ffn_layer(x, g, bln, W1, b1, W2, b2):
            mu = x.mean(-1, keepdims=True)
            var = ((x - mu) ** 2).mean(-1, keepdims=True)
            xn = (x - mu) / jnp.sqrt(var + 1e-05) * g + bln
            hg = xn @ W1 + b1
            a, gate = jnp.split(hg, 2, -1)
            return a * jax.nn.gelu(gate, approximate=False) @ W2 + b2
        for i in range(DEPTH):
            x = attn_layer(shift_tokens(x), Wqkv[i], q_scale[i], k_scale[i], Wo[i]) + x
            x = ffn_layer(shift_tokens(x), ln_g[i], ln_b[i], W1[i], b1[i], W2[i], b2[i]) + x
        return x
    x = L0_attn_x
    mod = (_silu(L0_c) @ L0_wmod).reshape(L0_c.shape[0], 6, 1, -1)
    sa, ca, ga, sb, cb, gb = (mod[:, 0], mod[:, 1], mod[:, 2], mod[:, 3], mod[:, 4], mod[:, 5])
    ga = (2 * (ga >= 0) - 1) * jnp.maximum(jnp.abs(ga), 0.25)
    gb = (2 * (gb >= 0) - 1) * jnp.maximum(jnp.abs(gb), 0.25)
    h = _layernorm(x, axis=-1) * (1 + ca) + sa
    x = x + ga * _L0_attn_ref(h, L0_attn_Wq, L0_attn_Wk, L0_attn_Wv, L0_attn_Wo)
    h = _layernorm(x, axis=-1) * (1 + cb) + sb
    x = x + gb * _L0_ffn_ref(h, L0_ffn_Wqkv, L0_ffn_q_scale, L0_ffn_k_scale, L0_ffn_Wo, L0_ffn_ln_g, L0_ffn_ln_b, L0_ffn_W1, L0_ffn_b1, L0_ffn_W2, L0_ffn_b2)
    return x

_drawn_inputs = setup_inputs


def setup_inputs(seed=0):
    import zlib

    import numpy as np

    out = dict(_drawn_inputs(seed))
    spreads = {'L0_ffn_q_scale': (1.0, 0.6),
     'L0_ffn_k_scale': (1.0, 0.6),
     'L0_ffn_ln_g': (1.0, 0.6),
     'L0_ffn_ln_b': (0.0, 0.8),
     'L0_ffn_b1': (0.0, 0.8),
     'L0_ffn_b2': (0.0, 0.653)}
    factors = {'L0_attn_Wq': 8.0,
     'L0_attn_Wk': 8.0,
     'L0_attn_Wv': 8.0,
     'L0_attn_Wo': 8.0,
     'L0_ffn_W1': 7.418,
     'L0_ffn_W2': 7.286}
    for name, (base, spread) in spreads.items():
        noise = np.random.default_rng([zlib.crc32(name.encode()), seed]).standard_normal(out[name].shape)
        drawn = base * np.exp(spread * noise) if base else spread * noise
        out[name] = jnp.asarray(drawn.astype(out[name].dtype))
    for name, factor in factors.items():
        out[name] = (out[name] * factor).astype(out[name].dtype)
    return out
```

```python
import concourse.bass as bass
from concourse import mybir
from contextlib import ExitStack
import numpy as np

BATCH, TOKENS, DIM = 8, 512, 128
P = 128
TILES = TOKENS // P
A_HEADS = 16
A_HDIM = DIM // A_HEADS
DEPTH, HEADS, HDIM, WINDOW = 6, 16, 64, 32
INNER = HEADS * HDIM
FF = int(DIM * 4 * 2 / 3)
PAIRS = HEADS // 2
KEYS = 2 * WINDOW
QKV = 3 * INNER
WCHUNK = QKV // BATCH
NSEQ = DEPTH * BATCH
MASKED = -1e30
FFC = [(0, 128), (128, 128), (256, FF - 256)]
VECS = 9


def constants():
    f = np.float32
    out = {"ident": np.eye(P, dtype=f)}
    inv = (1.0 / 10000.0 ** (np.arange(0, A_HDIM, 2, dtype=f) / A_HDIM)).astype(f)
    ang = np.outer(np.arange(TOKENS, dtype=f), inv).astype(f)
    cos, sin = np.cos(ang).astype(f), np.sin(ang).astype(f)
    row = (np.arange(DIM) % A_HDIM) // 2
    root = f(1.0 / np.sqrt(A_HDIM))
    out["a_rope"] = np.stack([cos.T[row] * root, sin.T[row] * root, cos.T[row], sin.T[row]], 1).astype(f)
    sel = np.zeros((P, 4, 4, P), f)
    for g in range(4):
        for hh in range(4):
            for e in range(4):
                for d in range(A_HDIM):
                    src, dst = A_HDIM * (4 * g + hh) + d, 32 * hh + A_HDIM * e + d
                    sel[src, g, 0 + e % 2, dst] = 1.0
                    sel[src, g, 2 + e // 2, dst] = 1.0
    out["a_sel"] = sel
    causal = np.where(np.arange(P)[None, :] > np.arange(P)[:, None], MASKED, 0.0)
    half = np.arange(0, HDIM, 2, dtype=f)
    inv = (1.0 / 10000.0 ** (half / HDIM)).astype(f)
    t = np.arange(TOKENS, dtype=f)
    fr = (t[:, None] * inv[None, :]).astype(f)
    base = ((half + f(0.4 * HDIM)) / f(1.4 * HDIM)).astype(f)
    scale = (base[None, :] ** ((t - TOKENS // 2) / (WINDOW // 2))[:, None]).astype(f)
    c, s = np.cos(fr).astype(f), np.sin(fr).astype(f)
    rope = np.zeros((2, TOKENS, 2, HDIM), f)
    for i, z in enumerate((scale * f(8.0), f(1.0) / scale)):
        rope[0, :, i, :32], rope[0, :, i, 32:] = c * z, c * z
        rope[1, :, i, :32], rope[1, :, i, 32:] = -s * z, s * z
    out["b_rope"] = rope.reshape(2, TILES, P, 2, HDIM).transpose(2, 0, 1, 3, 4).copy()
    a = (np.arange(P) % WINDOW)[:, None]
    b = np.arange(KEYS)[None, :]
    bad = (b < a) | (b > a + WINDOW)
    first = bad | ((np.arange(P)[:, None] < WINDOW) & (b < WINDOW))
    m = np.concatenate([np.where(bad, MASKED, 0.0), np.where(first, MASKED, 0.0), causal, np.eye(P)], 1)
    out["masks"] = m.astype(mybir.dt.np(mybir.dt.bfloat16))
    return out


class Tally:

    def __init__(self, steady, keep=lambda e: True):
        self.steady = [e for e in steady if keep(e)]
        self.first = [e for e in self.steady if not e.endswith("'")]
        self.last = [e for e in self.steady if e.endswith("'")]

    def at(self, n, name):
        if isinstance(n, int) and n == 0:
            return self.first.index(name) + 1
        if isinstance(n, int) and n == NSEQ:
            return len(self.first) + (NSEQ - 1) * len(self.steady) + self.last.index(name) + 1
        return (n - 1) * len(self.steady) + len(self.first) + self.steady.index(name) + 1

    def before(self, n, name):
        if isinstance(n, int) and n == 0:
            return 0
        if isinstance(n, int) and n == NSEQ:
            return len(self.first) + (NSEQ - 2) * len(self.steady) + self.steady.index(name) + 1
        gap = len(self.steady) - self.steady.index(name)
        assert name in self.first and gap == len(self.first) - self.first.index(name)
        return (n - 1) * len(self.steady) + len(self.first) - gap + 1


def fill_order():
    out = []
    for j in range(TILES):
        t, pr = ((j - 1) % TILES, "'" if j == 0 else "")
        out += ["spread'"] if j == 3 else []
        out += [f"V{t}{i}{pr}" for i in range(4)]
        out += {1: ["wo'"], 2: ["mean'"], 3: [f"up{i}'" for i in range(6)]}.get(j, [])
        out += [f"P{t}{i}{pr}" for i in range(2)]
        out += ["var'"] if j == 2 else []
        out += [f"O{t}{i}{pr}" for i in range(2)]
        out += [f"T{j}0", f"T{j}1"] + (["down'"] if j == 3 else []) + [f"T{j}2", f"T{j}3"]
    return out


FILLS = fill_order()
BY_VECTOR = ("wo'", "mean'", "var'", "spread'", "up3'", "up4'", "up5'", "down'")
FILL = Tally(FILLS)
ACT_FREE = Tally(FILLS, lambda e: e not in BY_VECTOR)
DVE_FREE = Tally(FILLS, lambda e: e in BY_VECTOR)


def bank_of(name):
    return FILLS.index(name) % 2


def program(nc, t_in, out):
    f32, f32r, bf16 = mybir.dt.float32, mybir.dt.float32r, mybir.dt.bfloat16
    ALU, ACT, AX = mybir.AluOpType, mybir.ActivationFunctionType, mybir.AxisListType

    def need(eng, sem, value):
        if not isinstance(value, int) or value > 0:
            eng.wait_ge(sem, value)

    ctx = ExitStack()
    with ctx:
        def alloc(stack):
            return (lambda n, s, d=f32: stack.enter_context(nc.sbuf_tensor(n, s, d)),
                    lambda n, s, d=f32: stack.enter_context(nc.psum_tensor(n, s, d)),
                    lambda n: stack.enter_context(nc.semaphore(n)))

        sb, _, _ = alloc(ctx)
        resT = sb("resT", [P, BATCH, TOKENS])
        xtok = sb("xtok", [P, BATCH * TILES, DIM])
        ident = sb("ident", [P, P])
        masks = sb("masks", [P, 2 * KEYS + 2 * P], bf16)
        win_mask = [masks[:, KEYS:2 * KEYS]] + [masks[:, 0:KEYS]] * (TILES - 1)
        causal_mask = masks[:, 2 * KEYS:2 * KEYS + P]
        ident_bf = masks[:, 2 * KEYS + P:2 * KEYS + 2 * P]
        mod = sb("mod", [P, 6, BATCH])
        vecs = sb("vecs", [P, VECS, DEPTH])

        part_a(nc, t_in, alloc, need, resT, xtok, ident, masks, causal_mask, ident_bf, mod, vecs)
        part_b(nc, t_in, alloc, need, resT, ident, win_mask, ident_bf, vecs)
        part_c(nc, out, alloc, need, resT, xtok, ident, mod)


NEWTON = 3
RSQRT_STEPS = 1 + 3 * NEWTON


def rsqrt(nc, dve, x, y, t, sem, base):
    i32, ALU = mybir.dt.int32, mybir.AluOpType
    nc.vector.tensor_scalar(y.bitcast(i32), x.bitcast(i32), -0.5, float(0x5F3759DF), ALU.mult, ALU.add).then_inc(sem, 1)
    for i in range(NEWTON):
        dve.wait_ge(sem, base + 3 * i + 1)
        nc.vector.tensor_tensor(t, y, y, ALU.mult).then_inc(sem, 1)
        dve.wait_ge(sem, base + 3 * i + 2)
        nc.vector.scalar_tensor_tensor(t, t, -0.5, x, ALU.mult, ALU.mult).then_inc(sem, 1)
        dve.wait_ge(sem, base + 3 * i + 3)
        nc.vector.scalar_tensor_tensor(y, t, 1.5, y, ALU.add, ALU.mult).then_inc(sem, 1)
    dve.wait_ge(sem, base + RSQRT_STEPS)


def part_a(nc, t_in, alloc, need, resT, xtok, ident, masks, causal_mask, ident_bf, mod, vecs):
    f32, f32r, bf16 = mybir.dt.float32, mybir.dt.float32r, mybir.dt.bfloat16
    ALU, ACT, AX = mybir.AluOpType, mybir.ActivationFunctionType, mybir.AxisListType
    ctx = ExitStack()
    with ctx:
        sb, ps, sem = alloc(ctx)
        w_raw = sb("w_raw", [P, 4, P])
        wT = sb("wT", [P, 6, P])
        wmod = sb("wmod", [P, 6, P])
        c_row = sb("c_row", [BATCH, P])
        cT = sb("cT", [P, BATCH])
        sgn = sb("sgn", [P, 2, BATCH])
        rope = sb("rope", [P, 4, TOKENS])
        sel_raw = sb("sel_raw", [P, 16, P])
        sel = sb("sel", [P, 16, P], f32r)
        rows = sb("rows", [DEPTH, 3 * P + 2 * FF])
        stats = sb("stats", [P, TILES, 6])
        mv = sb("mv", [P, TILES, 2])
        rstd = sb("rstd", [P, TILES])
        var = sb("var", [P, TILES])
        var_t = sb("var_t", [P, TILES])
        xn = sb("xn", [P, TILES, P])
        hT = sb("hT", [P, TOKENS])
        cur = sb("cur", [P, 6])
        rot1 = sb("rot1", [P, 2, TOKENS])
        rot2 = sb("rot2", [P, 2, TOKENS])
        qk_hi = sb("qk_hi", [P, 2, TOKENS], f32r)
        qk_lo = sb("qk_lo", [P, 2, TOKENS], f32r)
        qkG = sb("qkG", [P, 2, 4, TOKENS], f32r)
        vtok = sb("vtok", [P, TILES, P])
        negmax = sb("negmax", [P, A_HEADS * TILES])
        den = sb("den", [P, TILES, A_HEADS])
        rden = sb("rden", [P, TILES, A_HEADS])
        prob = sb("prob", [P, 3, TOKENS])
        probT = sb("probT", [P, 2, TOKENS])
        otok = sb("otok", [P, TILES, P])
        oT = sb("oT", [P, TOKENS])
        yT = sb("yT", [P, TOKENS])

        sc = [ps(f"sc{i}", [P, TOKENS]) for i in range(3)]
        pt = [ps(f"pt{i}", [P, TOKENS]) for i in range(2)]
        po = ps("po", [P, TOKENS])
        gen = [ps(f"gen{i}", [P, TOKENS]) for i in range(2)]

        loaded = sem("loaded")
        x_in = sem("x_in")
        tr_w = sem("tr_w"); tr_v = sem("tr_v"); ev_w = sem("ev_w"); silu_d = sem("silu_d")
        mod_p = sem("mod_p"); mod_e = sem("mod_e"); mod_d = sem("mod_d"); sel_d = sem("sel_d")
        rot_w = sem("rot_w"); vec_e = sem("vec_e"); vec_z = sem("vec_z")
        st = sem("st"); passed = sem("passed"); rstd_d = sem("rstd_d"); nrm = sem("nrm"); cur_d = sem("cur_d")
        g_fill = sem("g_fill"); g_act = sem("g_act"); g_dve = sem("g_dve")
        rope_m = sem("rope_m"); rope_a = sem("rope_a"); hi_d = sem("hi_d"); lo_d = sem("lo_d")
        s_full = sem("s_full"); m_d = sem("m_d"); e_d = sem("e_d"); t_full = sem("t_full")
        t_act = sem("t_act"); t_dve = sem("t_dve"); o_full = sem("o_full")
        rd_d = sem("rd_d"); ot_d = sem("ot_d"); x_d = sem("x_d")
        block = ctx.enter_context(nc.Block())

        units = [(h, j) for h in range(A_HEADS) for j in range(TILES)]
        NU = len(units)
        by_act = [h % 3 == 0 for h, j in units]
        act_count = [sum(by_act[:i + 1]) for i in range(NU)]
        dve_count = [i + 1 - act_count[i] for i in range(NU)]
        gens = ["h", "q", "qr", "k", "kr", "v"] + [f"g{i}" for i in range(8)] + ["oT", "y", "yt", "h2"]
        gen_act = [g in ("h", "v", "oT", "y", "h2") or g[0] == "g" for g in gens]
        NG = len(gens)
        NA = sum(gen_act)

        def gfull(b, name):
            return b * NG + gens.index(name) + 1

        def gfree(b, i):
            if i < 0:
                b, i = b - 1, i + NG
            if gen_act[i]:
                return g_act, b * NA + sum(gen_act[:i + 1])
            return g_dve, b * (NG - NA) + i + 1 - sum(gen_act[:i + 1])

        xv = t_in["L0_attn_x"].rearrange("b (t p) d -> p (b t) d", p=P)

        @block.sync
        def _(sp):
            sp.dma_start(c_row[:, :], t_in["L0_c"]).then_inc(loaded, 16)
            for i, w in enumerate(("Wq", "Wk", "Wv", "Wo")):
                sp.dma_start(w_raw[:, i, :], t_in["L0_attn_" + w]).then_inc(loaded, 16)
            sp.dma_start(ident[:, :], t_in["ident"]).then_inc(loaded, 16)
            sp.dma_start(masks[:, :], t_in["masks"]).then_inc(loaded, 16)
            sp.dma_start(wmod[:, :, :], t_in["L0_wmod"].rearrange("k (m f) -> k m f", m=6)).then_inc(loaded, 16)
            sp.dma_start(rows[:, 0:P], t_in["L0_ffn_ln_g"]).then_inc(loaded, 16)
            sp.dma_start(rows[:, P:2 * P], t_in["L0_ffn_ln_b"]).then_inc(loaded, 16)
            sp.dma_start(rows[:, 2 * P:3 * P], t_in["L0_ffn_b2"]).then_inc(loaded, 16)
            sp.dma_start(rows[:, 3 * P:], t_in["L0_ffn_b1"]).then_inc(loaded, 16)
            sp.dma_start(rope[:, :, :], t_in["a_rope"]).then_inc(loaded, 16)
            sp.dma_start(sel_raw[:, :, :], t_in["a_sel"].rearrange("p g s f -> p (g s) f")).then_inc(loaded, 16)
            sp.dma_start(xtok[:, :, :], xv).then_inc(x_in, 16)
        NLOAD = 14 * 16
        pieces = [(0, P), (P, P), (2 * P, P)] + [(3 * P + o, w) for o, w in FFC] + \
                 [(3 * P + FF + o, w) for o, w in FFC]

        @block.tensor
        def _(pe):
            pe.wait_ge(loaded, NLOAD)
            for i in range(4):
                nc.tensor.transpose(sc[0][:, i * P:(i + 1) * P], w_raw[:, i, :], ident[:, :])
            nc.tensor.transpose(sc[1][:, 0:BATCH], c_row[:, :], ident[0:BATCH, 0:BATCH]).then_inc(tr_w, 1)
            for i, (o, w) in enumerate(pieces):
                last = nc.tensor.transpose(sc[2][0:w, 8 * i:8 * i + DEPTH], rows[:, o:o + w],
                                           ident[0:DEPTH, 0:DEPTH])
            last.then_inc(tr_v, 1)
            pe.wait_ge(silu_d, 1)
            for m in range(6):
                last = nc.tensor.matmul(gen[0][:, m * BATCH:(m + 1) * BATCH], wmod[:, m, :], cT[:, :],
                                        start=True, stop=True)
            last.then_inc(mod_p, 1)
            pe.wait_ge(mod_d, 5)
            pe.wait_ge(rot_w, 4)
            pe.wait_ge(sel_d, 1)
            pe.wait_ge(vec_e, VECS)

            with nc.tensor.Fori(0, BATCH) as b:
                def fill(name, body):
                    i = gens.index(name)
                    if i >= 2:
                        pe.wait_ge(*gfree(b, i - 2))
                    body(gen[i % 2]).then_inc(g_fill, 1)

                def transposes4(src):
                    def body(bank):
                        for j in range(TILES):
                            last = nc.tensor.transpose(bank[:, j * P:(j + 1) * P], src(j), ident[:, :])
                        return last
                    return body

                def project(w, src):
                    return lambda bank: nc.tensor.matmul(bank[:, :], w, src, start=True, stop=True)

                pe.wait_ge(nrm, b * 8 + 4)
                fill("h", transposes4(lambda j: xn[:, j, :]))
                s, v = gfree(b, gens.index("h"))
                pe.wait_ge(s, v)
                fill("q", project(wT[:, 0, :], hT[:, :]))
                fill("qr", project(wT[:, 4, :], hT[:, :]))
                fill("k", project(wT[:, 1, :], hT[:, :]))
                fill("kr", project(wT[:, 5, :], hT[:, :]))

                def values(bank):
                    for j in range(TILES):
                        last = nc.tensor.matmul(bank[:, j * P:(j + 1) * P], hT[:, j * P:(j + 1) * P],
                                                wT[:, 2, :], start=True, stop=True)
                    return last
                fill("v", values)
                pe.wait_ge(lo_d, b * 2 + 2)
                for g in range(4):
                    for c in range(2):
                        def stack(bank, g=g, c=c):
                            nc.tensor.matmul(bank[:, :], sel[:, 4 * g + 2 * c, :], qk_hi[:, c, :],
                                             start=True, stop=False)
                            return nc.tensor.matmul(bank[:, :], sel[:, 4 * g + 2 * c + 1, :], qk_lo[:, c, :],
                                                    start=False, stop=True)
                        fill(f"g{2 * g + c}", stack)

                def scores(i):
                    h, j = units[i]
                    g, hh = divmod(h, 4)
                    if j == 0 and hh == 0:
                        pe.wait_ge(*gfree(b, gens.index(f"g{2 * g + 1}")))
                    if i >= 3:
                        pe.wait_ge(e_d, b * NU + i - 2)
                    r = slice(32 * hh, 32 * hh + 32)
                    bank, width = sc[i % 3], (j + 1) * P
                    nc.tensor.matmul(bank[:, 0:width], qkG[r, 0, g, j * P:(j + 1) * P],
                                     qkG[r, 1, g, 0:width], start=True, stop=False)
                    nc.tensor.matmul(bank[:, j * P:width], ident_bf, causal_mask,
                                     start=False, stop=True).then_inc(s_full, 1)

                def attend(i):
                    h, j = units[i]
                    pe.wait_ge(e_d, b * NU + i + 1)
                    if i >= 2:
                        if by_act[i - 2]:
                            pe.wait_ge(t_act, b * act_count[-1] + act_count[i - 2])
                        else:
                            pe.wait_ge(t_dve, b * dve_count[-1] + dve_count[i - 2])
                    for k in range(j + 1):
                        last = nc.tensor.transpose(pt[i % 2][:, k * P:(k + 1) * P],
                                                   prob[:, i % 3, k * P:(k + 1) * P], ident[:, :])
                    last.then_inc(t_full, 1)

                def weigh(i):
                    h, j = units[i]
                    if by_act[i]:
                        pe.wait_ge(t_act, b * act_count[-1] + act_count[i])
                    else:
                        pe.wait_ge(t_dve, b * dve_count[-1] + dve_count[i])
                    if i == 0:
                        pe.wait_ge(*gfree(b, gens.index("v")))
                    for k in range(j + 1):
                        last = nc.tensor.matmul(po[:, j * P + A_HDIM * h:j * P + A_HDIM * (h + 1)],
                                                probT[:, i % 2, k * P:(k + 1) * P],
                                                vtok[:, k, A_HDIM * h:A_HDIM * (h + 1)],
                                                start=(k == 0), stop=(k == j))
                    last.then_inc(o_full, 1)

                for i in range(NU + 3):
                    if i < NU:
                        scores(i)
                    if 0 <= i - 2 < NU:
                        attend(i - 2)
                    if 0 <= i - 3 < NU:
                        weigh(i - 3)
                pe.wait_ge(ot_d, b + 1)
                fill("oT", transposes4(lambda j: otok[:, j, :]))
                s, v = gfree(b, gens.index("oT"))
                pe.wait_ge(s, v)
                fill("y", project(wT[:, 3, :], oT[:, :]))
                s, v = gfree(b, gens.index("y"))
                pe.wait_ge(s, v)
                fill("yt", transposes4(lambda j: yT[:, j * P:(j + 1) * P]))
                pe.wait_ge(nrm, b * 8 + 8)
                fill("h2", transposes4(lambda j: xn[:, j, :]))
                pe.wait_ge(*gfree(b, gens.index("h2")))

        @block.scalar
        def _(act):
            act.wait_ge(tr_w, 1)
            nc.scalar.activation(wT[:, 0:4, :], sc[0][:, :].rearrange("p (i f) -> p i f", i=4), ACT.Copy).then_inc(ev_w, 1)
            nc.scalar.activation(cT[:, :], sc[1][:, 0:BATCH], ACT.Silu).then_inc(silu_d, 1)
            act.wait_ge(loaded, NLOAD)
            nc.scalar.activation(sel[:, :, :], sel_raw[:, :, :], ACT.Copy).then_inc(sel_d, 1)
            with nc.scalar.Fori(0, BATCH) as b:
                def fill(name, *args, **kw):
                    act.wait_ge(g_fill, gfull(b, name))
                    nc.scalar.activation(*args, **kw).then_inc(g_act, 1)

                act.wait_ge(cur_d, b + 1)
                fill("h", hT[:, :], gen[0][:, :], ACT.Identity, bias=cur[:, 0:1], scale=cur[:, 1:2])
                for c in range(2):
                    act.wait_ge(rope_a, b * 2 + c + 1)
                    nc.scalar.activation(qk_hi[:, c, :], rot1[:, c, :], ACT.Copy).then_inc(hi_d, 1)
                fill("v", vtok[:, :, :], gen[gens.index("v") % 2][:, :].rearrange("p (t f) -> p t f", t=TILES), ACT.Copy)
                for g in range(4):
                    for c in range(2):
                        name = f"g{2 * g + c}"
                        fill(name, qkG[:, c, g, :], gen[gens.index(name) % 2][:, :], ACT.Copy)

                def empty(i):
                    h, j = units[i]
                    act.wait_ge(t_full, b * NU + i + 1)
                    if i >= 2:
                        act.wait_ge(o_full, b * NU + i - 1)
                    nc.scalar.activation(probT[:, i % 2, 0:(j + 1) * P], pt[i % 2][:, 0:(j + 1) * P],
                                         ACT.Copy).then_inc(t_act, 1)

                for i, (h, j) in enumerate(units):
                    act.wait_ge(m_d, b * NU + i + 1)
                    if i >= 3:
                        act.wait_ge(t_full, b * NU + i - 2)
                    nc.scalar.activation(prob[:, i % 3, 0:(j + 1) * P], sc[i % 3][:, 0:(j + 1) * P], ACT.Exp,
                                         bias=negmax[:, i:i + 1], accum_out=den[:, j, h:h + 1]).then_inc(e_d, 1)
                    if i >= 1 and by_act[i - 1]:
                        empty(i - 1)
                if by_act[NU - 1]:
                    empty(NU - 1)
                fill("oT", oT[:, :], gen[gens.index("oT") % 2][:, :], ACT.Copy)
                fill("y", yT[:, :], gen[gens.index("y") % 2][:, :], ACT.Copy, scale=cur[:, 2:3])
                fill("h2", resT[:, bass.ds(b, 1), :], gen[gens.index("h2") % 2][:, :].rearrange("p (o t) -> p o t", o=1), ACT.Identity,
                     bias=cur[:, 3:4], scale=cur[:, 4:5])

        @block.vector
        def _(dve):
            nc.vector.memset(vecs[:, :, :], 0.0).then_inc(vec_z, 1)
            dve.wait_ge(ev_w, 1)
            for i in range(2):
                src = wT[:, i, :].rearrange("p (a two) -> p a two", two=2)
                dst = wT[:, 4 + i, :].rearrange("p (a two) -> p a two", two=2)
                nc.vector.tensor_scalar(dst[:, :, 0:1], src[:, :, 1:2], -1.0, None, ALU.mult).then_inc(rot_w, 1)
                nc.vector.tensor_copy(dst[:, :, 1:2], src[:, :, 0:1]).then_inc(rot_w, 1)
            dve.wait_ge(tr_v, 1)
            dve.wait_ge(vec_z, 1)
            for i, (o, w) in enumerate(pieces):
                nc.vector.tensor_copy(vecs[0:w, i, :], sc[2][0:w, 8 * i:8 * i + DEPTH]).then_inc(vec_e, 1)
            dve.wait_ge(mod_p, 1)
            nc.vector.tensor_copy(mod[:, :, :], gen[0][:, 0:6 * BATCH].rearrange("p (m b) -> p m b", m=6)).then_inc(mod_e, 1)
            dve.wait_ge(mod_e, 1)
            both = mod[:, 1:5:3, :]
            gates = mod[:, 2:6:3, :]
            nc.vector.tensor_scalar(both, both, 1.0, None, ALU.add).then_inc(mod_d, 1)
            nc.vector.tensor_scalar(sgn[:, :, :], gates, 0.0, 2.0, ALU.is_ge, ALU.mult).then_inc(mod_d, 1)
            dve.wait_ge(mod_d, 2)
            nc.vector.tensor_scalar(sgn[:, :, :], sgn[:, :, :], -1.0, None, ALU.add).then_inc(mod_d, 1)
            dve.wait_ge(mod_d, 3)
            nc.vector.tensor_tensor(gates, gates, sgn[:, :, :], ALU.mult).then_inc(mod_d, 1)
            dve.wait_ge(mod_d, 4)
            nc.vector.scalar_tensor_tensor(gates, gates, 0.25, sgn[:, :, :], ALU.max, ALU.mult).then_inc(mod_d, 1)
            dve.wait_ge(mod_d, 5)
            dve.wait_ge(x_in, 16)
            with nc.vector.Fori(0, BATCH) as b:
                nc.vector.tensor_copy(cur[:, :].rearrange("p (m o) -> p m o", o=1), mod[:, :, bass.ds(b, 1)]).then_inc(cur_d, 1)

                def norm(half):
                    base = b * 18 + 9 * half
                    for j in range(TILES):
                        nc.vector.bn_stats(stats[:, j:j + 1, :], xtok[:, bass.ds(b * TILES + j, 1), :]).then_inc(st, 1)
                    dve.wait_ge(st, base + 4)
                    dve.sem_inc(passed, 1)
                    for j in range(TILES):
                        nc.vector.bn_aggr(mv[:, j, :], stats[:, j, :]).then_inc(st, 1)
                    dve.wait_ge(st, base + 8)
                    nc.vector.tensor_scalar(var[:, :].rearrange("p (t o) -> p t o", o=1), mv[:, :, 1:2], 1e-5, None,
                                            ALU.add).then_inc(st, 1)
                    dve.wait_ge(st, base + 9)
                    rsqrt(nc, dve, var[:, :], rstd[:, :], var_t[:, :], rstd_d, (b * 2 + half) * RSQRT_STEPS)
                    for j in range(TILES):
                        nc.vector.tensor_scalar(xn[:, j:j + 1, :], xtok[:, bass.ds(b * TILES + j, 1), :], mv[:, j, 0:1],
                                                rstd[:, j:j + 1], ALU.subtract, ALU.mult).then_inc(nrm, 1)

                norm(0)
                for c, (name, rname) in enumerate((("q", "qr"), ("k", "kr"))):
                    dve.wait_ge(g_fill, gfull(b, name))
                    nc.vector.tensor_tensor(rot1[:, c, :], gen[gens.index(name) % 2][:, :], rope[:, 2 * c, :],
                                            ALU.mult).then_inc(g_dve, 1)
                    dve.wait_ge(g_fill, gfull(b, rname))
                    nc.vector.tensor_tensor(rot2[:, c, :], gen[gens.index(rname) % 2][:, :], rope[:, 2 * c + 1, :],
                                            ALU.mult).then_inc(g_dve, 1)
                    dve.wait_ge(*gfree(b, gens.index(rname)))
                    nc.vector.tensor_tensor(rot1[:, c, :], rot1[:, c, :], rot2[:, c, :], ALU.add).then_inc(rope_a, 1)
                for c in range(2):
                    dve.wait_ge(hi_d, b * 2 + c + 1)
                    nc.vector.tensor_tensor(qk_lo[:, c, :], rot1[:, c, :], qk_hi[:, c, :].bitcast(f32),
                                            ALU.subtract).then_inc(lo_d, 1)

                def empty(i):
                    h, j = units[i]
                    dve.wait_ge(t_full, b * NU + i + 1)
                    if i >= 2:
                        dve.wait_ge(o_full, b * NU + i - 1)
                    nc.vector.tensor_copy(probT[:, i % 2, 0:(j + 1) * P], pt[i % 2][:, 0:(j + 1) * P]).then_inc(t_dve, 1)

                for i, (h, j) in enumerate(units):
                    dve.wait_ge(s_full, b * NU + i + 1)
                    nc.vector.tensor_reduce(negmax[:, i:i + 1], sc[i % 3][:, 0:(j + 1) * P], AX.X, ALU.max,
                                            negate=True).then_inc(m_d, 1)
                    if i >= 2 and not by_act[i - 2]:
                        empty(i - 2)
                for i in (NU - 2, NU - 1):
                    if not by_act[i]:
                        empty(i)
                dve.wait_ge(e_d, (b + 1) * NU)
                nc.vector.reciprocal(rden[:, :, :], den[:, :, :]).then_inc(rd_d, 1)
                dve.wait_ge(rd_d, b + 1)
                dve.wait_ge(o_full, (b + 1) * NU)
                nc.vector.tensor_tensor(otok[:, :, :].rearrange("p t (h d) -> p t h d", h=A_HEADS),
                                        po[:, :].rearrange("p (t h d) -> p t h d", t=TILES, h=A_HEADS),
                                        rden[:, :, :].rearrange("p t (h o) -> p t h o", o=1).broadcast_to([P, TILES, A_HEADS, A_HDIM]),
                                        ALU.mult).then_inc(ot_d, 1)
                dve.wait_ge(g_fill, gfull(b, "yt"))
                xb = xtok[:, bass.ds(b * TILES, TILES), :]
                nc.vector.tensor_tensor(xb, gen[gens.index("yt") % 2][:, :].rearrange("p (t f) -> p t f", t=TILES), xb,
                                        ALU.add).then_inc(g_dve, 1)
                dve.wait_ge(*gfree(b, gens.index("yt")))
                dve.sem_inc(passed, 1)
                norm(1)
                dve.wait_ge(*gfree(b, gens.index("h2")))


def part_b(nc, t_in, alloc, need, resT, ident, win_mask, ident_bf, vecs):
    f32, f32r, bf16 = mybir.dt.float32, mybir.dt.float32r, mybir.dt.bfloat16
    ALU, ACT, AX = mybir.AluOpType, mybir.ActivationFunctionType, mybir.AxisListType
    ctx = ExitStack()
    with ctx:
        sb, ps, sem = alloc(ctx)
        w_raw = sb("wqkv_raw", [P, WCHUNK])
        w_hi = sb("wqkv_hi", [P, 2, QKV], f32r)
        w_lo = sb("wqkv_lo", [P, 2, QKV], f32r)
        wo = sb("wo", [P, PAIRS, DIM])
        w1 = sb("w1", [P, 2 * FF])
        w2 = sb("w2", [P, 3, DIM])
        vec = sb("vec", [P, VECS])
        rope0 = sb("rope0", [P, 2, TILES, 2, HDIM])
        rope = sb("rope_b", [P, 2, TILES, 2, HDIM])
        qks = sb("qks", [P, 2, HDIM])
        mean_w = sb("mean_w", [P, P])
        xa_hi = sb("xa_hi", [P, WINDOW + TOKENS], f32r)
        xa_lo = sb("xa_lo", [P, WINDOW + TOKENS], f32r)
        xsw = sb("xsw", [P, 2, 2, TILES, P], f32r)
        squares = sb("squares", [P, INNER])
        ssum = sb("ssum", [P, 2, HEADS])
        rnorm = sb("rnorm", [P, 2, HEADS])
        rtmp = sb("rtmp", [P, 2, HEADS])
        var = sb("var_b", [P, 3, TILES])
        qkn = sb("qkn", [P, 2, INNER])
        rc = sb("rc", [P, 2, INNER])
        rs = sb("rs", [P, 2, INNER])
        qT = sb("qT", [P, PAIRS, P])
        kT = sb("kT", [P, PAIRS, WINDOW + TOKENS])
        prob = sb("prob_b", [P, PAIRS, 2, KEYS])
        prob_s = prob[:, :, :, :].rearrange("p q s k -> p s q k")
        rmax = sb("rmax", [P, 2, PAIRS])
        rsum = sb("rsum", [P, PAIRS, 2])
        rinv = sb("rinv", [P, PAIRS, 2])
        pT = sb("pT", [P, PAIRS, P])
        val = sb("val", [P, 2, 2, PAIRS, HDIM])
        oT = sb("oT_b", [P, PAIRS, TOKENS])
        x1 = sb("x1", [P, TOKENS])
        xs = sb("xs", [P, TOKENS])
        xc = sb("xc", [P, TOKENS])
        hid = sb("hid", [P, 3, TOKENS])
        xq = hid[:, 0, :]
        dev = hid[:, 1, :].rearrange("p (t f) -> p t f", t=TILES)

        proj = [ps(f"proj{c}", [P, INNER]) for c in range(2)]
        ring = [ps(f"ring{i}", [P, 512]) for i in range(2)]
        scr = ps("scr", [P, 2, PAIRS, KEYS])

        qks_in = sem("qks_in"); consts_in = sem("consts_in"); raw_in = sem("raw_in"); wo_in = sem("wo_in")
        w1_in = sem("w1_in"); w2_in = sem("w2_in")
        zeroed = sem("zeroed")
        w_hi_done = sem("w_hi_done"); w_lo_done = sem("w_lo_done")
        x_hi_done = sem("x_hi_done"); x_lo_done = sem("x_lo_done")
        swap_done = sem("swap_done")
        pe_passed = sem("pe_passed"); pool_passed = sem("pool_passed")
        rope_done = sem("rope_done")
        proj_full = sem("proj_full"); sq_done = sem("sq_done"); ss_done = sem("ss_done")
        clamp_done = sem("clamp_done"); spread_done = sem("spread_done")
        rn_done = sem("rn_done"); qkn_done = sem("qkn_done"); rc_done = sem("rc_done"); rs_done = sem("rs_done")
        fill = sem("fill"); act_free = sem("act_free"); dve_free = sem("dve_free")
        scr_full = sem("scr_full"); max_done = sem("max_done"); sub_done = sem("sub_done")
        exp_done = sem("exp_done"); sum_done = sem("sum_done"); inv_done = sem("inv_done")
        prob_done = sem("prob_done")
        xs_done = sem("xs_done"); xq_done = sem("xq_done"); rstd_done = sem("rstd_done")
        h_done = sem("h_done")
        vec_done = sem("vec_done")
        block = ctx.enter_context(nc.Block())

        wqkv = t_in["L0_ffn_Wqkv"]
        half_tokens = TOKENS // 2
        stage = [[(slice(0, 64), WINDOW, 0, half_tokens), (slice(64, P), WINDOW + 1, 0, half_tokens - 1)],
                 [(slice(0, 64), WINDOW + half_tokens, half_tokens, half_tokens),
                  (slice(64, P), WINDOW + half_tokens, half_tokens - 1, half_tokens)]]

        def pipelined(eng, engine, body):
            body(0, True, False)
            with engine.Fori(1, NSEQ) as n:
                body(n, True, True)
            body(NSEQ, False, True)

        def free_before(n, name):
            kind = FILL.first if isinstance(n, int) and n == 0 else \
                FILL.last if isinstance(n, int) and n == NSEQ else FILL.steady
            i = kind.index(name)
            for k in range(i - 1, -1, -1):
                if bank_of(kind[k]) == bank_of(name):
                    e = kind[k]
                    return (dve_free, DVE_FREE.at(n, e)) if e in BY_VECTOR else (act_free, ACT_FREE.at(n, e))
            if kind is FILL.first:
                return act_free, 0
            e = [x for x in FILL.steady if bank_of(x) == bank_of(name)][-1]
            return act_free, ACT_FREE.before(n, e)

        @block.sync
        def _(sp):
            sp.dma_start(rope0[:, :, :, :, :], t_in["b_rope"]).then_inc(consts_in, 16)

            def load_qks(layer):
                for c, name in enumerate(("L0_ffn_q_scale", "L0_ffn_k_scale")):
                    sp.dma_start(qks[:, c, :], t_in[name][layer, :].broadcast_to([P, HDIM])).then_inc(qks_in, 16)

            load_qks(bass.ds(0, 1))
            def load_wo(layer):
                sp.dma_start(wo[:, :, :], t_in["L0_ffn_Wo"][layer, :, :].rearrange("l (c p) f -> p (l c) f", p=P)).then_inc(wo_in, 16)

            def load_ffn(layer):
                sp.dma_start(w1[:, :], t_in["L0_ffn_W1"][layer, :, :].rearrange("l p f -> p (l f)")).then_inc(w1_in, 16)
                w2v = t_in["L0_ffn_W2"]
                sp.dma_start(w2[:, 0:2, :], w2v[layer, 0:2 * P, :].rearrange("l (c p) f -> p (l c) f", p=P)).then_inc(w2_in, 16)
                sp.dma_start(w2[0:FF - 2 * P, 2, :], w2v[layer, 2 * P:FF, :].rearrange("l p f -> p (l f)")).then_inc(w2_in, 16)

            for s in range(BATCH):
                need(sp, w_lo_done, s)
                sp.dma_start(w_raw[:, :], wqkv[0, :, s * WCHUNK:(s + 1) * WCHUNK]).then_inc(raw_in, 16)
            load_wo(bass.ds(0, 1))
            load_ffn(bass.ds(0, 1))

            def body(n, cur, prev):
                if cur:
                    sp.wait_ge(w_lo_done, BATCH + n)
                    src = wqkv[bass.ds((n // BATCH + 1) % DEPTH, 1), :, bass.ds((n % BATCH) * WCHUNK, WCHUNK)]
                    sp.dma_start(w_raw[:, :], src.rearrange("l p f -> p (l f)")).then_inc(raw_in, 16)
                    sp.wait_ge(rope_done, n * 3 + 3)
                    load_qks(bass.ds(((n + 1) // BATCH) % DEPTH, 1))
                if cur and prev:
                    layer = bass.ds(n // BATCH, 1)
                    sp.wait_ge(fill, FILL.at(n, "wo'"))
                    load_wo(layer)
                    sp.wait_ge(fill, FILL.at(n, "down'"))
                    load_ffn(layer)
            pipelined(sp, nc.sync, body)

        @block.tensor
        def _(pe):
            pe.wait_ge(zeroed, 5)

            def body(n, cur, prev):
                m = n - 1
                parity = (n // BATCH) % 2

                def begin(name):
                    need(pe, *free_before(n, name))
                    return ring[bank_of(name)]

                def split_product(bank, x_cols, w_cols):
                    nc.tensor.matmul(bank, xa_hi[:, x_cols], w_cols(w_hi), start=True, stop=False)
                    nc.tensor.matmul(bank, xa_hi[:, x_cols], w_cols(w_lo), start=False, stop=False)
                    return nc.tensor.matmul(bank, xa_lo[:, x_cols], w_cols(w_hi), start=False, stop=True)

                def project(j):
                    if j == 0:
                        pe.wait_ge(x_lo_done, 2 + n * 4)
                        pe.wait_ge(w_lo_done, BATCH + n)
                    if j == 2:
                        pe.wait_ge(x_lo_done, 4 + n * 4)
                    xcols = slice(WINDOW + j * P, WINDOW + (j + 1) * P)
                    for c in range(2):
                        need(pe, qkn_done, n * 8 + 2 * j + c - 1)
                        for k in range(2):
                            off = c * INNER + k * 512

                            def cols(w, off=off):
                                return w[:, bass.ds(parity, 1), off:off + 512]
                            last = split_product(proj[c][:, k * 512:(k + 1) * 512], xcols, cols)
                        last.then_inc(proj_full, 1)

                def values(t, mark):
                    q = m if mark else n
                    pe.wait_ge(swap_done, q * 8 + (4 if t < 2 else 8))
                    lo = WINDOW + t * P
                    for a in range(2):
                        for b in range(2):
                            name = f"V{t}{2 * a + b}{mark}"
                            bank = begin(name)
                            start = lo - WINDOW * a
                            par = parity if not mark else (m // BATCH) % 2
                            for i, (x, w) in enumerate(((xa_hi, w_hi), (xa_hi, w_lo), (xa_lo, w_hi))):
                                wv = w[:, bass.ds(par, 1), 2 * INNER:3 * INNER].rearrange(
                                    "p o (q h d) -> p (o q) h d", h=2, d=HDIM)[:, :, b, :]
                                if b:
                                    xv = xsw[:, i // 2, a, t, :]
                                else:
                                    xv = x[:, start:start + P]
                                last = nc.tensor.matmul(bank[:, :], xv, wv, start=(i == 0), stop=(i == 2))
                            last.then_inc(fill, 1)

                def transpose_probs(t, mark):
                    pe.wait_ge(prob_done, (m if mark else n) * 4 + t + 1)
                    for i in range(2):
                        bank = begin(f"P{t}{i}{mark}")
                        for p in range(4):
                            last = nc.tensor.transpose(bank[:, p * P:(p + 1) * P], prob[:, 4 * i + p, :, :].rearrange("p s k -> p (s k)"), ident[:, :])
                        last.then_inc(fill, 1)

                def weigh(t, mark):
                    pe.wait_ge(act_free, ACT_FREE.at(n, f"P{t}1{mark}"))
                    for i in range(2):
                        bank = begin(f"O{t}{i}{mark}")[:, :].rearrange("p (q k) -> p q k", q=PAIRS)
                        pe.sem_inc(pe_passed, 1)
                        for p in range(PAIRS):
                            for w in (2 * i, 2 * i + 1):
                                for b in range(2):
                                    s = b ^ i
                                    last = nc.tensor.matmul(
                                        bank[64 * b:64 * b + 64, p, 32 * (w % 2):32 * (w % 2) + 32],
                                        val[64 * s:64 * s + 64, 1 - w % 2, b, p, :],
                                        pT[64 * s:64 * s + 64, p, 32 * w:32 * w + 32], start=True, stop=True)
                        last.then_inc(fill, 1)

                def feed_down():
                    pe.wait_ge(w2_in, n * 32)
                    pe.wait_ge(dve_free, DVE_FREE.at(n, "up5'"))
                    bank = begin("down'")
                    for i, (o, w) in enumerate(FFC):
                        last = nc.tensor.matmul(bank[:, :], w2[0:w, i, :], hid[0:w, i, :], start=(i == 0), stop=(i == 2))
                    last.then_inc(fill, 1)

                def transpose_qk(j):
                    for c in range(2):
                        if c and prev and j == 3:
                            feed_down()
                        pe.wait_ge(rc_done, n * 8 + 2 * j + c + 1)
                        pe.wait_ge(rs_done, n * 8 + 2 * j + c + 1)
                        for k in range(2):
                            bank = begin(f"T{j}{2 * c + k}")
                            for p in range(4):
                                o = (4 * k + p) * P
                                dst = bank[:, p * P:(p + 1) * P]
                                nc.tensor.matmul(dst, rc[:, c, o:o + P], ident[:, :], is_transpose=True,
                                                 start=True, stop=False)
                                last = nc.tensor.matmul(dst, rs[:, c, o:o + P], ident[:, :], is_transpose=True,
                                                        start=False, stop=True)
                            last.then_inc(fill, 1)

                def score(j):
                    pe.wait_ge(act_free, ACT_FREE.at(n, f"T{j}3"))
                    need(pe, sub_done, n * 4 + j)
                    for s in range(2):
                        mask = win_mask[j].rearrange("p (o k) -> p o k", o=1).broadcast_to([P, PAIRS, KEYS])
                        nc.tensor.matmul(scr[:, s, :, :], ident_bf, mask, start=True, stop=True)
                    for p in range(PAIRS):
                        for b in range(2):
                            for w in range(4):
                                s = b ^ (w // 2)
                                rows = slice(64 * b, 64 * b + 64)
                                last = nc.tensor.matmul(
                                    scr[32 * w:32 * w + 32, s, p, :], qT[rows, p, 32 * w:32 * w + 32],
                                    kT[rows, p, j * P + 32 * w:j * P + 32 * w + KEYS],
                                    start=False, stop=True, skip_group_check=True)
                    last.then_inc(scr_full, 1)

                for j in range(TILES):
                    t, mark = (j - 1) % TILES, "'" if j == 0 else ""
                    on = prev if j == 0 else cur
                    if cur:
                        project(j)
                    if prev and j == 3:
                        pe.wait_ge(spread_done, m + 1)
                        bank = begin("spread'")
                        for i in range(TILES):
                            last = nc.tensor.transpose(bank[:, i * P:(i + 1) * P], dev[:, i, :], ident[:, :])
                        last.then_inc(fill, 1)
                    if on:
                        values(t, mark)
                    if prev and j == 1:
                        pe.wait_ge(wo_in, n * 16)
                        pe.wait_ge(act_free, ACT_FREE.at(n, "O31'"))
                        bank = begin("wo'")
                        for p in range(PAIRS):
                            last = nc.tensor.matmul(bank[:, :], wo[:, p, :], oT[:, p, :], start=(p == 0),
                                                    stop=(p == PAIRS - 1))
                        last.then_inc(fill, 1)
                    if prev and j == 2:
                        pe.wait_ge(xs_done, n * 2)
                        bank = begin("mean'")
                        nc.tensor.matmul(bank[:, :], mean_w[:, :], xs[:, :], start=True, stop=True).then_inc(fill, 1)
                    if prev and j == 3:
                        pe.wait_ge(w1_in, n * 16)
                        pe.wait_ge(h_done, m + 1)
                        for i in range(6):
                            o, w = FFC[i % 3]
                            o += FF if i < 3 else 0
                            bank = begin(f"up{i}'")
                            nc.tensor.matmul(bank[0:w, :], w1[:, o:o + w], xc[:, :], start=True, stop=True)\
                              .then_inc(fill, 1)
                    if on:
                        transpose_probs(t, mark)
                    if prev and j == 2:
                        pe.wait_ge(xq_done, m + 1)
                        bank = begin("var'")
                        for i in range(TILES):
                            last = nc.tensor.matmul(bank[:, i:i + 1], xq[:, i * P:(i + 1) * P], mean_w[:, 0:1],
                                                    start=True, stop=True)
                        last.then_inc(fill, 1)
                    if on:
                        weigh(t, mark)
                    if cur:
                        transpose_qk(j)
                        score(j)
                    elif j == 3:
                        feed_down()
            pipelined(pe, nc.tensor, body)

        @block.scalar
        def _(act):
            act.wait_ge(zeroed, 5)

            def stage_hi(seq, half):
                for rows, col, tok, width in stage[half]:
                    nc.scalar.activation(xa_hi[rows, col:col + width], resT[rows, seq, tok:tok + width],
                                         ACT.Copy).then_inc(x_hi_done, 1)

            def split_hi(parity, off, count):
                act.wait_ge(raw_in, count)
                nc.scalar.activation(w_hi[:, parity, off], w_raw[:, :].rearrange("p (o f) -> p o f", o=1),
                                     ACT.Copy).then_inc(w_hi_done, 1)

            for s in range(BATCH):
                split_hi(slice(0, 1), slice(s * WCHUNK, (s + 1) * WCHUNK), (s + 1) * 16)
            stage_hi(slice(0, 1), 0)

            def body(n, cur, prev):
                m = n - 1

                def empty(name, dst, src=None):
                    act.wait_ge(fill, FILL.at(n, name))
                    nc.scalar.activation(dst, ring[bank_of(name)][:, :] if src is None else src, ACT.Copy).then_inc(act_free, 1)

                for j in range(TILES):
                    t, mark = (j - 1) % TILES, "'" if j == 0 else ""
                    on = prev if j == 0 else cur
                    if on:
                        q = m if mark else n
                        act.wait_ge(sub_done, q * 4 + t + 1)
                        nc.scalar.activation(prob[:, :, :, :], prob[:, :, :, :], ACT.Exp).then_inc(exp_done, 1)
                    if cur:
                        for c in range(2):
                            act.wait_ge(proj_full, n * 8 + 2 * j + c + 1)
                            need(act, ss_done, n * 8 + 2 * j + c)
                            nc.scalar.activation(squares[:, :], proj[c][:, :], ACT.Square).then_inc(sq_done, 1)
                    if on:
                        for i in range(4):
                            name = f"V{t}{i}{mark}"
                            empty(name, val[:, i // 2, i % 2, :, :],
                                  ring[bank_of(name)][:, :].rearrange("p (q d) -> p q d", q=PAIRS))
                    if cur and j == 0:
                        stage_hi(bass.ds(n % BATCH, 1), 1)
                    if cur and j == 3:
                        act.wait_ge(swap_done, n * 8 + 8)
                        stage_hi(bass.ds((n + 1) % BATCH, 1), 0)
                    if cur and j == 1:
                        split_hi(bass.ds((n // BATCH + 1) % 2, 1), bass.ds((n % BATCH) * WCHUNK, WCHUNK),
                                 (n + 1 + BATCH) * 16)
                    if prev and j == 1:
                        act.wait_ge(dve_free, DVE_FREE.at(n, "wo'"))
                        nc.scalar.activation(xs[0:64, :], x1[0:64, :], ACT.Copy).then_inc(xs_done, 1)
                        nc.scalar.activation(xs[64:P, 1:TOKENS], x1[64:P, 0:TOKENS - 1], ACT.Copy).then_inc(xs_done, 1)
                    if prev and j == 3:
                        for i in range(3):
                            w = FFC[i][1]
                            act.wait_ge(fill, FILL.at(n, f"up{i}'"))
                            nc.scalar.activation(hid[0:w, i, :], ring[bank_of(f"up{i}'")][0:w, :], ACT.Gelu,
                                                 bias=vec[0:w, 6 + i:7 + i]).then_inc(act_free, 1)
                    if on:
                        for i in range(2):
                            name = f"P{t}{i}{mark}"
                            empty(name, pT[:, 4 * i:4 * i + 4, :], ring[bank_of(name)][:, :].rearrange("p (q k) -> p q k", q=4))
                    if prev and j == 2:
                        act.wait_ge(dve_free, DVE_FREE.at(n, "mean'"))
                        nc.scalar.activation(xq, xc[:, :], ACT.Square).then_inc(xq_done, 1)
                    if on:
                        for i in range(2):
                            name = f"O{t}{i}{mark}"
                            empty(name, oT[:, :, t * P + 64 * i:t * P + 64 * i + 64],
                                  ring[bank_of(name)][:, :].rearrange("p (q k) -> p q k", q=PAIRS))
                    if cur:
                        for i in range(4):
                            name = f"T{j}{i}"
                            src = ring[bank_of(name)][:, :].rearrange("p (q k) -> p q k", q=4)
                            k = 4 * (i % 2)
                            if i < 2:
                                empty(name, qT[:, k:k + 4, :], src)
                            else:
                                empty(name, kT[:, k:k + 4, WINDOW + j * P:WINDOW + (j + 1) * P], src)
            pipelined(act, nc.scalar, body)

        @block.gpsimd
        def _(pool):
            nc.gpsimd.memset(xa_hi[:, 0:WINDOW + 1].bitcast(f32), 0.0).then_inc(zeroed, 1)
            nc.gpsimd.memset(xa_lo[:, 0:WINDOW + 1].bitcast(f32), 0.0).then_inc(zeroed, 1)
            nc.gpsimd.memset(kT[:, :, 0:WINDOW], 0.0).then_inc(zeroed, 1)
            nc.gpsimd.memset(xs[:, 0:1], 0.0).then_inc(zeroed, 1)
            nc.gpsimd.memset(mean_w[:, :], 1.0 / DIM).then_inc(zeroed, 1)

            def swap(half, count):
                pool.wait_ge(x_lo_done, count)
                pool.sem_inc(pool_passed, 1)
                for i, x in enumerate((xa_hi, xa_lo)):
                    for a in range(2):
                        lo = WINDOW * (1 - a) + 2 * half * P
                        src = x[:, lo:lo + 2 * P].rearrange("p (t s k) -> p t s k", t=2, s=2)[:, :, ::-1, :]
                        dst = xsw[:, i, a, 2 * half:2 * half + 2, :].rearrange("p t (s k) -> p t s k", s=2)
                        nc.gpsimd.tensor_copy(dst, src).then_inc(swap_done, 1)

            swap(0, 2)

            def body(n, cur, prev):
                m = n - 1
                for j in range(TILES):
                    t, mark = (j - 1) % TILES, "'" if j == 0 else ""
                    if cur and j == 1:
                        swap(1, 4 + n * 4)
                    if prev if j == 0 else cur:
                        q = m if mark else n
                        pool.wait_ge(inv_done, q * 4 + t + 1)
                        nc.gpsimd.tensor_tensor(
                            prob[:, :, :, :], prob[:, :, :, :],
                            rinv[:, :, :].rearrange("p q (s o) -> p q s o", o=1).broadcast_to([P, PAIRS, 2, KEYS]),
                            ALU.mult).then_inc(prob_done, 1)
                    if cur:
                        for c in range(2):
                            u = 2 * j + c
                            pool.wait_ge(qkn_done, n * 8 + u + 1)
                            if j:
                                pool.wait_ge(fill, FILL.at(n, f"T{j - 1}{2 * c + 1}"))
                            elif prev:
                                pool.wait_ge(fill, FILL.before(n, "T33"))
                            src = qkn[:, c, :].rearrange("p (h s d) -> p h s d", h=HEADS, s=2)
                            dst = rs[:, c, :].rearrange("p (h s d) -> p h s d", h=HEADS, s=2)
                            tab = rope[:, 1, j, c, :].rearrange("p (o s d) -> p o s d", o=1, s=2)
                            for s in range(2):
                                ins = nc.gpsimd.tensor_tensor(dst[:, :, s, :], src[:, :, 1 - s, :],
                                                              tab[:, :, s, :].broadcast_to([P, HEADS, HDIM // 2]),
                                                              ALU.mult)
                            ins.then_inc(rs_done, 1)
                    if cur and j == 3:
                        swap(0, 6 + n * 4)
            pipelined(pool, nc.gpsimd, body)

        @block.vector
        def _(dve):
            dve.wait_ge(zeroed, 5)
            dve.wait_ge(consts_in, 16)

            def stage_lo(seq, half, count):
                for i, (rows, col, tok, width) in enumerate(stage[half]):
                    dve.wait_ge(x_hi_done, count + i + 1)
                    nc.vector.tensor_tensor(xa_lo[rows, col:col + width], resT[rows, seq, tok:tok + width],
                                            xa_hi[rows, col:col + width].bitcast(f32), ALU.subtract).then_inc(x_lo_done, 1)

            def split_lo(parity, off, count):
                dve.wait_ge(w_hi_done, count)
                nc.vector.tensor_tensor(w_lo[:, parity, off], w_raw[:, :].rearrange("p (o f) -> p o f", o=1),
                                        w_hi[:, parity, off].bitcast(f32), ALU.subtract).then_inc(w_lo_done, 1)

            def load_vec(layer):
                nc.vector.tensor_copy(vec[:, :].rearrange("p (v o) -> p v o", o=1), vecs[:, :, layer]).then_inc(vec_done, 1)

            for s in range(BATCH):
                split_lo(slice(0, 1), slice(s * WCHUNK, (s + 1) * WCHUNK), s + 1)
            stage_lo(slice(0, 1), 0, 0)
            load_vec(slice(0, 1))

            def body(n, cur, prev):
                m = n - 1
                if cur:
                    need(dve, rs_done, n * 8)
                    need(dve, rc_done, n * 8)
                    dve.wait_ge(qks_in, n * 32 + 32)
                    nc.vector.tensor_tensor(rope[:, 0, :, :, :], rope0[:, 0, :, :, :],
                                            qks[:, :, :].rearrange("p (o c) d -> p o c d", o=1).broadcast_to([P, TILES, 2, HDIM]), ALU.mult).then_inc(rope_done, 1)
                    for s in range(2):
                        h, o = slice(32 * s, 32 * s + 32), slice(32 - 32 * s, 64 - 32 * s)
                        nc.vector.tensor_tensor(rope[:, 1, :, :, h], rope0[:, 1, :, :, h],
                                                qks[:, :, o].rearrange("p (o c) d -> p o c d", o=1).broadcast_to([P, TILES, 2, HDIM // 2]), ALU.mult).then_inc(rope_done, 1)
                    dve.wait_ge(rope_done, n * 3 + 3)
                for j in range(TILES):
                    t, mark = (j - 1) % TILES, "'" if j == 0 else ""
                    on = prev if j == 0 else cur
                    q4 = (m if mark else n) * 4 + t
                    if on:
                        dve.wait_ge(scr_full, q4 + 1)
                        nc.vector.tensor_reduce(rmax[:, :, :], scr[:, :, :, :], AX.X, ALU.max).then_inc(max_done, 1)
                        dve.wait_ge(max_done, q4 + 1)
                        nc.vector.tensor_tensor(
                            prob_s, scr[:, :, :, :],
                            rmax[:, :, :].rearrange("p s (q o) -> p s q o", o=1).broadcast_to([P, 2, PAIRS, KEYS]),
                            ALU.subtract).then_inc(sub_done, 1)

                    if prev and j == 3:
                        dve.wait_ge(fill, FILL.at(n, "spread'"))
                        nc.vector.tensor_tensor(xc[:, :], xc[:, :], ring[bank_of("spread'")][:, :], ALU.mult).then_inc(dve_free, 1)
                        dve.wait_ge(dve_free, DVE_FREE.at(n, "spread'"))
                        nc.vector.tensor_scalar(xc[:, :], xc[:, :], vec[:, 0:1], vec[:, 1:2], ALU.mult, ALU.add).then_inc(h_done, 1)

                    def sums():
                        dve.wait_ge(exp_done, q4 + 1)
                        nc.vector.tensor_reduce(rsum[:, :, :], prob[:, :, :, :], AX.X, ALU.add).then_inc(sum_done, 1)
                        dve.wait_ge(sum_done, q4 + 1)
                        nc.vector.reciprocal(rinv[:, :, :], rsum[:, :, :]).then_inc(inv_done, 1)

                    if cur:
                        for c in range(2):
                            u = 2 * j + c
                            dve.wait_ge(sq_done, n * 8 + u + 1)
                            nc.vector.tensor_reduce(ssum[:, c, :], squares[:, :].rearrange("p (h d) -> p h d", h=HEADS),
                                                    AX.X, ALU.add).then_inc(ss_done, 1)
                        dve.wait_ge(ss_done, n * 8 + 2 * j + 2)
                        nc.vector.tensor_scalar(ssum[:, :, :], ssum[:, :, :], 1e-24, None, ALU.max).then_inc(clamp_done, 1)
                        dve.wait_ge(clamp_done, n * 4 + j + 1)
                        rsqrt(nc, dve, ssum[:, :, :], rnorm[:, :, :], rtmp[:, :, :], rn_done, (n * 4 + j) * RSQRT_STEPS)
                        for c in range(2):
                            u = 2 * j + c
                            need(dve, rs_done, n * 8 + u - 1)
                            nc.vector.tensor_tensor(
                                qkn[:, c, :].rearrange("p (h d) -> p h d", h=HEADS),
                                proj[c][:, :].rearrange("p (h d) -> p h d", h=HEADS),
                                rnorm[:, c, :].rearrange("p (h o) -> p h o", o=1).broadcast_to([P, HEADS, HDIM]),
                                ALU.mult).then_inc(qkn_done, 1)
                            if c == 0 and on:
                                sums()
                            dve.wait_ge(qkn_done, n * 8 + u + 1)
                            if j:
                                dve.wait_ge(fill, FILL.at(n, f"T{j - 1}{2 * c + 1}"))
                            elif prev:
                                dve.wait_ge(fill, FILL.before(n, "T33"))
                            nc.vector.tensor_tensor(
                                rc[:, c, :].rearrange("p (h d) -> p h d", h=HEADS),
                                qkn[:, c, :].rearrange("p (h d) -> p h d", h=HEADS),
                                rope[:, 0, j, c:c + 1, :].broadcast_to([P, HEADS, HDIM]), ALU.mult).then_inc(rc_done, 1)
                    elif on:
                        sums()
                    if cur and j == 0:
                        stage_lo(bass.ds(n % BATCH, 1), 1, 2 + n * 4)
                    if cur and j == 3:
                        stage_lo(bass.ds((n + 1) % BATCH, 1), 0, 4 + n * 4)
                    if cur and j == 1:
                        split_lo(bass.ds((n // BATCH + 1) % 2, 1), bass.ds((n % BATCH) * WCHUNK, WCHUNK), n + 1 + BATCH)
                    seq = bass.ds(m % BATCH, 1)

                    def r3(ap):
                        return ap.rearrange("p (o t) -> p o t", o=1)
                    if prev and j == 1:
                        dve.wait_ge(fill, FILL.at(n, "wo'"))
                        nc.vector.tensor_tensor(r3(x1[:, :]), r3(ring[bank_of("wo'")][:, :]), resT[:, seq, :], ALU.add)\
                          .then_inc(dve_free, 1)
                    if prev and j == 2:
                        dve.wait_ge(fill, FILL.at(n, "mean'"))
                        nc.vector.tensor_tensor(xc[:, :], xs[:, :], ring[bank_of("mean'")][:, :], ALU.subtract).then_inc(dve_free, 1)
                        dve.wait_ge(fill, FILL.at(n, "var'"))
                        nc.vector.tensor_scalar(var[:, 0, :], ring[bank_of("var'")][:, 0:TILES], 1e-5, None, ALU.add)\
                          .then_inc(dve_free, 1)
                        dve.wait_ge(dve_free, DVE_FREE.at(n, "var'"))
                        rsqrt(nc, dve, var[:, 0, :], var[:, 1, :], var[:, 2, :], rstd_done, m * RSQRT_STEPS)
                        nc.vector.tensor_copy(dev, var[:, 1, :].rearrange("p (t o) -> p t o", o=1).broadcast_to([P, TILES, P]))\
                          .then_inc(spread_done, 1)
                    if prev and j == 3:
                        for i in range(3):
                            w = FFC[i][1]
                            name = f"up{3 + i}'"
                            dve.wait_ge(act_free, ACT_FREE.at(n, f"up{i}'"))
                            dve.wait_ge(fill, FILL.at(n, name))
                            nc.vector.scalar_tensor_tensor(hid[0:w, i, :], ring[bank_of(name)][0:w, :], vec[0:w, 3 + i:4 + i],
                                                           hid[0:w, i, :], ALU.add, ALU.mult).then_inc(dve_free, 1)
                        dve.wait_ge(fill, FILL.at(n, "down'"))
                        nc.vector.scalar_tensor_tensor(resT[:, seq, :], r3(ring[bank_of("down'")][:, :]), vec[:, 2:3],
                                                       r3(x1[:, :]), ALU.add, ALU.add).then_inc(dve_free, 1)
                        if cur:
                            dve.wait_ge(dve_free, DVE_FREE.at(n, "down'"))
                            load_vec(bass.ds(n // BATCH, 1))
                            dve.wait_ge(vec_done, n + 1)
            pipelined(dve, nc.vector, body)


def part_c(nc, out, alloc, need, resT, xtok, ident, mod):
    f32 = mybir.dt.float32
    ALU, ACT = mybir.AluOpType, mybir.ActivationFunctionType
    ctx = ExitStack()
    with ctx:
        sb, ps, sem = alloc(ctx)
        yt = [ps(f"yt{i}", [P, TOKENS]) for i in range(2)]
        scaled = sem("scaled"); turned = sem("turned"); added = sem("added"); stored = sem("stored")
        block = ctx.enter_context(nc.Block())
        ov = out.rearrange("b (t p) d -> p b t d", p=P)

        @block.scalar
        def _(act):
            for b in range(BATCH):
                nc.scalar.activation(resT[:, b, :], resT[:, b, :], ACT.Copy, scale=mod[:, 5, b:b + 1]).then_inc(scaled, 1)

        @block.tensor
        def _(pe):
            for b in range(BATCH):
                pe.wait_ge(scaled, b + 1)
                need(pe, added, b - 1)
                for j in range(TILES):
                    last = nc.tensor.transpose(yt[b % 2][:, j * P:(j + 1) * P], resT[:, b, j * P:(j + 1) * P], ident[:, :])
                last.then_inc(turned, 1)

        @block.vector
        def _(dve):
            for b in range(BATCH):
                dve.wait_ge(turned, b + 1)
                xb = xtok[:, b * TILES:(b + 1) * TILES, :]
                nc.vector.tensor_tensor(xb, yt[b % 2][:, :].rearrange("p (t f) -> p t f", t=TILES), xb, ALU.add).then_inc(added, 1)

        @block.sync
        def _(sp):
            for b in range(BATCH):
                sp.wait_ge(added, b + 1)
                sp.dma_start(ov[:, b, :, :], xtok[:, b * TILES:(b + 1) * TILES, :]).then_inc(stored, 16)
            sp.wait_ge(stored, 16 * BATCH)


_INS = ['L0_attn_x', 'L0_attn_Wq', 'L0_attn_Wk', 'L0_attn_Wv', 'L0_attn_Wo', 'L0_ffn_Wqkv', 'L0_ffn_q_scale',
        'L0_ffn_k_scale', 'L0_ffn_Wo', 'L0_ffn_ln_g', 'L0_ffn_ln_b', 'L0_ffn_W1', 'L0_ffn_b1', 'L0_ffn_W2',
        'L0_ffn_b2', 'L0_c', 'L0_wmod']


def kernel(**inputs):
    import numpy as _np
    import concourse.bacc as _bacc
    from concourse import mybir as _mybir
    from concourse.bass_utils import run_bass_kernel_spmd as _run

    nc = _bacc.Bacc("TRN2", target_bir_lowering=False, num_devices=1)
    arrays, args = {}, {}
    given = {name: _np.ascontiguousarray(inputs[name]) for name in _INS}
    given.update(constants())
    for name, a in given.items():
        arrays[f"in_{name}"] = a
        args[name] = nc.dram_tensor(f"in_{name}", a.shape, _mybir.dt.from_np(a.dtype), kind="ExternalInput").ap()
    o = nc.dram_tensor("out_0", (BATCH, TOKENS, DIM), _mybir.dt.float32, kind="ExternalOutput").ap()
    program(nc, args, o)
    r = _run(nc, [arrays], core_ids=[0])
    return r.results[0]["out_0"]
```

```python
import concourse.bass as bass
from concourse import mybir
from contextlib import ExitStack
import numpy as np

BATCH, TOKENS, DIM = 8, 512, 128
P = 128
TILES = TOKENS // P
A_HEADS = 16
A_HDIM = DIM // A_HEADS
DEPTH, HEADS, HDIM, WINDOW = 6, 16, 64, 32
INNER = HEADS * HDIM
FF = int(DIM * 4 * 2 / 3)
PAIRS = HEADS // 2
KEYS = 2 * WINDOW
QKV = 3 * INNER
WCHUNK = QKV // BATCH
NSEQ = DEPTH * BATCH
MASKED = -1e30
FFC = [(0, 128), (128, 128), (256, FF - 256)]
VECS = 9


def constants():
    f = np.float32
    out = {"ident": np.eye(P, dtype=f)}
    inv = (1.0 / 10000.0 ** (np.arange(0, A_HDIM, 2, dtype=f) / A_HDIM)).astype(f)
    ang = np.outer(np.arange(TOKENS, dtype=f), inv).astype(f)
    cos, sin = np.cos(ang).astype(f), np.sin(ang).astype(f)
    row = (np.arange(DIM) % A_HDIM) // 2
    root = f(1.0 / np.sqrt(A_HDIM))
    out["a_rope"] = np.stack([cos.T[row] * root, sin.T[row] * root, cos.T[row], sin.T[row]], 1).astype(f)
    sel = np.zeros((P, 4, 4, P), f)
    for g in range(4):
        for hh in range(4):
            for e in range(4):
                for d in range(A_HDIM):
                    src, dst = A_HDIM * (4 * g + hh) + d, 32 * hh + A_HDIM * e + d
                    sel[src, g, 0 + e % 2, dst] = 1.0
                    sel[src, g, 2 + e // 2, dst] = 1.0
    out["a_sel"] = sel
    causal = np.where(np.arange(P)[None, :] > np.arange(P)[:, None], MASKED, 0.0)
    half = np.arange(0, HDIM, 2, dtype=f)
    inv = (1.0 / 10000.0 ** (half / HDIM)).astype(f)
    t = np.arange(TOKENS, dtype=f)
    fr = (t[:, None] * inv[None, :]).astype(f)
    base = ((half + f(0.4 * HDIM)) / f(1.4 * HDIM)).astype(f)
    scale = (base[None, :] ** ((t - TOKENS // 2) / (WINDOW // 2))[:, None]).astype(f)
    c, s = np.cos(fr).astype(f), np.sin(fr).astype(f)
    rope = np.zeros((2, TOKENS, 2, HDIM), f)
    for i, z in enumerate((scale * f(8.0), f(1.0) / scale)):
        rope[0, :, i, :32], rope[0, :, i, 32:] = c * z, c * z
        rope[1, :, i, :32], rope[1, :, i, 32:] = -s * z, s * z
    out["b_rope"] = rope.reshape(2, TILES, P, 2, HDIM).transpose(2, 0, 1, 3, 4).copy()
    a = (np.arange(P) % WINDOW)[:, None]
    b = np.arange(KEYS)[None, :]
    bad = (b < a) | (b > a + WINDOW)
    first = bad | ((np.arange(P)[:, None] < WINDOW) & (b < WINDOW))
    m = np.concatenate([np.where(bad, MASKED, 0.0), np.where(first, MASKED, 0.0), causal, np.eye(P)], 1)
    out["masks"] = m.astype(mybir.dt.np(mybir.dt.bfloat16))
    return out


class Tally:

    def __init__(self, steady, keep=lambda e: True):
        self.steady = [e for e in steady if keep(e)]
        self.first = [e for e in self.steady if not e.endswith("'")]
        self.last = [e for e in self.steady if e.endswith("'")]

    def at(self, n, name):
        if isinstance(n, int) and n == 0:
            return self.first.index(name) + 1
        if isinstance(n, int) and n == NSEQ:
            return len(self.first) + (NSEQ - 1) * len(self.steady) + self.last.index(name) + 1
        return (n - 1) * len(self.steady) + len(self.first) + self.steady.index(name) + 1

    def all_before(self, n):
        if isinstance(n, int):
            return 0 if n == 0 else len(self.first) + (n - 1) * len(self.steady)
        return (n - 1) * len(self.steady) + len(self.first)


def fill_order():
    out = []
    for j in range(TILES):
        t, pr = ((j - 1) % TILES, "'" if j == 0 else "")
        out += [f"up{i}'" for i in range(3)] if j == 3 else []
        out += ["wo0'"] if j == 1 else []
        out += [f"T{j}0", f"T{j}1"]
        out += ["wo1'"] if j == 1 else []
        out += [f"T{j}2", f"T{j}3"]
        out += ["var'"] if j == 2 else []
        out += [f"V{j}0", f"P{t}0{pr}", f"P{t}1{pr}"]
        out += {0: [f"V{j}1"], 1: ["mean'"], 2: ["spread'"], 3: [f"up{i}'" for i in range(3, 6)]}[j]
        out += [f"O{t}{i}{pr}" for i in range(2)]
        out += [f"V{j}1"] if j else []
        out += [f"Q{t}{i}{pr}" for i in range(2)]
        out += ["down'"] if j == 3 else []
    return out


FILLS = fill_order()
BY_VECTOR = ("wo0'", "wo1'", "mean'", "var'", "spread'", "up3'", "up4'", "up5'")
FILL = Tally(FILLS)
ACT_FREE = Tally(FILLS, lambda e: e not in BY_VECTOR)
DVE_FREE = Tally(FILLS, lambda e: e in BY_VECTOR)


def bank_of(name):
    return FILLS.index(name) % 2


def program(nc, t_in, out):
    f32, f32r, bf16 = mybir.dt.float32, mybir.dt.float32r, mybir.dt.bfloat16
    ALU, ACT, AX = mybir.AluOpType, mybir.ActivationFunctionType, mybir.AxisListType

    def need(eng, sem, value):
        if not isinstance(value, int) or value > 0:
            eng.wait_ge(sem, value)

    ctx = ExitStack()
    with ctx:
        def alloc(stack):
            return (lambda n, s, d=f32: stack.enter_context(nc.sbuf_tensor(n, s, d)),
                    lambda n, s, d=f32: stack.enter_context(nc.psum_tensor(n, s, d)),
                    lambda n: stack.enter_context(nc.semaphore(n)))

        sb, _, _ = alloc(ctx)
        resT = sb("resT", [P, BATCH, TOKENS])
        ident = sb("ident", [P, P])
        masks = sb("masks", [P, 2 * KEYS + 2 * P], bf16)
        win_mask = [masks[:, KEYS:2 * KEYS]] + [masks[:, 0:KEYS]] * (TILES - 1)
        causal_mask = masks[:, 2 * KEYS:2 * KEYS + P]
        ident_bf = masks[:, 2 * KEYS + P:2 * KEYS + 2 * P]
        mod = sb("mod", [P, 6, BATCH])
        vecs = sb("vecs", [P, VECS, DEPTH])

        x_attended = nc.dram_tensor("x_attended", (P, BATCH * TILES, DIM), f32, kind="Internal").ap()
        part_a(nc, t_in, alloc, need, x_attended, resT, ident, masks, causal_mask, ident_bf, mod, vecs)
        part_b(nc, t_in, alloc, need, resT, ident, win_mask, ident_bf, vecs)
        part_c(nc, out, alloc, need, x_attended, resT, ident, mod)


NEWTON = 3
RSQRT_STEPS = 1 + 3 * NEWTON


def rsqrt(nc, dve, x, y, t, sem, base):
    i32, ALU = mybir.dt.int32, mybir.AluOpType
    nc.vector.tensor_scalar(y.bitcast(i32), x.bitcast(i32), -0.5, float(0x5F3759DF), ALU.mult, ALU.add).then_inc(sem, 1)
    for i in range(NEWTON):
        dve.wait_ge(sem, base + 3 * i + 1)
        nc.vector.tensor_tensor(t, y, y, ALU.mult).then_inc(sem, 1)
        dve.wait_ge(sem, base + 3 * i + 2)
        nc.vector.scalar_tensor_tensor(t, t, -0.5, x, ALU.mult, ALU.mult).then_inc(sem, 1)
        dve.wait_ge(sem, base + 3 * i + 3)
        nc.vector.scalar_tensor_tensor(y, t, 1.5, y, ALU.add, ALU.mult).then_inc(sem, 1)
    dve.wait_ge(sem, base + RSQRT_STEPS)


def part_a(nc, t_in, alloc, need, x_attended, resT, ident, masks, causal_mask, ident_bf, mod, vecs):
    f32, f32r, bf16 = mybir.dt.float32, mybir.dt.float32r, mybir.dt.bfloat16
    ALU, ACT, AX = mybir.AluOpType, mybir.ActivationFunctionType, mybir.AxisListType
    ctx = ExitStack()
    with ctx:
        sb, ps, sem = alloc(ctx)
        xtok = sb("xtok", [P, BATCH * TILES, DIM])
        w_raw = sb("w_raw", [P, 4, P])
        wT = sb("wT", [P, 6, P])
        wmod = sb("wmod", [P, 6, P])
        c_row = sb("c_row", [BATCH, P])
        cT = sb("cT", [P, BATCH])
        sgn = sb("sgn", [P, 2, BATCH])
        rope = sb("rope", [P, 4, TOKENS])
        sel_raw = sb("sel_raw", [P, 16, P])
        sel = sb("sel", [P, 16, P], f32r)
        rows = sb("rows", [DEPTH, 3 * P + 2 * FF])
        stats = sb("stats", [P, TILES, 6])
        mv = sb("mv", [P, TILES, 2])
        rstd = sb("rstd", [P, TILES])
        var = sb("var", [P, TILES])
        var_t = sb("var_t", [P, TILES])
        xn = sb("xn", [P, TILES, P])
        hT = sb("hT", [P, TOKENS])
        cur = sb("cur", [P, 6])
        rot1 = sb("rot1", [P, 2, TOKENS])
        rot2 = sb("rot2", [P, 2, TOKENS])
        qk_hi = sb("qk_hi", [P, 2, TOKENS], f32r)
        qk_lo = sb("qk_lo", [P, 2, TOKENS], f32r)
        qkG = sb("qkG", [P, 2, 4, TOKENS], f32r)
        vtok = sb("vtok", [P, TILES, P])
        negmax = sb("negmax", [P, A_HEADS * TILES])
        den = sb("den", [P, TILES, A_HEADS])
        rden = sb("rden", [P, TILES, A_HEADS])
        prob = sb("prob", [P, 3, TOKENS])
        probT = sb("probT", [P, 2, TOKENS])
        otok = sb("otok", [P, TILES, P])
        oT = sb("oT", [P, TOKENS])
        yT = sb("yT", [P, TOKENS])

        sc = [ps(f"sc{i}", [P, TOKENS]) for i in range(3)]
        pt = [ps(f"pt{i}", [P, TOKENS]) for i in range(2)]
        po = ps("po", [P, TOKENS])
        gen = [ps(f"gen{i}", [P, TOKENS]) for i in range(2)]

        loaded = sem("loaded")
        x_in = sem("x_in"); kept = sem("kept")
        tr_w = sem("tr_w"); tr_v = sem("tr_v"); ev_w = sem("ev_w"); silu_d = sem("silu_d")
        mod_p = sem("mod_p"); mod_e = sem("mod_e"); mod_d = sem("mod_d"); sel_d = sem("sel_d")
        rot_w = sem("rot_w"); vec_e = sem("vec_e"); vec_z = sem("vec_z")
        st = sem("st"); passed = sem("passed"); rstd_d = sem("rstd_d"); nrm = sem("nrm"); cur_d = sem("cur_d")
        g_fill = sem("g_fill"); g_act = sem("g_act"); g_dve = sem("g_dve")
        rope_m = sem("rope_m"); rope_a = sem("rope_a"); hi_d = sem("hi_d"); lo_d = sem("lo_d")
        s_full = sem("s_full"); m_d = sem("m_d"); e_d = sem("e_d"); t_full = sem("t_full")
        t_act = sem("t_act"); t_dve = sem("t_dve"); o_full = sem("o_full")
        rd_d = sem("rd_d"); ot_d = sem("ot_d"); x_d = sem("x_d")
        block = ctx.enter_context(nc.Block())

        units = [(h, j) for h in range(A_HEADS) for j in range(TILES)]
        NU = len(units)
        by_act = [h % 3 == 0 for h, j in units]
        act_count = [sum(by_act[:i + 1]) for i in range(NU)]
        dve_count = [i + 1 - act_count[i] for i in range(NU)]
        gens = ["h", "q", "qr", "k", "kr", "v"] + [f"g{i}" for i in range(8)] + ["oT", "y", "yt", "h2"]
        gen_act = [g in ("h", "v", "oT", "y", "h2") or g[0] == "g" for g in gens]
        NG = len(gens)
        NA = sum(gen_act)

        def gfull(b, name):
            return b * NG + gens.index(name) + 1

        def gfree(b, i):
            if i < 0:
                b, i = b - 1, i + NG
            if gen_act[i]:
                return g_act, b * NA + sum(gen_act[:i + 1])
            return g_dve, b * (NG - NA) + i + 1 - sum(gen_act[:i + 1])

        xv = t_in["L0_attn_x"].rearrange("b (t p) d -> p (b t) d", p=P)

        @block.sync
        def _(sp):
            sp.dma_start(c_row[:, :], t_in["L0_c"]).then_inc(loaded, 16)
            for i, w in enumerate(("Wq", "Wk", "Wv", "Wo")):
                sp.dma_start(w_raw[:, i, :], t_in["L0_attn_" + w]).then_inc(loaded, 16)
            sp.dma_start(ident[:, :], t_in["ident"]).then_inc(loaded, 16)
            sp.dma_start(masks[:, :], t_in["masks"]).then_inc(loaded, 16)
            sp.dma_start(wmod[:, :, :], t_in["L0_wmod"].rearrange("k (m f) -> k m f", m=6)).then_inc(loaded, 16)
            sp.dma_start(rows[:, 0:P], t_in["L0_ffn_ln_g"]).then_inc(loaded, 16)
            sp.dma_start(rows[:, P:2 * P], t_in["L0_ffn_ln_b"]).then_inc(loaded, 16)
            sp.dma_start(rows[:, 2 * P:3 * P], t_in["L0_ffn_b2"]).then_inc(loaded, 16)
            sp.dma_start(rows[:, 3 * P:], t_in["L0_ffn_b1"]).then_inc(loaded, 16)
            sp.dma_start(rope[:, :, :], t_in["a_rope"]).then_inc(loaded, 16)
            sp.dma_start(sel_raw[:, :, :], t_in["a_sel"].rearrange("p g s f -> p (g s) f")).then_inc(loaded, 16)
            sp.dma_start(xtok[:, :, :], xv).then_inc(x_in, 16)
            with nc.sync.Fori(0, BATCH) as b:
                sp.wait_ge(g_dve, (b + 1) * (NG - NA))
                tiles = bass.ds(b * TILES, TILES)
                sp.dma_start(x_attended[:, tiles, :], xtok[:, tiles, :]).then_inc(kept, 16)
            sp.wait_ge(kept, 16 * BATCH)
        NLOAD = 14 * 16
        pieces = [(0, P), (P, P), (2 * P, P)] + [(3 * P + o, w) for o, w in FFC] + \
                 [(3 * P + FF + o, w) for o, w in FFC]

        @block.tensor
        def _(pe):
            pe.wait_ge(loaded, NLOAD)
            for i in range(4):
                nc.tensor.transpose(sc[0][:, i * P:(i + 1) * P], w_raw[:, i, :], ident[:, :])
            nc.tensor.transpose(sc[1][:, 0:BATCH], c_row[:, :], ident[0:BATCH, 0:BATCH]).then_inc(tr_w, 1)
            for i, (o, w) in enumerate(pieces):
                last = nc.tensor.transpose(sc[2][0:w, 8 * i:8 * i + DEPTH], rows[:, o:o + w],
                                           ident[0:DEPTH, 0:DEPTH])
            last.then_inc(tr_v, 1)
            pe.wait_ge(silu_d, 1)
            for m in range(6):
                last = nc.tensor.matmul(gen[0][:, m * BATCH:(m + 1) * BATCH], wmod[:, m, :], cT[:, :],
                                        start=True, stop=True)
            last.then_inc(mod_p, 1)
            pe.wait_ge(mod_d, 5)
            pe.wait_ge(rot_w, 4)
            pe.wait_ge(sel_d, 1)
            pe.wait_ge(vec_e, VECS)

            with nc.tensor.Fori(0, BATCH) as b:
                def fill(name, body):
                    i = gens.index(name)
                    if i >= 2:
                        pe.wait_ge(*gfree(b, i - 2))
                    body(gen[i % 2]).then_inc(g_fill, 1)

                def transposes4(src):
                    def body(bank):
                        for j in range(TILES):
                            last = nc.tensor.transpose(bank[:, j * P:(j + 1) * P], src(j), ident[:, :])
                        return last
                    return body

                def project(w, src):
                    return lambda bank: nc.tensor.matmul(bank[:, :], w, src, start=True, stop=True)

                pe.wait_ge(nrm, b * 8 + 4)
                fill("h", transposes4(lambda j: xn[:, j, :]))
                s, v = gfree(b, gens.index("h"))
                pe.wait_ge(s, v)
                fill("q", project(wT[:, 0, :], hT[:, :]))
                fill("qr", project(wT[:, 4, :], hT[:, :]))
                fill("k", project(wT[:, 1, :], hT[:, :]))
                fill("kr", project(wT[:, 5, :], hT[:, :]))

                def values(bank):
                    for j in range(TILES):
                        last = nc.tensor.matmul(bank[:, j * P:(j + 1) * P], hT[:, j * P:(j + 1) * P],
                                                wT[:, 2, :], start=True, stop=True)
                    return last
                fill("v", values)
                pe.wait_ge(lo_d, b * 2 + 2)
                for g in range(4):
                    for c in range(2):
                        def stack(bank, g=g, c=c):
                            nc.tensor.matmul(bank[:, :], sel[:, 4 * g + 2 * c, :], qk_hi[:, c, :],
                                             start=True, stop=False)
                            return nc.tensor.matmul(bank[:, :], sel[:, 4 * g + 2 * c + 1, :], qk_lo[:, c, :],
                                                    start=False, stop=True)
                        fill(f"g{2 * g + c}", stack)

                def scores(i):
                    h, j = units[i]
                    g, hh = divmod(h, 4)
                    if j == 0 and hh == 0:
                        pe.wait_ge(*gfree(b, gens.index(f"g{2 * g + 1}")))
                    if i >= 3:
                        pe.wait_ge(e_d, b * NU + i - 2)
                    r = slice(32 * hh, 32 * hh + 32)
                    bank, width = sc[i % 3], (j + 1) * P
                    nc.tensor.matmul(bank[:, 0:width], qkG[r, 0, g, j * P:(j + 1) * P],
                                     qkG[r, 1, g, 0:width], start=True, stop=False)
                    nc.tensor.matmul(bank[:, j * P:width], ident_bf, causal_mask,
                                     start=False, stop=True).then_inc(s_full, 1)

                def attend(i):
                    h, j = units[i]
                    pe.wait_ge(e_d, b * NU + i + 1)
                    if i >= 2:
                        if by_act[i - 2]:
                            pe.wait_ge(t_act, b * act_count[-1] + act_count[i - 2])
                        else:
                            pe.wait_ge(t_dve, b * dve_count[-1] + dve_count[i - 2])
                    for k in range(j + 1):
                        last = nc.tensor.transpose(pt[i % 2][:, k * P:(k + 1) * P],
                                                   prob[:, i % 3, k * P:(k + 1) * P], ident[:, :])
                    last.then_inc(t_full, 1)

                def weigh(i):
                    h, j = units[i]
                    if by_act[i]:
                        pe.wait_ge(t_act, b * act_count[-1] + act_count[i])
                    else:
                        pe.wait_ge(t_dve, b * dve_count[-1] + dve_count[i])
                    if i == 0:
                        pe.wait_ge(*gfree(b, gens.index("v")))
                    for k in range(j + 1):
                        last = nc.tensor.matmul(po[:, j * P + A_HDIM * h:j * P + A_HDIM * (h + 1)],
                                                probT[:, i % 2, k * P:(k + 1) * P],
                                                vtok[:, k, A_HDIM * h:A_HDIM * (h + 1)],
                                                start=(k == 0), stop=(k == j))
                    last.then_inc(o_full, 1)

                for i in range(NU + 3):
                    if i < NU:
                        scores(i)
                    if 0 <= i - 2 < NU:
                        attend(i - 2)
                    if 0 <= i - 3 < NU:
                        weigh(i - 3)
                pe.wait_ge(ot_d, b + 1)
                fill("oT", transposes4(lambda j: otok[:, j, :]))
                s, v = gfree(b, gens.index("oT"))
                pe.wait_ge(s, v)
                fill("y", project(wT[:, 3, :], oT[:, :]))
                s, v = gfree(b, gens.index("y"))
                pe.wait_ge(s, v)
                fill("yt", transposes4(lambda j: yT[:, j * P:(j + 1) * P]))
                pe.wait_ge(nrm, b * 8 + 8)
                fill("h2", transposes4(lambda j: xn[:, j, :]))
                pe.wait_ge(*gfree(b, gens.index("h2")))

        @block.scalar
        def _(act):
            act.wait_ge(tr_w, 1)
            nc.scalar.activation(wT[:, 0:4, :], sc[0][:, :].rearrange("p (i f) -> p i f", i=4), ACT.Copy).then_inc(ev_w, 1)
            nc.scalar.activation(cT[:, :], sc[1][:, 0:BATCH], ACT.Silu).then_inc(silu_d, 1)
            act.wait_ge(loaded, NLOAD)
            nc.scalar.activation(sel[:, :, :], sel_raw[:, :, :], ACT.Copy).then_inc(sel_d, 1)
            with nc.scalar.Fori(0, BATCH) as b:
                def fill(name, *args, **kw):
                    act.wait_ge(g_fill, gfull(b, name))
                    nc.scalar.activation(*args, **kw).then_inc(g_act, 1)

                act.wait_ge(cur_d, b + 1)
                fill("h", hT[:, :], gen[0][:, :], ACT.Identity, bias=cur[:, 0:1], scale=cur[:, 1:2])
                for c in range(2):
                    act.wait_ge(rope_a, b * 2 + c + 1)
                    nc.scalar.activation(qk_hi[:, c, :], rot1[:, c, :], ACT.Copy).then_inc(hi_d, 1)
                fill("v", vtok[:, :, :], gen[gens.index("v") % 2][:, :].rearrange("p (t f) -> p t f", t=TILES), ACT.Copy)
                for g in range(4):
                    for c in range(2):
                        name = f"g{2 * g + c}"
                        fill(name, qkG[:, c, g, :], gen[gens.index(name) % 2][:, :], ACT.Copy)

                def empty(i):
                    h, j = units[i]
                    act.wait_ge(t_full, b * NU + i + 1)
                    if i >= 2:
                        act.wait_ge(o_full, b * NU + i - 1)
                    nc.scalar.activation(probT[:, i % 2, 0:(j + 1) * P], pt[i % 2][:, 0:(j + 1) * P],
                                         ACT.Copy).then_inc(t_act, 1)

                for i, (h, j) in enumerate(units):
                    act.wait_ge(m_d, b * NU + i + 1)
                    if i >= 3:
                        act.wait_ge(t_full, b * NU + i - 2)
                    nc.scalar.activation(prob[:, i % 3, 0:(j + 1) * P], sc[i % 3][:, 0:(j + 1) * P], ACT.Exp,
                                         bias=negmax[:, i:i + 1], accum_out=den[:, j, h:h + 1]).then_inc(e_d, 1)
                    if i >= 1 and by_act[i - 1]:
                        empty(i - 1)
                if by_act[NU - 1]:
                    empty(NU - 1)
                fill("oT", oT[:, :], gen[gens.index("oT") % 2][:, :], ACT.Copy)
                fill("y", yT[:, :], gen[gens.index("y") % 2][:, :], ACT.Copy, scale=cur[:, 2:3])
                fill("h2", resT[:, bass.ds(b, 1), :], gen[gens.index("h2") % 2][:, :].rearrange("p (o t) -> p o t", o=1), ACT.Identity,
                     bias=cur[:, 3:4], scale=cur[:, 4:5])

        @block.vector
        def _(dve):
            nc.vector.memset(vecs[:, :, :], 0.0).then_inc(vec_z, 1)
            dve.wait_ge(ev_w, 1)
            for i in range(2):
                src = wT[:, i, :].rearrange("p (a two) -> p a two", two=2)
                dst = wT[:, 4 + i, :].rearrange("p (a two) -> p a two", two=2)
                nc.vector.tensor_scalar(dst[:, :, 0:1], src[:, :, 1:2], -1.0, None, ALU.mult).then_inc(rot_w, 1)
                nc.vector.tensor_copy(dst[:, :, 1:2], src[:, :, 0:1]).then_inc(rot_w, 1)
            dve.wait_ge(tr_v, 1)
            dve.wait_ge(vec_z, 1)
            for i, (o, w) in enumerate(pieces):
                nc.vector.tensor_copy(vecs[0:w, i, :], sc[2][0:w, 8 * i:8 * i + DEPTH]).then_inc(vec_e, 1)
            dve.wait_ge(mod_p, 1)
            nc.vector.tensor_copy(mod[:, :, :], gen[0][:, 0:6 * BATCH].rearrange("p (m b) -> p m b", m=6)).then_inc(mod_e, 1)
            dve.wait_ge(mod_e, 1)
            both = mod[:, 1:5:3, :]
            gates = mod[:, 2:6:3, :]
            nc.vector.tensor_scalar(both, both, 1.0, None, ALU.add).then_inc(mod_d, 1)
            nc.vector.tensor_scalar(sgn[:, :, :], gates, 0.0, 2.0, ALU.is_ge, ALU.mult).then_inc(mod_d, 1)
            dve.wait_ge(mod_d, 2)
            nc.vector.tensor_scalar(sgn[:, :, :], sgn[:, :, :], -1.0, None, ALU.add).then_inc(mod_d, 1)
            dve.wait_ge(mod_d, 3)
            nc.vector.tensor_tensor(gates, gates, sgn[:, :, :], ALU.mult).then_inc(mod_d, 1)
            dve.wait_ge(mod_d, 4)
            nc.vector.scalar_tensor_tensor(gates, gates, 0.25, sgn[:, :, :], ALU.max, ALU.mult).then_inc(mod_d, 1)
            dve.wait_ge(mod_d, 5)
            dve.wait_ge(x_in, 16)
            with nc.vector.Fori(0, BATCH) as b:
                nc.vector.tensor_copy(cur[:, :].rearrange("p (m o) -> p m o", o=1), mod[:, :, bass.ds(b, 1)]).then_inc(cur_d, 1)

                def norm(half):
                    base = b * 18 + 9 * half
                    for j in range(TILES):
                        nc.vector.bn_stats(stats[:, j:j + 1, :], xtok[:, bass.ds(b * TILES + j, 1), :]).then_inc(st, 1)
                    dve.wait_ge(st, base + 4)
                    dve.sem_inc(passed, 1)
                    for j in range(TILES):
                        nc.vector.bn_aggr(mv[:, j, :], stats[:, j, :]).then_inc(st, 1)
                    dve.wait_ge(st, base + 8)
                    nc.vector.tensor_scalar(var[:, :].rearrange("p (t o) -> p t o", o=1), mv[:, :, 1:2], 1e-5, None,
                                            ALU.add).then_inc(st, 1)
                    dve.wait_ge(st, base + 9)
                    rsqrt(nc, dve, var[:, :], rstd[:, :], var_t[:, :], rstd_d, (b * 2 + half) * RSQRT_STEPS)
                    for j in range(TILES):
                        nc.vector.tensor_scalar(xn[:, j:j + 1, :], xtok[:, bass.ds(b * TILES + j, 1), :], mv[:, j, 0:1],
                                                rstd[:, j:j + 1], ALU.subtract, ALU.mult).then_inc(nrm, 1)

                norm(0)
                for c, (name, rname) in enumerate((("q", "qr"), ("k", "kr"))):
                    dve.wait_ge(g_fill, gfull(b, name))
                    nc.vector.tensor_tensor(rot1[:, c, :], gen[gens.index(name) % 2][:, :], rope[:, 2 * c, :],
                                            ALU.mult).then_inc(g_dve, 1)
                    dve.wait_ge(g_fill, gfull(b, rname))
                    nc.vector.tensor_tensor(rot2[:, c, :], gen[gens.index(rname) % 2][:, :], rope[:, 2 * c + 1, :],
                                            ALU.mult).then_inc(g_dve, 1)
                    dve.wait_ge(*gfree(b, gens.index(rname)))
                    nc.vector.tensor_tensor(rot1[:, c, :], rot1[:, c, :], rot2[:, c, :], ALU.add).then_inc(rope_a, 1)
                for c in range(2):
                    dve.wait_ge(hi_d, b * 2 + c + 1)
                    nc.vector.tensor_tensor(qk_lo[:, c, :], rot1[:, c, :], qk_hi[:, c, :].bitcast(f32),
                                            ALU.subtract).then_inc(lo_d, 1)

                def empty(i):
                    h, j = units[i]
                    dve.wait_ge(t_full, b * NU + i + 1)
                    if i >= 2:
                        dve.wait_ge(o_full, b * NU + i - 1)
                    nc.vector.tensor_copy(probT[:, i % 2, 0:(j + 1) * P], pt[i % 2][:, 0:(j + 1) * P]).then_inc(t_dve, 1)

                for i, (h, j) in enumerate(units):
                    dve.wait_ge(s_full, b * NU + i + 1)
                    nc.vector.tensor_reduce(negmax[:, i:i + 1], sc[i % 3][:, 0:(j + 1) * P], AX.X, ALU.max,
                                            negate=True).then_inc(m_d, 1)
                    if i >= 2 and not by_act[i - 2]:
                        empty(i - 2)
                for i in (NU - 2, NU - 1):
                    if not by_act[i]:
                        empty(i)
                dve.wait_ge(e_d, (b + 1) * NU)
                nc.vector.reciprocal(rden[:, :, :], den[:, :, :]).then_inc(rd_d, 1)
                dve.wait_ge(rd_d, b + 1)
                dve.wait_ge(o_full, (b + 1) * NU)
                nc.vector.tensor_tensor(otok[:, :, :].rearrange("p t (h d) -> p t h d", h=A_HEADS),
                                        po[:, :].rearrange("p (t h d) -> p t h d", t=TILES, h=A_HEADS),
                                        rden[:, :, :].rearrange("p t (h o) -> p t h o", o=1).broadcast_to([P, TILES, A_HEADS, A_HDIM]),
                                        ALU.mult).then_inc(ot_d, 1)
                dve.wait_ge(g_fill, gfull(b, "yt"))
                xb = xtok[:, bass.ds(b * TILES, TILES), :]
                nc.vector.tensor_tensor(xb, gen[gens.index("yt") % 2][:, :].rearrange("p (t f) -> p t f", t=TILES), xb,
                                        ALU.add).then_inc(g_dve, 1)
                dve.wait_ge(*gfree(b, gens.index("yt")))
                dve.sem_inc(passed, 1)
                norm(1)
                dve.wait_ge(*gfree(b, gens.index("h2")))


def part_b(nc, t_in, alloc, need, resT, ident, win_mask, ident_bf, vecs):
    f32, f32r, bf16 = mybir.dt.float32, mybir.dt.float32r, mybir.dt.bfloat16
    ALU, ACT, AX = mybir.AluOpType, mybir.ActivationFunctionType, mybir.AxisListType
    ctx = ExitStack()
    with ctx:
        sb, ps, sem = alloc(ctx)
        w_raw = sb("wqkv_raw", [P, WCHUNK])
        w_hi = sb("wqkv_hi", [P, 2, QKV], f32r)
        w_lo = sb("wqkv_lo", [P, 2, QKV], f32r)
        wo = sb("wo", [P, 2, PAIRS, DIM])
        w1 = sb("w1", [P, 2 * FF])
        w2 = sb("w2", [P, 3, DIM])
        vec = sb("vec", [P, VECS])
        rope0 = sb("rope0", [P, 2, TILES, 2, HDIM])
        rope = sb("rope_b", [P, 2, TILES, 2, HDIM])
        qks = sb("qks", [P, 2, HDIM])
        mean_w = sb("mean_w", [P, P])
        xa_hi = sb("xa_hi", [P, WINDOW + TOKENS], f32r)
        xa_lo = sb("xa_lo", [P, WINDOW + TOKENS], f32r)
        squares = sb("squares", [P, INNER])
        ssum = sb("ssum", [P, 2, HEADS])
        rnorm = sb("rnorm", [P, 2, HEADS])
        rtmp = sb("rtmp", [P, 2, HEADS])
        var = sb("var_b", [P, 3, TILES])
        qkn = sb("qkn", [P, 2, INNER])
        rc = sb("rc", [P, 2, INNER])
        rs = sb("rs", [P, 2, INNER])
        qT = sb("qT", [P, PAIRS, P])
        kT = sb("kT", [P, PAIRS, WINDOW + TOKENS])
        prob = [sb(f"prob_b{i}", [P, PAIRS, 2, KEYS]) for i in range(2)]
        rmax = sb("rmax", [P, 2, PAIRS])
        rsum = sb("rsum", [P, PAIRS, 2])
        rinv = sb("rinv", [P, PAIRS, 2])
        pT = sb("pT", [P, PAIRS, P])
        vown = sb("vown", [P, 2, 2, PAIRS, HDIM])
        vmoved = sb("vmoved", [P, 3, PAIRS, HDIM])
        otok = sb("otok_b", [P, PAIRS, 2, HDIM])
        oT = sb("oT_b", [P, PAIRS, TOKENS])
        x1 = sb("x1", [P, TOKENS])
        xs = sb("xs", [P, TOKENS])
        xc = sb("xc", [P, TOKENS])
        hid = sb("hid", [P, 3, TOKENS])
        xq = hid[:, 0, :]
        dev = hid[:, 1, :].rearrange("p (t f) -> p t f", t=TILES)

        proj = [ps(f"proj{c}", [P, INNER]) for c in range(2)]
        ring = [ps(f"ring{i}", [P, 512]) for i in range(2)]
        scr = ps("scr", [P, 2, PAIRS, KEYS])

        qks_in = sem("qks_in"); consts_in = sem("consts_in"); raw_in = sem("raw_in"); wo_in = sem("wo_in")
        w1_in = sem("w1_in"); w2_in = sem("w2_in")
        zeroed = sem("zeroed")
        w_hi_done = sem("w_hi_done"); w_lo_done = sem("w_lo_done")
        x_hi_done = sem("x_hi_done"); x_lo_done = sem("x_lo_done")
        moved = sem("moved"); add_done = sem("add_done")
        pe_passed = sem("pe_passed"); sp_passed = sem("sp_passed")
        rope_done = sem("rope_done")
        proj_full = sem("proj_full"); sq_done = sem("sq_done"); ss_done = sem("ss_done")
        clamp_done = sem("clamp_done"); spread_done = sem("spread_done")
        rn_done = sem("rn_done"); qkn_done = sem("qkn_done"); rc_done = sem("rc_done"); rs_done = sem("rs_done")
        fill = sem("fill"); act_free = sem("act_free"); dve_free = sem("dve_free")
        scr_full = sem("scr_full"); max_done = sem("max_done"); sub_done = sem("sub_done")
        exp_done = sem("exp_done"); sum_done = sem("sum_done"); inv_done = sem("inv_done")
        prob_done = sem("prob_done")
        xs_done = sem("xs_done"); xq_done = sem("xq_done"); rstd_done = sem("rstd_done")
        h_done = sem("h_done")
        vec_done = sem("vec_done"); res_done = sem("res_done")
        block = ctx.enter_context(nc.Block())

        wqkv = t_in["L0_ffn_Wqkv"]
        half_tokens = TOKENS // 2
        stage = [[(slice(0, 64), WINDOW, 0, half_tokens), (slice(64, P), WINDOW + 1, 0, half_tokens - 1)],
                 [(slice(0, 64), WINDOW + half_tokens, half_tokens, half_tokens),
                  (slice(64, P), WINDOW + half_tokens, half_tokens - 1, half_tokens)]]

        def pipelined(eng, engine, body):
            body(0, True, False)
            with engine.Fori(1, NSEQ) as n:
                body(n, True, True)
            body(NSEQ, False, True)

        def free_before(n, name):
            kind = FILL.first if isinstance(n, int) and n == 0 else \
                FILL.last if isinstance(n, int) and n == NSEQ else FILL.steady
            i = kind.index(name)
            for k in range(i - 1, -1, -1):
                if bank_of(kind[k]) == bank_of(name):
                    e = kind[k]
                    return (dve_free, DVE_FREE.at(n, e)) if e in BY_VECTOR else (act_free, ACT_FREE.at(n, e))
            if kind is FILL.first:
                return act_free, 0
            return act_free, ACT_FREE.all_before(n)

        @block.sync
        def _(sp):
            sp.dma_start(rope0[:, :, :, :, :], t_in["b_rope"]).then_inc(consts_in, 16)

            def load_qks(layer):
                for c, name in enumerate(("L0_ffn_q_scale", "L0_ffn_k_scale")):
                    sp.dma_start(qks[:, c, :], t_in[name][layer, :].broadcast_to([P, HDIM])).then_inc(qks_in, 16)

            load_qks(bass.ds(0, 1))
            def load_wo(layer):
                src = t_in["L0_ffn_Wo"][layer, :, :]
                sp.dma_start(wo[:, 0, :, :], src.rearrange("l (c p) f -> p (l c) f", p=P)).then_inc(wo_in, 16)
                for s in range(2):
                    sp.dma_start(wo[64 * s:64 * s + 64, 1, :, :],
                                 src.rearrange("l (c s p) f -> s p (l c) f", s=2, p=64)[1 - s, :, :, :]).then_inc(wo_in, 16)

            def load_ffn(layer):
                sp.dma_start(w1[:, :], t_in["L0_ffn_W1"][layer, :, :].rearrange("l p f -> p (l f)")).then_inc(w1_in, 16)
                w2v = t_in["L0_ffn_W2"]
                sp.dma_start(w2[:, 0:2, :], w2v[layer, 0:2 * P, :].rearrange("l (c p) f -> p (l c) f", p=P)).then_inc(w2_in, 16)
                sp.dma_start(w2[0:FF - 2 * P, 2, :], w2v[layer, 2 * P:FF, :].rearrange("l p f -> p (l f)")).then_inc(w2_in, 16)

            for s in range(BATCH):
                need(sp, w_lo_done, s)
                sp.dma_start(w_raw[:, :], wqkv[0, :, s * WCHUNK:(s + 1) * WCHUNK]).then_inc(raw_in, 16)
            load_wo(bass.ds(0, 1))
            load_ffn(bass.ds(0, 1))

            def body(n, cur, prev):
                for j in range(TILES):
                    if cur and j == 0:
                        sp.wait_ge(w_lo_done, BATCH + n)
                        src = wqkv[bass.ds((n // BATCH + 1) % DEPTH, 1), :, bass.ds((n % BATCH) * WCHUNK, WCHUNK)]
                        sp.dma_start(w_raw[:, :], src.rearrange("l p f -> p (l f)")).then_inc(raw_in, 16)
                        sp.wait_ge(rope_done, n * 3 + 3)
                        load_qks(bass.ds(((n + 1) // BATCH) % DEPTH, 1))
                    if cur and prev:
                        layer = bass.ds(n // BATCH, 1)
                        if j == 1:
                            sp.wait_ge(fill, FILL.at(n, "wo1'"))
                            load_wo(layer)
                        if j == 3:
                            sp.wait_ge(fill, FILL.at(n, "down'"))
                            load_ffn(layer)
                    if cur:
                        sp.wait_ge(act_free, ACT_FREE.at(n, f"V{j}1"))
                        sp.sem_inc(sp_passed, 1)
                        if j or prev:
                            sp.wait_ge(fill, FILL.at(n, f"O{(j - 1) % TILES}1" + ("" if j else "'")))
                        own, before = vown[:, j % 2, :, :, :], vown[:, 1 - j % 2, :, :, :]
                        for dst, k, rows, src, b in ((64, 0, 64, own[0:64], 1), (0, 0, 64, own[64:P], 1),
                                                     (32, 1, 96, own[0:96], 0), (0, 1, 32, before[96:P], 0),
                                                     (0, 2, 64, own[32:96], 1), (96, 2, 32, own[0:32], 1),
                                                     (64, 2, 32, before[96:P], 1)):
                            sp.dma_start(vmoved[dst:dst + rows, k, :, :], src[:, b, :, :]).then_inc(moved, 16)
            pipelined(sp, nc.sync, body)

        @block.tensor
        def _(pe):
            pe.wait_ge(zeroed, 6)

            def body(n, cur, prev):
                m = n - 1
                parity = (n // BATCH) % 2

                def begin(name):
                    need(pe, *free_before(n, name))
                    return ring[bank_of(name)]

                def split_product(bank, x_cols, w_cols):
                    nc.tensor.matmul(bank, xa_hi[:, x_cols], w_cols(w_hi), start=True, stop=False)
                    nc.tensor.matmul(bank, xa_hi[:, x_cols], w_cols(w_lo), start=False, stop=False)
                    return nc.tensor.matmul(bank, xa_lo[:, x_cols], w_cols(w_hi), start=False, stop=True)

                def project(j, q, c):
                    if j == 0 and c == 0:
                        pe.wait_ge(x_lo_done, 2 + q * 4)
                        pe.wait_ge(w_lo_done, BATCH + q)
                    if j == 2 and c == 0:
                        pe.wait_ge(x_lo_done, 4 + q * 4)
                    xcols = slice(WINDOW + j * P, WINDOW + (j + 1) * P)
                    par = (q // BATCH) % 2
                    need(pe, qkn_done, q * 8 + 2 * j + c - 1)
                    for k in range(2):
                        off = c * INNER + k * 512

                        def cols(w, off=off):
                            return w[:, bass.ds(par, 1), off:off + 512]
                        last = split_product(proj[c][:, k * 512:(k + 1) * 512], xcols, cols)
                    last.then_inc(proj_full, 1)

                def values(t, b):
                    start = WINDOW + t * P
                    bank = begin(f"V{t}{b}")

                    def cols(w):
                        return w[:, bass.ds(parity, 1), 2 * INNER:3 * INNER].rearrange(
                            "p o (q h d) -> p (o q) h d", h=2, d=HDIM)[:, :, b, :]
                    split_product(bank[:, :], slice(start, start + P), cols).then_inc(fill, 1)

                def transpose_probs(t, mark):
                    pe.wait_ge(prob_done, (m if mark else n) * 4 + t + 1)
                    for i in range(2):
                        bank = begin(f"P{t}{i}{mark}")
                        for p in range(4):
                            last = nc.tensor.transpose(bank[:, p * P:(p + 1) * P], prob[t % 2][:, 4 * i + p, :, :].rearrange("p s k -> p (s k)"), ident[:, :])
                        last.then_inc(fill, 1)

                def weigh(t, mark):
                    pe.wait_ge(act_free, ACT_FREE.at(n, f"P{t}1{mark}"))
                    pe.wait_ge(moved, ((m if mark else n) * 4 + t + 1) * 7 * 16)
                    for s in range(2):
                        bank = begin(f"O{t}{s}{mark}")[:, :].rearrange("p (q k) -> p q k", q=PAIRS)
                        pe.sem_inc(pe_passed, 1)
                        for p in range(PAIRS):
                            for w in range(4):
                                b = s ^ (w // 2)
                                k = (w % 2 == 0) * 2 + b - 1
                                v = vown[:, t % 2, 0, p, :] if k < 0 else vmoved[:, k, p, :]
                                last = nc.tensor.matmul(
                                    bank[32 * w:32 * w + 32, p, :], pT[64 * s:64 * s + 64, p, 32 * w:32 * w + 32],
                                    v[64 * s:64 * s + 64, :], start=True, stop=True)
                        last.then_inc(fill, 1)

                def turn(t, mark):
                    pe.wait_ge(act_free, ACT_FREE.at(n, f"O{t}1{mark}"))
                    for i in range(2):
                        bank = begin(f"Q{t}{i}{mark}")
                        for p in range(4):
                            last = nc.tensor.transpose(bank[:, p * P:(p + 1) * P],
                                                       otok[:, 4 * i + p, :, :].rearrange("p s d -> p (s d)"), ident[:, :])
                        last.then_inc(fill, 1)

                def feed_down():
                    pe.wait_ge(w2_in, n * 32)
                    pe.wait_ge(dve_free, DVE_FREE.at(n, "up5'"))
                    bank = begin("down'")
                    for i, (o, w) in enumerate(FFC):
                        last = nc.tensor.matmul(bank[:, :], w2[0:w, i, :], hid[0:w, i, :], start=(i == 0), stop=(i == 2))
                    last.then_inc(fill, 1)

                def transpose_qk(j, k):
                    for c in range(2):
                        if k == 0:
                            pe.wait_ge(add_done, n * 8 + 2 * j + c + 1)
                        bank = begin(f"T{j}{2 * k + c}")
                        for p in range(4):
                            o = (4 * k + p) * P
                            last = nc.tensor.transpose(bank[:, p * P:(p + 1) * P], rc[:, c, o:o + P], ident[:, :])
                        last.then_inc(fill, 1)

                def score(j, k):
                    pe.wait_ge(act_free, ACT_FREE.at(n, f"T{j}{2 * k + 1}"))
                    if k == 0:
                        need(pe, sub_done, n * 4 + j)
                        for s in range(2):
                            mask = win_mask[j].rearrange("p (o k) -> p o k", o=1).broadcast_to([P, PAIRS, KEYS])
                            nc.tensor.matmul(scr[:, s, :, :], ident_bf, mask, start=True, stop=True)
                    else:
                        pe.sem_inc(pe_passed, 1)
                    for p in range(4 * k, 4 * k + 4):
                        for b in range(2):
                            for w in range(4):
                                s = b ^ (w // 2)
                                rows = slice(64 * b, 64 * b + 64)
                                last = nc.tensor.matmul(
                                    scr[32 * w:32 * w + 32, s, p, :], qT[rows, p, 32 * w:32 * w + 32],
                                    kT[rows, p, j * P + 32 * w:j * P + 32 * w + KEYS],
                                    start=False, stop=True, skip_group_check=True)
                    if k:
                        last.then_inc(scr_full, 1)

                if isinstance(n, int) and n == 0:
                    for c in range(2):
                        project(0, 0, c)

                def output(i):
                    pe.wait_ge(wo_in, n * 48)
                    pe.wait_ge(act_free, ACT_FREE.at(n, "Q31'"))
                    bank = begin(f"wo{i}'")
                    for p in range(PAIRS):
                        ot = oT[:, p, :].rearrange("p (t i k) -> p t i k", t=TILES, i=2)[:, :, i, :]
                        last = nc.tensor.matmul(bank[:, 0:TOKENS // 2], wo[:, i, p, :], ot, start=(p == 0),
                                                stop=(p == PAIRS - 1))
                    last.then_inc(fill, 1)

                def feed_up(first):
                    pe.wait_ge(w1_in, n * 16)
                    pe.wait_ge(h_done, m + 1)
                    for i in range(3):
                        o, w = FFC[i]
                        o += FF if first == 0 else 0
                        bank = begin(f"up{first + i}'")
                        nc.tensor.matmul(bank[0:w, :], w1[:, o:o + w], xc[:, :], start=True, stop=True).then_inc(fill, 1)

                for j in range(TILES):
                    t, mark = (j - 1) % TILES, "'" if j == 0 else ""
                    on = prev if j == 0 else cur
                    ahead = (j + 1, n) if j < TILES - 1 else (0, n + 1)
                    if prev and j == 3:
                        feed_up(0)
                    if cur:
                        project(*ahead, 0)
                    if prev and j == 1:
                        output(0)
                    if cur:
                        transpose_qk(j, 0)
                        project(*ahead, 1)
                    if prev and j == 1:
                        output(1)
                    if cur:
                        transpose_qk(j, 1)
                    if prev and j == 2:
                        pe.wait_ge(xq_done, m + 1)
                        bank = begin("var'")
                        for i in range(TILES):
                            last = nc.tensor.matmul(bank[:, i:i + 1], xq[:, i * P:(i + 1) * P], mean_w[:, 0:1],
                                                    start=True, stop=True)
                        last.then_inc(fill, 1)
                    if cur:
                        score(j, 0)
                        values(j, 0)
                        score(j, 1)
                    if on:
                        transpose_probs(t, mark)
                    if cur and j == 0:
                        values(j, 1)
                    if prev and j == 3:
                        feed_up(3)
                    if prev and j == 1:
                        pe.wait_ge(xs_done, n * 2)
                        bank = begin("mean'")
                        nc.tensor.matmul(bank[:, :], mean_w[:, :], xs[:, :], start=True, stop=True).then_inc(fill, 1)
                    if prev and j == 2:
                        pe.wait_ge(spread_done, m + 1)
                        bank = begin("spread'")
                        for i in range(TILES):
                            last = nc.tensor.transpose(bank[:, i * P:(i + 1) * P], dev[:, i, :], ident[:, :])
                        last.then_inc(fill, 1)
                    if on:
                        weigh(t, mark)
                    if cur and j:
                        values(j, 1)
                    if on:
                        turn(t, mark)
                    if prev and j == 3:
                        feed_down()
            pipelined(pe, nc.tensor, body)

        @block.scalar
        def _(act):
            act.wait_ge(zeroed, 6)

            def stage_hi(seq, half):
                for rows, col, tok, width in stage[half]:
                    nc.scalar.activation(xa_hi[rows, col:col + width], resT[rows, seq, tok:tok + width],
                                         ACT.Copy).then_inc(x_hi_done, 1)

            def split_hi(parity, off, count):
                act.wait_ge(raw_in, count)
                nc.scalar.activation(w_hi[:, parity, off], w_raw[:, :].rearrange("p (o f) -> p o f", o=1),
                                     ACT.Copy).then_inc(w_hi_done, 1)

            for s in range(BATCH):
                split_hi(slice(0, 1), slice(s * WCHUNK, (s + 1) * WCHUNK), (s + 1) * 16)
            stage_hi(slice(0, 1), 0)

            def body(n, cur, prev):
                m = n - 1

                def empty(name, dst, src=None):
                    act.wait_ge(fill, FILL.at(n, name))
                    nc.scalar.activation(dst, ring[bank_of(name)][:, :] if src is None else src, ACT.Copy).then_inc(act_free, 1)

                def squares_of(j, q, c):
                    act.wait_ge(proj_full, q * 8 + 2 * j + c + 1)
                    need(act, ss_done, q * 8 + 2 * j + c)
                    nc.scalar.activation(squares[:, :], proj[c][:, :], ACT.Square).then_inc(sq_done, 1)

                if isinstance(n, int) and n == 0:
                    for c in range(2):
                        squares_of(0, 0, c)
                for j in range(TILES):
                    t, mark = (j - 1) % TILES, "'" if j == 0 else ""
                    on = prev if j == 0 else cur
                    ahead = (j + 1, n) if j < TILES - 1 else (0, n + 1)

                    def qk_out(k):
                        for c, dst in enumerate((qT[:, 4 * k:4 * k + 4, :],
                                                 kT[:, 4 * k:4 * k + 4, WINDOW + j * P:WINDOW + (j + 1) * P])):
                            name = f"T{j}{2 * k + c}"
                            empty(name, dst, ring[bank_of(name)][:, :].rearrange("p (q k) -> p q k", q=4))

                    def values_out(b):
                        name = f"V{j}{b}"
                        if b == 0:
                            need(act, moved, (n * 4 + j) * 7 * 16)
                        empty(name, vown[:, j % 2, b, :, :],
                              ring[bank_of(name)][:, :].rearrange("p (q d) -> p q d", q=PAIRS))

                    if prev and j == 3:
                        for i in range(3):
                            w = FFC[i][1]
                            act.wait_ge(fill, FILL.at(n, f"up{i}'"))
                            nc.scalar.activation(hid[0:w, i, :], ring[bank_of(f"up{i}'")][0:w, :], ACT.Gelu,
                                                 bias=vec[0:w, 6 + i:7 + i]).then_inc(act_free, 1)
                    if cur:
                        squares_of(*ahead, 0)
                        qk_out(0)
                        squares_of(*ahead, 1)
                    if prev and j == 1:
                        act.wait_ge(dve_free, DVE_FREE.at(n, "wo1'"))
                        nc.scalar.activation(xs[0:64, :], x1[0:64, :], ACT.Copy).then_inc(xs_done, 1)
                        nc.scalar.activation(xs[64:P, 1:TOKENS], x1[64:P, 0:TOKENS - 1], ACT.Copy).then_inc(xs_done, 1)
                    if cur:
                        qk_out(1)
                    if cur and j == 0:
                        stage_hi(bass.ds(n % BATCH, 1), 1)
                    if cur and j == 2:
                        stage_hi(bass.ds((n + 1) % BATCH, 1), 0)
                    if cur:
                        values_out(0)
                    if on:
                        for i in range(2):
                            name = f"P{t}{i}{mark}"
                            empty(name, pT[:, 4 * i:4 * i + 4, :], ring[bank_of(name)][:, :].rearrange("p (q k) -> p q k", q=4))
                    if cur and j == 0:
                        values_out(1)
                    if cur:
                        act.wait_ge(sub_done, n * 4 + j + 1)
                        pr = prob[j % 2][:, :, :, :]
                        nc.scalar.activation(pr, pr, ACT.Exp).then_inc(exp_done, 1)
                    if prev and j == 2:
                        act.wait_ge(vec_done, n)
                        act.wait_ge(dve_free, DVE_FREE.at(n, "spread'"))
                        nc.scalar.activation(xc[:, :], xc[:, :], ACT.Identity, bias=vec[:, 1:2],
                                             scale=vec[:, 0:1]).then_inc(h_done, 1)
                    if on:
                        for s in range(2):
                            name = f"O{t}{s}{mark}"
                            empty(name, otok[:, :, s, :],
                                  ring[bank_of(name)][:, :].rearrange("p (q k) -> p q k", q=PAIRS))
                    if cur and j:
                        values_out(1)
                    if on:
                        for i in range(2):
                            name = f"Q{t}{i}{mark}"
                            empty(name, oT[:, 4 * i:4 * i + 4, t * P:(t + 1) * P],
                                  ring[bank_of(name)][:, :].rearrange("p (q k) -> p q k", q=4))
                    if prev and j == 1:
                        act.wait_ge(dve_free, DVE_FREE.at(n, "mean'"))
                        nc.scalar.activation(xq, xc[:, :], ACT.Square).then_inc(xq_done, 1)
                    if prev and j == 3:
                        act.wait_ge(fill, FILL.at(n, "down'"))
                        nc.scalar.activation(xc[:, :], ring[bank_of("down'")][:, :], ACT.Identity,
                                             bias=vec[:, 2:3]).then_inc(act_free, 1)
                    if cur and j == 1:
                        split_hi(bass.ds((n // BATCH + 1) % 2, 1), bass.ds((n % BATCH) * WCHUNK, WCHUNK),
                                 (n + 1 + BATCH) * 16)
            pipelined(act, nc.scalar, body)

        @block.gpsimd
        def _(pool):
            nc.gpsimd.memset(xa_hi[:, 0:WINDOW + 1].bitcast(f32), 0.0).then_inc(zeroed, 1)
            nc.gpsimd.memset(xa_lo[:, 0:WINDOW + 1].bitcast(f32), 0.0).then_inc(zeroed, 1)
            nc.gpsimd.memset(kT[:, :, 0:WINDOW], 0.0).then_inc(zeroed, 1)
            nc.gpsimd.memset(xs[:, 0:1], 0.0).then_inc(zeroed, 1)
            nc.gpsimd.memset(mean_w[:, :], 1.0 / DIM).then_inc(zeroed, 1)
            nc.gpsimd.memset(vown[:, 1, :, :, :], 0.0).then_inc(zeroed, 1)
            pool.wait_ge(consts_in, 16)

            def split_lo(parity, off, count):
                pool.wait_ge(w_hi_done, count)
                nc.gpsimd.tensor_tensor(w_lo[:, parity, off], w_raw[:, :].rearrange("p (o f) -> p o f", o=1),
                                        w_hi[:, parity, off].bitcast(f32), ALU.subtract).then_inc(w_lo_done, 1)

            def load_vec(layer):
                nc.gpsimd.tensor_copy(vec[:, :].rearrange("p (v o) -> p v o", o=1), vecs[:, :, layer]).then_inc(vec_done, 1)

            for s in range(BATCH):
                split_lo(slice(0, 1), slice(s * WCHUNK, (s + 1) * WCHUNK), s + 1)
            load_vec(slice(0, 1))

            def body(n, cur, prev):
                def make_rope(q):
                    need(pool, rs_done, q * 8)
                    need(pool, rc_done, q * 8)
                    pool.wait_ge(qks_in, q * 32 + 32)
                    nc.gpsimd.tensor_tensor(rope[:, 0, :, :, :], rope0[:, 0, :, :, :],
                                            qks[:, :, :].rearrange("p (o c) d -> p o c d", o=1).broadcast_to([P, TILES, 2, HDIM]), ALU.mult).then_inc(rope_done, 1)
                    for s in range(2):
                        h, o = slice(32 * s, 32 * s + 32), slice(32 - 32 * s, 64 - 32 * s)
                        nc.gpsimd.tensor_tensor(rope[:, 1, :, :, h], rope0[:, 1, :, :, h],
                                                qks[:, :, o].rearrange("p (o c) d -> p o c d", o=1).broadcast_to([P, TILES, 2, HDIM // 2]), ALU.mult).then_inc(rope_done, 1)
                    pool.wait_ge(rope_done, q * 3 + 3)

                def turned_half(j, q):
                    for c in range(2):
                        u = 2 * j + c
                        pool.wait_ge(qkn_done, q * 8 + u + 1)
                        need(pool, add_done, q * 8 + u - 1)
                        src = qkn[:, c, :].rearrange("p (h s d) -> p h s d", h=HEADS, s=2)
                        dst = rs[:, c, :].rearrange("p (h s d) -> p h s d", h=HEADS, s=2)
                        tab = rope[:, 1, j, c, :].rearrange("p (o s d) -> p o s d", o=1, s=2)
                        for s in range(2):
                            ins = nc.gpsimd.tensor_tensor(dst[:, :, s, :], src[:, :, 1 - s, :],
                                                          tab[:, :, s, :].broadcast_to([P, HEADS, HDIM // 2]),
                                                          ALU.mult)
                        ins.then_inc(rs_done, 1)

                if isinstance(n, int) and n == 0:
                    make_rope(0)
                    turned_half(0, 0)
                if cur:
                    for j in range(TILES):
                        if j == 3:
                            make_rope(n + 1)
                        turned_half(*((j + 1, n) if j < TILES - 1 else (0, n + 1)))
                        pool.wait_ge(inv_done, n * 4 + j + 1)
                        pr = prob[j % 2][:, :, :, :]
                        nc.gpsimd.tensor_tensor(
                            pr, pr, rinv[:, :, :].rearrange("p q (s o) -> p q s o", o=1).broadcast_to([P, PAIRS, 2, KEYS]),
                            ALU.mult).then_inc(prob_done, 1)
                        if j == 1:
                            split_lo(bass.ds((n // BATCH + 1) % 2, 1), bass.ds((n % BATCH) * WCHUNK, WCHUNK), n + 1 + BATCH)
                if prev:
                    seq = bass.ds((n - 1) % BATCH, 1)
                    pool.wait_ge(act_free, ACT_FREE.at(n, "down'"))
                    nc.gpsimd.tensor_tensor(resT[:, seq, :], xc[:, :].rearrange("p (o t) -> p o t", o=1),
                                            x1[:, :].rearrange("p (o t) -> p o t", o=1), ALU.add).then_inc(res_done, 1)
                    if cur:
                        load_vec(bass.ds(n // BATCH, 1))
            pipelined(pool, nc.gpsimd, body)

        @block.vector
        def _(dve):
            dve.wait_ge(zeroed, 6)
            dve.wait_ge(consts_in, 16)

            def stage_lo(seq, half, count):
                for i, (rows, col, tok, width) in enumerate(stage[half]):
                    dve.wait_ge(x_hi_done, count + i + 1)
                    nc.vector.tensor_tensor(xa_lo[rows, col:col + width], resT[rows, seq, tok:tok + width],
                                            xa_hi[rows, col:col + width].bitcast(f32), ALU.subtract).then_inc(x_lo_done, 1)

            stage_lo(slice(0, 1), 0, 0)

            def body(n, cur, prev):
                m = n - 1
                def norms_of(j, q, between=False):
                    for c in range(2):
                        if between:
                            add_attention(c)
                        dve.wait_ge(sq_done, q * 8 + 2 * j + c + 1)
                        nc.vector.tensor_reduce(ssum[:, c, :], squares[:, :].rearrange("p (h d) -> p h d", h=HEADS),
                                                AX.X, ALU.add).then_inc(ss_done, 1)
                    dve.wait_ge(ss_done, q * 8 + 2 * j + 2)
                    nc.vector.tensor_scalar(ssum[:, :, :], ssum[:, :, :], 1e-24, None, ALU.max).then_inc(clamp_done, 1)
                    dve.wait_ge(clamp_done, q * 4 + j + 1)
                    rsqrt(nc, dve, ssum[:, :, :], rnorm[:, :, :], rtmp[:, :, :], rn_done, (q * 4 + j) * RSQRT_STEPS)

                def r3(ap):
                    return ap.rearrange("p (o t) -> p o t", o=1)

                def normalise(c, j, q):
                    u = q * 8 + 2 * j + c
                    need(dve, rs_done, u - 1)
                    nc.vector.tensor_tensor(
                        qkn[:, c, :].rearrange("p (h d) -> p h d", h=HEADS),
                        proj[c][:, :].rearrange("p (h d) -> p h d", h=HEADS),
                        rnorm[:, c, :].rearrange("p (h o) -> p h o", o=1).broadcast_to([P, HEADS, HDIM]),
                        ALU.mult).then_inc(qkn_done, 1)

                def straight_half(c, j, q):
                    if j == 0 and c == 0:
                        dve.wait_ge(rope_done, q * 3 + 3)
                    dve.wait_ge(qkn_done, q * 8 + 2 * j + c + 1)
                    nc.vector.tensor_tensor(
                        rc[:, c, :].rearrange("p (h d) -> p h d", h=HEADS),
                        qkn[:, c, :].rearrange("p (h d) -> p h d", h=HEADS),
                        rope[:, 0, j, c:c + 1, :].broadcast_to([P, HEADS, HDIM]), ALU.mult).then_inc(rc_done, 1)

                def add_halves(c, j, q):
                    dve.wait_ge(rs_done, q * 8 + 2 * j + c + 1)
                    dve.wait_ge(rc_done, q * 8 + 2 * j + c + 1)
                    nc.vector.tensor_tensor(rc[:, c, :], rc[:, c, :], rs[:, c, :], ALU.add).then_inc(add_done, 1)

                def add_attention(i):
                    dve.wait_ge(fill, FILL.at(n, f"wo{i}'"))

                    def part(ap):
                        return ap.rearrange("p o (t i k) -> p (o t) i k", t=TILES, i=2)[:, :, i, :]
                    nc.vector.tensor_tensor(part(r3(x1[:, :])),
                                            ring[bank_of(f"wo{i}'")][:, 0:TOKENS // 2].rearrange("p (t k) -> p t k", t=TILES),
                                            part(resT[:, seq, :]), ALU.add).then_inc(dve_free, 1)

                if isinstance(n, int) and n == 0:
                    norms_of(0, 0)
                    for c in range(2):
                        normalise(c, 0, 0)
                        straight_half(c, 0, 0)
                    for c in range(2):
                        add_halves(c, 0, 0)
                seq = bass.ds(m % BATCH, 1)
                for j in range(TILES):
                    ahead = (j + 1, n) if j < TILES - 1 else (0, n + 1)
                    if prev and j == 1 and not cur:
                        dve.wait_ge(res_done, n - 1)
                        add_attention(0)
                        add_attention(1)
                    if cur:
                        norms_of(*ahead, j == 1 and prev)
                    if cur and j == 0:
                        stage_lo(bass.ds(n % BATCH, 1), 1, 2 + n * 4)
                    if cur and j == 2:
                        stage_lo(bass.ds((n + 1) % BATCH, 1), 0, 4 + n * 4)
                    if prev and j == 2:
                        dve.wait_ge(fill, FILL.at(n, "var'"))
                        nc.vector.tensor_scalar(var[:, 0, :], ring[bank_of("var'")][:, 0:TILES], 1e-5, None, ALU.add)\
                          .then_inc(dve_free, 1)
                        dve.wait_ge(dve_free, DVE_FREE.at(n, "var'"))
                        rsqrt(nc, dve, var[:, 0, :], var[:, 1, :], var[:, 2, :], rstd_done, m * RSQRT_STEPS)
                        nc.vector.tensor_copy(dev, var[:, 1, :].rearrange("p (t o) -> p t o", o=1).broadcast_to([P, TILES, P]))\
                          .then_inc(spread_done, 1)
                    if cur:
                        dve.wait_ge(scr_full, n * 4 + j + 1)
                        nc.vector.tensor_reduce(rmax[:, :, :], scr[:, :, :, :], AX.X, ALU.max).then_inc(max_done, 1)
                        dve.wait_ge(max_done, n * 4 + j + 1)
                        nc.vector.tensor_tensor(
                            prob[j % 2][:, :, :, :].rearrange("p q s k -> p s q k"), scr[:, :, :, :],
                            rmax[:, :, :].rearrange("p s (q o) -> p s q o", o=1).broadcast_to([P, 2, PAIRS, KEYS]),
                            ALU.subtract).then_inc(sub_done, 1)
                    if prev and j == 1:
                        dve.wait_ge(fill, FILL.at(n, "mean'"))
                        nc.vector.tensor_tensor(xc[:, :], xs[:, :], ring[bank_of("mean'")][:, :], ALU.subtract).then_inc(dve_free, 1)
                    if prev and j == 2:
                        dve.wait_ge(fill, FILL.at(n, "spread'"))
                        nc.vector.tensor_tensor(xc[:, :], xc[:, :], ring[bank_of("spread'")][:, :], ALU.mult).then_inc(dve_free, 1)
                    if prev and j == 3:
                        for i in range(3):
                            w = FFC[i][1]
                            name = f"up{3 + i}'"
                            dve.wait_ge(act_free, ACT_FREE.at(n, f"up{i}'"))
                            dve.wait_ge(fill, FILL.at(n, name))
                            nc.vector.scalar_tensor_tensor(hid[0:w, i, :], ring[bank_of(name)][0:w, :], vec[0:w, 3 + i:4 + i],
                                                           hid[0:w, i, :], ALU.add, ALU.mult).then_inc(dve_free, 1)
                    if cur:
                        dve.wait_ge(rn_done, (ahead[1] * 4 + ahead[0] + 1) * RSQRT_STEPS)
                        normalise(0, *ahead)
                        dve.wait_ge(exp_done, n * 4 + j + 1)
                        nc.vector.tensor_reduce(rsum[:, :, :], prob[j % 2][:, :, :, :], AX.X, ALU.add).then_inc(sum_done, 1)
                    if cur:
                        normalise(1, *ahead)
                        dve.wait_ge(sum_done, n * 4 + j + 1)
                        need(dve, prob_done, n * 4 + j)
                        nc.vector.reciprocal(rinv[:, :, :], rsum[:, :, :]).then_inc(inv_done, 1)
                        for c in range(2):
                            dve.wait_ge(fill, FILL.at(n, f"T{j}{2 + c}"))
                            straight_half(c, *ahead)
                    if cur:
                        for c in range(2):
                            add_halves(c, *ahead)
            pipelined(dve, nc.vector, body)


def part_c(nc, out, alloc, need, x_attended, resT, ident, mod):
    f32 = mybir.dt.float32
    ALU, ACT = mybir.AluOpType, mybir.ActivationFunctionType
    ctx = ExitStack()
    with ctx:
        sb, ps, sem = alloc(ctx)
        yt = [ps(f"yt{i}", [P, TOKENS]) for i in range(2)]
        xtok = sb("xtok_c", [P, BATCH * TILES, DIM])
        x_back = sem("x_back"); scaled = sem("scaled"); turned = sem("turned"); added = sem("added"); stored = sem("stored")
        block = ctx.enter_context(nc.Block())
        ov = out.rearrange("b (t p) d -> p b t d", p=P)

        @block.scalar
        def _(act):
            for b in range(BATCH):
                nc.scalar.activation(resT[:, b, :], resT[:, b, :], ACT.Copy, scale=mod[:, 5, b:b + 1]).then_inc(scaled, 1)

        @block.tensor
        def _(pe):
            for b in range(BATCH):
                pe.wait_ge(scaled, b + 1)
                need(pe, added, b - 1)
                for j in range(TILES):
                    last = nc.tensor.transpose(yt[b % 2][:, j * P:(j + 1) * P], resT[:, b, j * P:(j + 1) * P], ident[:, :])
                last.then_inc(turned, 1)

        @block.vector
        def _(dve):
            for b in range(BATCH):
                dve.wait_ge(x_back, 16 * BATCH)
                dve.wait_ge(turned, b + 1)
                xb = xtok[:, b * TILES:(b + 1) * TILES, :]
                nc.vector.tensor_tensor(xb, yt[b % 2][:, :].rearrange("p (t f) -> p t f", t=TILES), xb, ALU.add).then_inc(added, 1)

        @block.sync
        def _(sp):
            for b in range(BATCH):
                tiles = slice(b * TILES, (b + 1) * TILES)
                sp.dma_start(xtok[:, tiles, :], x_attended[:, tiles, :]).then_inc(x_back, 16)
            for b in range(BATCH):
                sp.wait_ge(added, b + 1)
                sp.dma_start(ov[:, b, :, :], xtok[:, b * TILES:(b + 1) * TILES, :]).then_inc(stored, 16)
            sp.wait_ge(stored, 16 * BATCH)


_INS = ['L0_attn_x', 'L0_attn_Wq', 'L0_attn_Wk', 'L0_attn_Wv', 'L0_attn_Wo', 'L0_ffn_Wqkv', 'L0_ffn_q_scale',
        'L0_ffn_k_scale', 'L0_ffn_Wo', 'L0_ffn_ln_g', 'L0_ffn_ln_b', 'L0_ffn_W1', 'L0_ffn_b1', 'L0_ffn_W2',
        'L0_ffn_b2', 'L0_c', 'L0_wmod']


def kernel(**inputs):
    import numpy as _np
    import concourse.bacc as _bacc
    from concourse import mybir as _mybir
    from concourse.bass_utils import run_bass_kernel_spmd as _run

    nc = _bacc.Bacc("TRN2", target_bir_lowering=False, num_devices=1)
    arrays, args = {}, {}
    given = {name: _np.ascontiguousarray(inputs[name]) for name in _INS}
    given.update(constants())
    for name, a in given.items():
        arrays[f"in_{name}"] = a
        args[name] = nc.dram_tensor(f"in_{name}", a.shape, _mybir.dt.from_np(a.dtype), kind="ExternalInput").ap()
    o = nc.dram_tensor("out_0", (BATCH, TOKENS, DIM), _mybir.dt.float32, kind="ExternalOutput").ap()
    program(nc, args, o)
    r = _run(nc, [arrays], core_ids=[0])
    return r.results[0]["out_0"]
```

```python
import concourse.bass as bass
from concourse import mybir
from contextlib import ExitStack
import numpy as np

BATCH, TOKENS, DIM = 8, 512, 128
P = 128
TILES = TOKENS // P
A_HEADS = 16
A_HDIM = DIM // A_HEADS
DEPTH, HEADS, HDIM, WINDOW = 6, 16, 64, 32
INNER = HEADS * HDIM
FF = int(DIM * 4 * 2 / 3)
PAIRS = HEADS // 2
KEYS = 2 * WINDOW
QKV = 3 * INNER
WCHUNK = QKV // BATCH
NSEQ = DEPTH * BATCH
MASKED = -1e30
FFC = [(0, 128), (128, 128), (256, FF - 256)]
VECS = 9


def constants():
    f = np.float32
    out = {"ident": np.eye(P, dtype=f)}
    inv = (1.0 / 10000.0 ** (np.arange(0, A_HDIM, 2, dtype=f) / A_HDIM)).astype(f)
    ang = np.outer(np.arange(TOKENS, dtype=f), inv).astype(f)
    cos, sin = np.cos(ang).astype(f), np.sin(ang).astype(f)
    row = (np.arange(DIM) % A_HDIM) // 2
    root = f(1.0 / np.sqrt(A_HDIM))
    out["a_rope"] = np.stack([cos.T[row] * root, sin.T[row] * root, cos.T[row], sin.T[row]], 1).astype(f)
    sel = np.zeros((P, 4, 4, P), f)
    for g in range(4):
        for hh in range(4):
            for e in range(4):
                for d in range(A_HDIM):
                    src, dst = A_HDIM * (4 * g + hh) + d, 32 * hh + A_HDIM * e + d
                    sel[src, g, 0 + e % 2, dst] = 1.0
                    sel[src, g, 2 + e // 2, dst] = 1.0
    out["a_sel"] = sel
    causal = np.where(np.arange(P)[None, :] > np.arange(P)[:, None], MASKED, 0.0)
    half = np.arange(0, HDIM, 2, dtype=f)
    inv = (1.0 / 10000.0 ** (half / HDIM)).astype(f)
    t = np.arange(TOKENS, dtype=f)
    fr = (t[:, None] * inv[None, :]).astype(f)
    base = ((half + f(0.4 * HDIM)) / f(1.4 * HDIM)).astype(f)
    scale = (base[None, :] ** ((t - TOKENS // 2) / (WINDOW // 2))[:, None]).astype(f)
    c, s = np.cos(fr).astype(f), np.sin(fr).astype(f)
    rope = np.zeros((2, TOKENS, 2, HDIM), f)
    for i, z in enumerate((scale * f(8.0), f(1.0) / scale)):
        rope[0, :, i, :32], rope[0, :, i, 32:] = c * z, c * z
        rope[1, :, i, :32], rope[1, :, i, 32:] = -s * z, s * z
    out["b_rope"] = rope.reshape(2, TILES, P, 2, HDIM).transpose(2, 0, 1, 3, 4).copy()
    a = (np.arange(P) % WINDOW)[:, None]
    b = np.arange(KEYS)[None, :]
    bad = (b < a) | (b > a + WINDOW)
    first = bad | ((np.arange(P)[:, None] < WINDOW) & (b < WINDOW))
    m = np.concatenate([np.where(bad, MASKED, 0.0), np.where(first, MASKED, 0.0), causal, np.eye(P)], 1)
    out["masks"] = m.astype(mybir.dt.np(mybir.dt.bfloat16))
    return out


class Tally:

    def __init__(self, steady, keep=lambda e: True):
        self.steady = [e for e in steady if keep(e)]
        self.first = [e for e in self.steady if not e.endswith("'")]
        self.last = [e for e in self.steady if e.endswith("'")]

    def at(self, n, name):
        if isinstance(n, int) and n == 0:
            return self.first.index(name) + 1
        if isinstance(n, int) and n == NSEQ:
            return len(self.first) + (NSEQ - 1) * len(self.steady) + self.last.index(name) + 1
        return (n - 1) * len(self.steady) + len(self.first) + self.steady.index(name) + 1

    def all_before(self, n):
        if isinstance(n, int):
            return 0 if n == 0 else len(self.first) + (n - 1) * len(self.steady)
        return (n - 1) * len(self.steady) + len(self.first)


class AttnTally:

    AHEAD = ["h", "q", "qr", "k", "kr"] + [f"g{i}" for i in range(6)]

    def __init__(self, steady, keep=lambda e: True):
        self.steady = [e for e in steady if keep(e)]

    def events(self, b):
        if not isinstance(b, int):
            return self.steady
        return [e for e in self.steady if (e in self.AHEAD and b < BATCH - 1) or (e[-1] == "'" and b > 0)
                or (e not in self.AHEAD and e[-1] != "'" and 0 <= b < BATCH)]

    def start(self, b):
        if isinstance(b, int):
            return sum(len(self.events(k)) for k in range(-1, b))
        return len(self.events(-1)) + len(self.events(0)) + (b - 1) * len(self.steady)

    def at(self, b, name):
        return self.start(b) + self.events(b).index(name) + 1


A_FILLS = ["g6", "g7", "v", "y'", "yt'", "h2'"] + AttnTally.AHEAD
A_BY_VECTOR = ("q", "qr", "k", "kr", "yt'")
A_FILL = AttnTally(A_FILLS)
A_ACT = AttnTally(A_FILLS, lambda e: e not in A_BY_VECTOR)
A_DVE = AttnTally(A_FILLS, lambda e: e in A_BY_VECTOR)


def fill_order():
    out = []
    for j in range(TILES):
        t, pr = ((j - 1) % TILES, "'" if j == 0 else "")
        out += [f"up{i}'" for i in range(3)] if j == 3 else []
        out += ["wo0'"] if j == 1 else []
        out += [f"T{j}{i}" for i in range(3)]
        out += ["wo1'"] if j == 1 else []
        out += [f"T{j}3"]
        out += [f"V{j}0"]
        out += ["var'"] if j == 2 else []
        out += [f"P{t}0{pr}", f"P{t}1{pr}"]
        out += {0: [f"V{j}1"], 1: ["mean'"], 2: ["spread'"], 3: [f"up{i}'" for i in range(3, 6)]}[j]
        out += [f"O{t}{i}{pr}" for i in range(2)]
        out += [f"V{j}1"] if j else []
        out += [f"Q{t}{i}{pr}" for i in range(2)]
        out += ["down'"] if j == 3 else []
    return out


FILLS = fill_order()
BY_VECTOR = ("wo0'", "wo1'", "mean'", "var'", "spread'", "up3'", "up4'", "up5'")
FILL = Tally(FILLS)
ACT_FREE = Tally(FILLS, lambda e: e not in BY_VECTOR)
DVE_FREE = Tally(FILLS, lambda e: e in BY_VECTOR)


def bank_of(name):
    return FILLS.index(name) % 2


def program(nc, t_in, out):
    f32, f32r, bf16 = mybir.dt.float32, mybir.dt.float32r, mybir.dt.bfloat16
    ALU, ACT, AX = mybir.AluOpType, mybir.ActivationFunctionType, mybir.AxisListType

    def need(eng, sem, value):
        if not isinstance(value, int) or value > 0:
            eng.wait_ge(sem, value)

    ctx = ExitStack()
    with ctx:
        def alloc(stack):
            return (lambda n, s, d=f32: stack.enter_context(nc.sbuf_tensor(n, s, d)),
                    lambda n, s, d=f32: stack.enter_context(nc.psum_tensor(n, s, d)),
                    lambda n: stack.enter_context(nc.semaphore(n)))

        sb, _, _ = alloc(ctx)
        resT = sb("resT", [P, BATCH, TOKENS])
        ident = sb("ident", [P, P])
        masks = sb("masks", [P, 2 * KEYS + 2 * P], bf16)
        win_mask = [masks[:, KEYS:2 * KEYS]] + [masks[:, 0:KEYS]] * (TILES - 1)
        causal_mask = masks[:, 2 * KEYS:2 * KEYS + P]
        ident_bf = masks[:, 2 * KEYS + P:2 * KEYS + 2 * P]
        mod = sb("mod", [P, 6, BATCH])
        vecs = sb("vecs", [P, VECS, DEPTH])

        x_attended = nc.dram_tensor("x_attended", (P, BATCH * TILES, DIM), f32, kind="Internal").ap()
        part_a(nc, t_in, alloc, need, x_attended, resT, ident, masks, causal_mask, ident_bf, mod, vecs)
        part_b(nc, t_in, alloc, need, resT, ident, win_mask, ident_bf, vecs)
        part_c(nc, out, alloc, need, x_attended, resT, ident, mod)


NEWTON = 3
RSQRT_STEPS = 1 + 3 * NEWTON


def rsqrt(nc, dve, x, y, t, sem, base):
    first_guess(nc, x, y, sem)
    for i in range(NEWTON):
        newton(nc, dve, x, y, t, sem, base, i)
    dve.wait_ge(sem, base + RSQRT_STEPS)


def first_guess(nc, x, y, sem):
    i32, ALU = mybir.dt.int32, mybir.AluOpType
    nc.vector.tensor_scalar(y.bitcast(i32), x.bitcast(i32), -0.5, float(0x5F3759DF), ALU.mult, ALU.add).then_inc(sem, 1)


def newton(nc, dve, x, y, t, sem, base, i):
    ALU = mybir.AluOpType
    dve.wait_ge(sem, base + 3 * i + 1)
    nc.vector.tensor_tensor(t, y, y, ALU.mult).then_inc(sem, 1)
    dve.wait_ge(sem, base + 3 * i + 2)
    nc.vector.scalar_tensor_tensor(t, t, -0.5, x, ALU.mult, ALU.mult).then_inc(sem, 1)
    dve.wait_ge(sem, base + 3 * i + 3)
    nc.vector.scalar_tensor_tensor(y, t, 1.5, y, ALU.add, ALU.mult).then_inc(sem, 1)


def part_a(nc, t_in, alloc, need, x_attended, resT, ident, masks, causal_mask, ident_bf, mod, vecs):
    f32, f32r, bf16 = mybir.dt.float32, mybir.dt.float32r, mybir.dt.bfloat16
    ALU, ACT, AX = mybir.AluOpType, mybir.ActivationFunctionType, mybir.AxisListType
    ctx = ExitStack()
    with ctx:
        sb, ps, sem = alloc(ctx)
        LAG = 12
        RING = LAG // 4 + 1
        xtok = sb("xtok", [P, BATCH * TILES, DIM])
        w_raw = sb("w_raw", [P, 4, P])
        wT = sb("wT", [P, 6, P])
        wmod = sb("wmod", [P, 6, P])
        c_row = sb("c_row", [BATCH, P])
        cT = sb("cT", [P, BATCH])
        sgn = sb("sgn", [P, 2, BATCH])
        rope = sb("rope", [P, 4, TOKENS])
        sel_raw = sb("sel_raw", [P, 16, P])
        sel = sb("sel", [P, 16, P], f32r)
        rows = sb("rows", [DEPTH, 3 * P + 2 * FF])
        stats = sb("stats", [P, TILES, 6])
        mv = sb("mv", [P, TILES, 2])
        rstd = sb("rstd", [P, TILES])
        var = sb("var", [P, TILES])
        var_t = sb("var_t", [P, TILES])
        xn = sb("xn", [P, TILES, P])
        hT = sb("hT", [P, TOKENS])
        ahead_mod = sb("ahead_mod", [P, 2])
        after_mod = sb("after_mod", [P, 4])
        rot1 = sb("rot1", [P, 2, TOKENS])
        rot2 = sb("rot2", [P, 2, TOKENS])
        qk_hi = sb("qk_hi", [P, 2, TOKENS], f32r)
        qk_lo = sb("qk_lo", [P, 2, TOKENS], f32r)
        qkG = sb("qkG", [P, 2, 4, TOKENS], f32r)
        wo_rows = sb("wo_rows", [P, 4, P])
        values = sb("values", [P, TILES, A_HEADS, 32])
        negmax = sb("negmax", [P, A_HEADS * TILES])
        den = sb("den", [P, 2, 4])
        rden = sb("rden", [P, 2, 4])
        prob = sb("prob", [P, RING, 4, TOKENS])
        probT = sb("probT", [P, 2, 4, TOKENS])
        oT = sb("oT", [P, 4, TOKENS])
        yT = sb("yT", [P, TOKENS])

        sc = [ps(f"sc{i}", [P, TOKENS]) for i in range(3)]
        pt = [ps(f"pt{i}", [P, TOKENS]) for i in range(2)]
        po = ps("po", [P, TOKENS])
        gen = [ps(f"gen{i}", [P, TOKENS]) for i in range(2)]

        loaded = sem("loaded")
        x_in = sem("x_in"); kept = sem("kept")
        tr_w = sem("tr_w"); tr_v = sem("tr_v"); ev_w = sem("ev_w"); silu_d = sem("silu_d")
        mod_p = sem("mod_p"); mod_e = sem("mod_e"); mod_d = sem("mod_d"); sel_d = sem("sel_d")
        rot_w = sem("rot_w"); vec_e = sem("vec_e"); vec_z = sem("vec_z")
        st = sem("st"); passed = sem("passed"); rstd_d = sem("rstd_d"); nrm = sem("nrm"); ahead_d = sem("ahead_d"); after_d = sem("after_d")
        g_fill = sem("g_fill"); g_act = sem("g_act"); g_dve = sem("g_dve")
        rope_a = sem("rope_a"); hi_d = sem("hi_d"); lo_d = sem("lo_d")
        s_full = sem("s_full"); m_d = sem("m_d"); e_d = sem("e_d"); t_full = sem("t_full")
        t_act = sem("t_act"); t_dve = sem("t_dve"); o_full = sem("o_full"); o_act = sem("o_act")
        rd_d = sem("rd_d"); scaled = sem("scaled_a"); val_z = sem("val_z"); wo_p = sem("wo_p"); wo_d = sem("wo_d")
        pe_passed = sem("pe_passed_a")
        block = ctx.enter_context(nc.Block())

        units = [(4 * g + hh, j) for g in range(4) for j in range(TILES) for hh in range(4)]
        NU, NQ = len(units), len(units) // 4
        by_act = [i % 2 == 0 for i in range(NU)]
        STEPS = NU + LAG + 4

        def pipelined(eng, engine, body):
            body(-1, False, False, True)
            body(0, True, False, True)
            with engine.Fori(1, BATCH - 1) as b:
                body(b, True, True, True)
            body(BATCH - 1, True, True, False)
            body(BATCH, False, True, False)

        def norms_before(b, ahead):
            if isinstance(b, int) and b in (-1, BATCH):
                return 0 if b < 0 else 2 * BATCH - 1
            return 2 * b + ahead

        def gbank(name):
            return gen[A_FILLS.index(name) % 2]

        def gfree(b, name):
            return (g_dve, A_DVE.at(b, name)) if name in A_BY_VECTOR else (g_act, A_ACT.at(b, name))

        def gfree_before(b, name):
            events = A_FILL.events(b)
            for e in reversed(events[:events.index(name)]):
                if gbank(e) is gbank(name):
                    return gfree(b, e)
            return g_act, A_ACT.start(b)

        xv = t_in["L0_attn_x"].rearrange("b (t p) d -> p (b t) d", p=P)

        @block.sync
        def _(sp):
            sp.dma_start(c_row[:, :], t_in["L0_c"]).then_inc(loaded, 16)
            for i, w in enumerate(("Wq", "Wk", "Wv", "Wo")):
                sp.dma_start(w_raw[:, i, :], t_in["L0_attn_" + w]).then_inc(loaded, 16)
            sp.dma_start(ident[:, :], t_in["ident"]).then_inc(loaded, 16)
            sp.dma_start(masks[:, :], t_in["masks"]).then_inc(loaded, 16)
            sp.dma_start(wmod[:, :, :], t_in["L0_wmod"].rearrange("k (m f) -> k m f", m=6)).then_inc(loaded, 16)
            sp.dma_start(rows[:, 0:P], t_in["L0_ffn_ln_g"]).then_inc(loaded, 16)
            sp.dma_start(rows[:, P:2 * P], t_in["L0_ffn_ln_b"]).then_inc(loaded, 16)
            sp.dma_start(rows[:, 2 * P:3 * P], t_in["L0_ffn_b2"]).then_inc(loaded, 16)
            sp.dma_start(rows[:, 3 * P:], t_in["L0_ffn_b1"]).then_inc(loaded, 16)
            sp.dma_start(rope[:, :, :], t_in["a_rope"]).then_inc(loaded, 16)
            sp.dma_start(sel_raw[:, :, :], t_in["a_sel"].rearrange("p g s f -> p (g s) f")).then_inc(loaded, 16)
            sp.dma_start(xtok[:, :, :], xv).then_inc(x_in, 16)
            with nc.sync.Fori(1, BATCH) as b:
                sp.wait_ge(g_dve, A_DVE.at(b, "yt'"))
                tiles = bass.ds((b - 1) * TILES, TILES)
                sp.dma_start(x_attended[:, tiles, :], xtok[:, tiles, :]).then_inc(kept, 16)
            sp.wait_ge(g_dve, A_DVE.at(BATCH, "yt'"))
            tiles = slice((BATCH - 1) * TILES, BATCH * TILES)
            sp.dma_start(x_attended[:, tiles, :], xtok[:, tiles, :]).then_inc(kept, 16)
            sp.wait_ge(kept, 16 * BATCH)
        NLOAD = 14 * 16
        pieces = [(0, P), (P, P), (2 * P, P)] + [(3 * P + o, w) for o, w in FFC] + \
                 [(3 * P + FF + o, w) for o, w in FFC]

        @block.tensor
        def _(pe):
            pe.wait_ge(loaded, NLOAD)
            for i in range(4):
                nc.tensor.transpose(sc[0][:, i * P:(i + 1) * P], w_raw[:, i, :], ident[:, :])
            nc.tensor.transpose(sc[1][:, 0:BATCH], c_row[:, :], ident[0:BATCH, 0:BATCH]).then_inc(tr_w, 1)
            for i, (o, w) in enumerate(pieces):
                last = nc.tensor.transpose(sc[2][0:w, 8 * i:8 * i + DEPTH], rows[:, o:o + w],
                                           ident[0:DEPTH, 0:DEPTH])
            last.then_inc(tr_v, 1)
            pe.wait_ge(ev_w, 1)
            for g in range(4):
                last = nc.tensor.matmul(sc[0][:, g * P:(g + 1) * P], sel_raw[:, 4 * g, :], wT[:, 3, :], start=True, stop=True)
            last.then_inc(wo_p, 1)
            pe.wait_ge(silu_d, 1)
            for m in range(6):
                last = nc.tensor.matmul(gen[0][:, m * BATCH:(m + 1) * BATCH], wmod[:, m, :], cT[:, :],
                                        start=True, stop=True)
            last.then_inc(mod_p, 1)
            pe.wait_ge(mod_d, 5)
            pe.wait_ge(rot_w, 4)
            pe.wait_ge(sel_d, 1)
            pe.wait_ge(vec_e, VECS)
            pe.wait_ge(wo_d, 1)
            pe.wait_ge(val_z, 1)

            def body(b, cur, prev, nxt):
                def fill(name, body):
                    need(pe, *gfree_before(b, name))
                    body(gbank(name)).then_inc(g_fill, 1)

                def transposes4(src):
                    def body(bank):
                        for j in range(TILES):
                            last = nc.tensor.transpose(bank[:, j * P:(j + 1) * P], src(j), ident[:, :])
                        return last
                    return body

                def project(w, src):
                    return lambda bank: nc.tensor.matmul(bank[:, :], w, src, start=True, stop=True)

                def value_rows(bank):
                    for j in range(TILES):
                        last = nc.tensor.matmul(bank[:, j * P:(j + 1) * P], hT[:, j * P:(j + 1) * P],
                                                wT[:, 2, :], start=True, stop=True)
                    return last

                def stack(name):
                    g, c = divmod(int(name[1:]), 2)

                    def product(bank):
                        nc.tensor.matmul(bank[:, :], sel[:, 4 * g + 2 * c, :], qk_hi[:, c, :],
                                         start=True, stop=False)
                        return nc.tensor.matmul(bank[:, :], sel[:, 4 * g + 2 * c + 1, :], qk_lo[:, c, :],
                                                start=False, stop=True)
                    fill(name, product)

                def scores(i):
                    h, j = units[i]
                    g, hh = divmod(h, 4)
                    if j == 0 and hh == 0:
                        pe.wait_ge(g_act, A_ACT.at(b, "g7") if g == 3 else A_ACT.start(b))
                    if i >= 3:
                        pe.wait_ge(e_d, b * NU + i - 2)
                    r = slice(32 * hh, 32 * hh + 32)
                    bank, width = sc[i % 3], (j + 1) * P
                    nc.tensor.matmul(bank[:, 0:width], qkG[r, 0, g, j * P:(j + 1) * P],
                                     qkG[r, 1, g, 0:width], start=True, stop=False)
                    nc.tensor.matmul(bank[:, j * P:width], ident_bf, causal_mask,
                                     start=False, stop=True).then_inc(s_full, 1)

                def turn(i):
                    h, j = units[i]
                    if i % 4 == 0:
                        pe.wait_ge(scaled, b * NQ + i // 4 + 1)
                    if i >= 2:
                        pe.wait_ge(t_act if by_act[i] else t_dve, b * (NU // 2) + i // 2)
                    for k in range(j + 1):
                        last = nc.tensor.transpose(pt[i % 2][:, k * P:(k + 1) * P],
                                                   prob[:, i // 4 % RING, i % 4, k * P:(k + 1) * P], ident[:, :])
                    last.then_inc(t_full, 1)

                def weigh(u):
                    g, j = divmod(u, 4)
                    pe.wait_ge(t_act, b * (NU // 2) + 2 * u + 2)
                    pe.wait_ge(t_dve, b * (NU // 2) + 2 * u + 2)
                    if u == 0:
                        pe.wait_ge(*gfree(b, "v"))
                    if j == 0 and g:
                        pe.wait_ge(o_act, b * 4 + g)
                    pe.sem_inc(pe_passed, 1)
                    for k in range(j + 1):
                        for hh in range(4):
                            last = nc.tensor.matmul(po[32 * hh:32 * hh + 32, j * P:(j + 1) * P],
                                                    values[:, k, 4 * g + hh, :],
                                                    probT[:, u % 2, hh, k * P:(k + 1) * P],
                                                    start=(k == 0), stop=(k == j))
                    last.then_inc(o_full, 1)

                def output(bank):
                    for g in range(4):
                        last = nc.tensor.matmul(bank[:, :], wo_rows[:, g, :], oT[:, g, :], start=(g == 0), stop=(g == 3))
                    return last

                for i in range(STEPS):
                    if cur and i == 2:
                        stack("g6")
                        stack("g7")
                    if cur and i == 3:
                        fill("v", value_rows)
                    if prev and i == 6:
                        pe.wait_ge(o_act, b * 4)
                        fill("y'", output)
                    if prev and i == 10:
                        pe.wait_ge(*gfree(b, "y'"))
                        fill("yt'", transposes4(lambda j: yT[:, j * P:(j + 1) * P]))
                    if prev and i == 18:
                        pe.wait_ge(nrm, norms_before(b, 0) * TILES + TILES)
                        fill("h2'", transposes4(lambda j: xn[:, j, :]))
                    if nxt and i == 26:
                        pe.wait_ge(nrm, norms_before(b, 1) * TILES + TILES)
                        fill("h", transposes4(lambda j: xn[:, j, :]))
                    if nxt and 28 <= i < 32:
                        if i == 28:
                            pe.wait_ge(*gfree(b, "h"))
                        name, w = (("q", 0), ("qr", 4), ("k", 1), ("kr", 5))[i - 28]
                        fill(name, project(wT[:, w, :], hT[:, :]))
                    if nxt and i == 36:
                        pe.wait_ge(lo_d, b * 2 + 4)
                    if nxt and 36 <= i < 40:
                        stack(f"g{i - 36}")
                    if nxt and i in (50, 51):
                        stack(f"g{i - 46}")
                    if cur and i < NU:
                        scores(i)
                    if cur and 0 <= i - LAG < NU:
                        turn(i - LAG)
                    if cur and i - LAG >= 6 and (i - LAG) % 4 == 2:
                        weigh((i - LAG) // 4 - 1)
            pipelined(pe, nc.tensor, body)

        @block.scalar
        def _(act):
            act.wait_ge(tr_w, 1)
            nc.scalar.activation(wT[:, 0:4, :], sc[0][:, :].rearrange("p (i f) -> p i f", i=4), ACT.Copy).then_inc(ev_w, 1)
            nc.scalar.activation(cT[:, :], sc[1][:, 0:BATCH], ACT.Silu).then_inc(silu_d, 1)
            act.wait_ge(loaded, NLOAD)
            nc.scalar.activation(sel[:, :, :], sel_raw[:, :, :], ACT.Copy).then_inc(sel_d, 1)
            act.wait_ge(wo_p, 1)
            nc.scalar.activation(wo_rows[:, :, :], sc[0][:, :].rearrange("p (i f) -> p i f", i=4), ACT.Copy).then_inc(wo_d, 1)
            act.wait_ge(val_z, 1)
            def body(b, cur, prev, nxt):
                def out(name, *args, **kw):
                    act.wait_ge(g_fill, A_FILL.at(b, name))
                    nc.scalar.activation(*args, **kw).then_inc(g_act, 1)

                def stack_out(name):
                    g, c = divmod(int(name[1:]), 2)
                    out(name, qkG[:, c, g, :], gbank(name)[:, :], ACT.Copy)

                def empty(i):
                    h, j = units[i]
                    act.wait_ge(t_full, b * NU + i + 1)
                    if i >= 8 and i % 4 == 0:
                        act.wait_ge(o_full, b * NQ + i // 4 - 1)
                    nc.scalar.activation(probT[:, i // 4 % 2, i % 4, 0:(j + 1) * P], pt[i % 2][:, 0:(j + 1) * P],
                                         ACT.Copy).then_inc(t_act, 1)

                def group_out(g):
                    act.wait_ge(o_full, b * NQ + 4 * g + 4)
                    nc.scalar.activation(oT[:, g, :], po[:, :], ACT.Copy).then_inc(o_act, 1)

                for i in range(STEPS):
                    if cur and i == 2:
                        stack_out("g6")
                        stack_out("g7")
                    if cur and i == 3:
                        out("v", values[:, :, :, 0:A_HDIM], gbank("v")[:, :].rearrange(
                            "p (t h d) -> p t h d", t=TILES, h=A_HEADS), ACT.Copy)
                    if prev and i == 6:
                        act.wait_ge(after_d, b)
                        out("y'", yT[:, :], gbank("y'")[:, :], ACT.Copy, scale=after_mod[:, 0:1])
                    if prev and i == 18:
                        out("h2'", resT[:, bass.ds(b - 1, 1), :], gbank("h2'")[:, :].rearrange("p (o t) -> p o t", o=1),
                            ACT.Identity, bias=after_mod[:, 1:2], scale=after_mod[:, 2:3])
                    if nxt and i == 26:
                        act.wait_ge(ahead_d, b + 2)
                        out("h", hT[:, :], gbank("h")[:, :], ACT.Identity, bias=ahead_mod[:, 0:1], scale=ahead_mod[:, 1:2])
                    if nxt and i in (30, 32):
                        c = (i - 30) // 2
                        act.wait_ge(rope_a, b * 2 + c + 3)
                        nc.scalar.activation(qk_hi[:, c, :], rot1[:, c, :], ACT.Copy).then_inc(hi_d, 1)
                    if nxt and 36 <= i < 40:
                        stack_out(f"g{i - 36}")
                    if nxt and i in (50, 51):
                        stack_out(f"g{i - 46}")
                    if cur and 0 <= i - LAG - 1 < NU and by_act[i - LAG - 1]:
                        empty(i - LAG - 1)
                    if cur and i - LAG - 1 >= 18 and (i - LAG - 1) % 16 == 2:
                        group_out((i - LAG - 1) // 16 - 1)
                    if cur and i < NU:
                        h, j = units[i]
                        u = i // 4
                        if i % 4 == 0 and u >= 2:
                            act.wait_ge(rd_d, b * NQ + u - 1)
                        if i % 4 == 0 and u >= RING:
                            act.wait_ge(t_full, b * NU + i - LAG)
                        act.wait_ge(m_d, b * NU + i + 1)
                        nc.scalar.activation(prob[:, u % RING, i % 4, 0:(j + 1) * P], sc[i % 3][:, 0:(j + 1) * P], ACT.Exp,
                                             bias=negmax[:, i:i + 1], accum_out=den[:, u % 2, i % 4:i % 4 + 1]).then_inc(e_d, 1)
            pipelined(act, nc.scalar, body)

        @block.gpsimd
        def _(pool):
            nc.gpsimd.memset(values[:, :, :, :], 0.0).then_inc(val_z, 1)
            with nc.gpsimd.Fori(0, BATCH) as b:
                for u in range(NQ):
                    w = (u % 4 + 1) * P
                    pool.wait_ge(rd_d, b * NQ + u + 1)
                    pr = prob[:, u % RING, :, 0:w]
                    nc.gpsimd.tensor_tensor(pr, pr, rden[:, u % 2, :].rearrange("p (h o) -> p h o", o=1)
                                            .broadcast_to([P, 4, w]), ALU.mult).then_inc(scaled, 1)

        @block.vector
        def _(dve):
            nc.vector.memset(vecs[:, :, :], 0.0).then_inc(vec_z, 1)
            dve.wait_ge(ev_w, 1)
            for i in range(2):
                src = wT[:, i, :].rearrange("p (a two) -> p a two", two=2)
                dst = wT[:, 4 + i, :].rearrange("p (a two) -> p a two", two=2)
                nc.vector.tensor_scalar(dst[:, :, 0:1], src[:, :, 1:2], -1.0, None, ALU.mult).then_inc(rot_w, 1)
                nc.vector.tensor_copy(dst[:, :, 1:2], src[:, :, 0:1]).then_inc(rot_w, 1)
            dve.wait_ge(tr_v, 1)
            dve.wait_ge(vec_z, 1)
            for i, (o, w) in enumerate(pieces):
                nc.vector.tensor_copy(vecs[0:w, i, :], sc[2][0:w, 8 * i:8 * i + DEPTH]).then_inc(vec_e, 1)
            dve.wait_ge(mod_p, 1)
            nc.vector.tensor_copy(mod[:, :, :], gen[0][:, 0:6 * BATCH].rearrange("p (m b) -> p m b", m=6)).then_inc(mod_e, 1)
            dve.wait_ge(mod_e, 1)
            both = mod[:, 1:5:3, :]
            gates = mod[:, 2:6:3, :]
            nc.vector.tensor_scalar(both, both, 1.0, None, ALU.add).then_inc(mod_d, 1)
            nc.vector.tensor_scalar(sgn[:, :, :], gates, 0.0, 2.0, ALU.is_ge, ALU.mult).then_inc(mod_d, 1)
            dve.wait_ge(mod_d, 2)
            nc.vector.tensor_scalar(sgn[:, :, :], sgn[:, :, :], -1.0, None, ALU.add).then_inc(mod_d, 1)
            dve.wait_ge(mod_d, 3)
            nc.vector.tensor_tensor(gates, gates, sgn[:, :, :], ALU.mult).then_inc(mod_d, 1)
            dve.wait_ge(mod_d, 4)
            nc.vector.scalar_tensor_tensor(gates, gates, 0.25, sgn[:, :, :], ALU.max, ALU.mult).then_inc(mod_d, 1)
            dve.wait_ge(mod_d, 5)
            dve.wait_ge(x_in, 16)
            def body(b, cur, prev, nxt):
                def norm(seq, ahead, part):
                    base = norms_before(b, ahead) * 9
                    root = norms_before(b, ahead) * RSQRT_STEPS
                    if part == 0:
                        for j in range(TILES):
                            nc.vector.bn_stats(stats[:, j:j + 1, :], xtok[:, bass.ds(seq * TILES + j, 1), :]).then_inc(st, 1)
                    if part == 1:
                        dve.wait_ge(st, base + 4)
                        dve.sem_inc(passed, 1)
                        for j in range(TILES):
                            nc.vector.bn_aggr(mv[:, j, :], stats[:, j, :]).then_inc(st, 1)
                        dve.wait_ge(st, base + 8)
                        nc.vector.tensor_scalar(var[:, :].rearrange("p (t o) -> p t o", o=1), mv[:, :, 1:2], 1e-5, None,
                                                ALU.add).then_inc(st, 1)
                        dve.wait_ge(st, base + 9)
                        first_guess(nc, var[:, :], rstd[:, :], rstd_d)
                    if 2 <= part < 2 + NEWTON:
                        newton(nc, dve, var[:, :], rstd[:, :], var_t[:, :], rstd_d, root, part - 2)
                    if part == 2 + NEWTON:
                        dve.wait_ge(rstd_d, root + RSQRT_STEPS)
                        for j in range(TILES):
                            nc.vector.tensor_scalar(xn[:, j:j + 1, :], xtok[:, bass.ds(seq * TILES + j, 1), :], mv[:, j, 0:1],
                                                    rstd[:, j:j + 1], ALU.subtract, ALU.mult).then_inc(nrm, 1)

                def empty(i):
                    h, j = units[i]
                    dve.wait_ge(t_full, b * NU + i + 1)
                    if i >= 8 and i % 4 == 1:
                        dve.wait_ge(o_full, b * NQ + i // 4 - 1)
                    nc.vector.tensor_copy(probT[:, i // 4 % 2, i % 4, 0:(j + 1) * P], pt[i % 2][:, 0:(j + 1) * P]).then_inc(t_dve, 1)

                for i in range(NU + LAG + 1):
                    if prev and i == 5:
                        nc.vector.tensor_copy(after_mod[:, :].rearrange("p (m o) -> p m o", o=1),
                                              mod[:, 2:6, bass.ds(b - 1, 1)]).then_inc(after_d, 1)
                    if prev and i == 10:
                        dve.wait_ge(g_fill, A_FILL.at(b, "yt'"))
                        xb = xtok[:, bass.ds((b - 1) * TILES, TILES), :]
                        nc.vector.tensor_tensor(xb, gbank("yt'")[:, :].rearrange("p (t f) -> p t f", t=TILES), xb,
                                                ALU.add).then_inc(g_dve, 1)
                        dve.wait_ge(*gfree(b, "yt'"))
                        dve.sem_inc(passed, 1)
                    if prev and 10 <= i < 13 + NEWTON:
                        norm(b - 1, 0, i - 10)
                    if nxt and i == 19:
                        if prev:
                            dve.wait_ge(g_fill, A_FILL.at(b, "h2'"))
                        nc.vector.tensor_copy(ahead_mod[:, :].rearrange("p (m o) -> p m o", o=1),
                                              mod[:, 0:2, bass.ds(b + 1, 1)]).then_inc(ahead_d, 1)
                    if nxt and 19 <= i < 22 + NEWTON:
                        norm(b + 1, 1, i - 19)
                    if nxt and 28 <= i < 32:
                        name, (c, r) = ("q", "qr", "k", "kr")[i - 28], divmod(i - 28, 2)
                        dve.wait_ge(g_fill, A_FILL.at(b, name))
                        nc.vector.tensor_tensor((rot1, rot2)[r][:, c, :], gbank(name)[:, :], rope[:, i - 28, :],
                                                ALU.mult).then_inc(g_dve, 1)
                        if r:
                            dve.wait_ge(*gfree(b, name))
                            nc.vector.tensor_tensor(rot1[:, c, :], rot1[:, c, :], rot2[:, c, :], ALU.add).then_inc(rope_a, 1)
                    if nxt and i in (31, 33):
                        c = (i - 31) // 2
                        dve.wait_ge(hi_d, b * 2 + c + 3)
                        nc.vector.tensor_tensor(qk_lo[:, c, :], rot1[:, c, :], qk_hi[:, c, :].bitcast(f32),
                                                ALU.subtract).then_inc(lo_d, 1)
                    if cur and 0 <= i - LAG - 1 and not by_act[i - LAG - 1]:
                        empty(i - LAG - 1)
                    if cur and i < NU:
                        h, j = units[i]
                        dve.wait_ge(s_full, b * NU + i + 1)
                        nc.vector.tensor_reduce(negmax[:, i:i + 1], sc[i % 3][:, 0:(j + 1) * P], AX.X, ALU.max,
                                                negate=True).then_inc(m_d, 1)
                    if cur and i >= 4 and i % 4 == 0 and i <= NU:
                        u = i // 4 - 1
                        dve.wait_ge(e_d, b * NU + i)
                        if u >= 2:
                            dve.wait_ge(scaled, b * NQ + u - 1)
                        nc.vector.reciprocal(rden[:, u % 2, :], den[:, u % 2, :]).then_inc(rd_d, 1)
            pipelined(dve, nc.vector, body)


def part_b(nc, t_in, alloc, need, resT, ident, win_mask, ident_bf, vecs):
    f32, f32r, bf16 = mybir.dt.float32, mybir.dt.float32r, mybir.dt.bfloat16
    ALU, ACT, AX = mybir.AluOpType, mybir.ActivationFunctionType, mybir.AxisListType
    ctx = ExitStack()
    with ctx:
        sb, ps, sem = alloc(ctx)
        w_raw = sb("wqkv_raw", [P, WCHUNK])
        w_hi = sb("wqkv_hi", [P, 2, QKV], f32r)
        w_lo = sb("wqkv_lo", [P, 2, QKV], f32r)
        wo = sb("wo", [P, 2, PAIRS, DIM])
        w1 = sb("w1", [P, 2 * FF])
        w2 = sb("w2", [P, 3, DIM])
        vec = sb("vec", [P, VECS])
        rope0 = sb("rope0", [P, 2, TILES, 2, HDIM])
        rope = sb("rope_b", [P, 2, TILES, 2, HDIM])
        qks = sb("qks", [P, 2, HDIM])
        mean_w = sb("mean_w", [P, P])
        xa_hi = sb("xa_hi", [P, WINDOW + TOKENS], f32r)
        xa_lo = sb("xa_lo", [P, WINDOW + TOKENS], f32r)
        squares = sb("squares", [P, INNER])
        sums = sb("sums", [P, 2 * HEADS + TILES])
        rnorm = sb("rnorm", [P, 2 * HEADS + TILES])
        rtmp = sb("rtmp", [P, 2 * HEADS + TILES])
        qkn = sb("qkn", [P, 2, INNER])
        rc = sb("rc", [P, 2, INNER])
        rs = sb("rs", [P, 2, INNER])
        qT = sb("qT", [P, PAIRS, P])
        kT = sb("kT", [P, PAIRS, WINDOW + TOKENS])
        prob = [sb(f"prob_b{i}", [P, PAIRS, 2, KEYS]) for i in range(2)]
        rmax = sb("rmax", [P, 2, PAIRS])
        rsum = sb("rsum", [P, PAIRS, 2])
        rinv = sb("rinv", [P, PAIRS, 2])
        pT = sb("pT", [P, PAIRS, P])
        vown = sb("vown", [P, 2, 2, PAIRS, HDIM])
        vmoved = sb("vmoved", [P, 3, PAIRS, HDIM])
        otok = sb("otok_b", [P, PAIRS, 2, HDIM])
        oT = sb("oT_b", [P, PAIRS, TOKENS])
        first_raw = oT[:, :, :].rearrange("p q t -> p (q t)")
        x1 = sb("x1", [P, TOKENS])
        xs = sb("xs", [P, TOKENS])
        xc = sb("xc", [P, TOKENS])
        hid = sb("hid", [P, 3, TOKENS])
        xq = hid[:, 0, :]
        dev = hid[:, 1, :].rearrange("p (t f) -> p t f", t=TILES)

        proj = [ps(f"proj{c}", [P, INNER]) for c in range(2)]
        ring = [ps(f"ring{i}", [P, 512]) for i in range(2)]
        scr = ps("scr", [P, 2, PAIRS, KEYS])

        qks_in = sem("qks_in"); consts_in = sem("consts_in"); raw_in = sem("raw_in"); wo_in = sem("wo_in")
        w1_in = sem("w1_in"); w2_in = sem("w2_in")
        zeroed = sem("zeroed")
        w_hi_done = sem("w_hi_done"); w_lo_done = sem("w_lo_done")
        x_hi_done = sem("x_hi_done"); x_lo_done = sem("x_lo_done")
        moved = sem("moved"); add_done = sem("add_done")
        pe_passed = sem("pe_passed"); sp_passed = sem("sp_passed")
        rope_done = sem("rope_done")
        proj_full = sem("proj_full"); sq_done = sem("sq_done"); ss_done = sem("ss_done")
        clamp_done = sem("clamp_done"); spread_done = sem("spread_done")
        rn_done = sem("rn_done"); qkn_done = sem("qkn_done"); rc_done = sem("rc_done"); rs_done = sem("rs_done")
        fill = sem("fill"); act_free = sem("act_free"); dve_free = sem("dve_free")
        scr_full = sem("scr_full"); max_done = sem("max_done"); sub_done = sem("sub_done")
        exp_done = sem("exp_done"); sum_done = sem("sum_done"); inv_done = sem("inv_done")
        prob_done = sem("prob_done")
        xs_done = sem("xs_done"); xq_done = sem("xq_done")
        h_done = sem("h_done")
        vec_done = sem("vec_done"); res_done = sem("res_done")
        block = ctx.enter_context(nc.Block())

        wqkv = t_in["L0_ffn_Wqkv"]
        half_tokens = TOKENS // 2
        stage = [[(slice(0, 64), WINDOW, 0, half_tokens), (slice(64, P), WINDOW + 1, 0, half_tokens - 1)],
                 [(slice(0, 64), WINDOW + half_tokens, half_tokens, half_tokens),
                  (slice(64, P), WINDOW + half_tokens, half_tokens - 1, half_tokens)]]

        def pipelined(eng, engine, body):
            body(0, True, False)
            with engine.Fori(1, NSEQ) as n:
                body(n, True, True)
            body(NSEQ, False, True)

        def free_before(n, name):
            kind = FILL.first if isinstance(n, int) and n == 0 else \
                FILL.last if isinstance(n, int) and n == NSEQ else FILL.steady
            i = kind.index(name)
            for k in range(i - 1, -1, -1):
                if bank_of(kind[k]) == bank_of(name):
                    e = kind[k]
                    return (dve_free, DVE_FREE.at(n, e)) if e in BY_VECTOR else (act_free, ACT_FREE.at(n, e))
            if kind is FILL.first:
                return act_free, 0
            return act_free, ACT_FREE.all_before(n)

        @block.sync
        def _(sp):
            sp.dma_start(rope0[:, :, :, :, :], t_in["b_rope"]).then_inc(consts_in, 16)

            def load_qks(layer):
                for c, name in enumerate(("L0_ffn_q_scale", "L0_ffn_k_scale")):
                    sp.dma_start(qks[:, c, :], t_in[name][layer, :].broadcast_to([P, HDIM])).then_inc(qks_in, 16)

            load_qks(bass.ds(0, 1))
            def load_wo(layer):
                src = t_in["L0_ffn_Wo"][layer, :, :]
                sp.dma_start(wo[:, 0, :, :], src.rearrange("l (c p) f -> p (l c) f", p=P)).then_inc(wo_in, 16)
                for s in range(2):
                    sp.dma_start(wo[64 * s:64 * s + 64, 1, :, :],
                                 src.rearrange("l (c s p) f -> s p (l c) f", s=2, p=64)[1 - s, :, :, :]).then_inc(wo_in, 16)

            def load_ffn(layer):
                sp.dma_start(w1[:, :], t_in["L0_ffn_W1"][layer, :, :].rearrange("l p f -> p (l f)")).then_inc(w1_in, 16)
                w2v = t_in["L0_ffn_W2"]
                sp.dma_start(w2[:, 0:2, :], w2v[layer, 0:2 * P, :].rearrange("l (c p) f -> p (l c) f", p=P)).then_inc(w2_in, 16)
                sp.dma_start(w2[0:FF - 2 * P, 2, :], w2v[layer, 2 * P:FF, :].rearrange("l p f -> p (l f)")).then_inc(w2_in, 16)

            for s in range(BATCH):
                chunk = slice(s * WCHUNK, (s + 1) * WCHUNK)
                sp.dma_start(first_raw[:, chunk], wqkv[0, :, chunk]).then_inc(raw_in, 16)
            load_wo(bass.ds(0, 1))
            load_ffn(bass.ds(0, 1))

            def body(n, cur, prev):
                for j in range(TILES):
                    if cur and j == 0:
                        sp.wait_ge(w_lo_done, BATCH + n)
                        src = wqkv[bass.ds((n // BATCH + 1) % DEPTH, 1), :, bass.ds((n % BATCH) * WCHUNK, WCHUNK)]
                        sp.dma_start(w_raw[:, :], src.rearrange("l p f -> p (l f)")).then_inc(raw_in, 16)
                        sp.wait_ge(rope_done, n * 3 + 3)
                        load_qks(bass.ds(((n + 1) // BATCH) % DEPTH, 1))
                    if cur and prev:
                        layer = bass.ds(n // BATCH, 1)
                        if j == 1:
                            sp.wait_ge(fill, FILL.at(n, "wo1'"))
                            load_wo(layer)
                        if j == 3:
                            sp.wait_ge(fill, FILL.at(n, "down'"))
                            load_ffn(layer)
                    if cur:
                        sp.wait_ge(act_free, ACT_FREE.at(n, f"V{j}1"))
                        sp.sem_inc(sp_passed, 1)
                        if j or prev:
                            sp.wait_ge(fill, FILL.at(n, f"O{(j - 1) % TILES}1" + ("" if j else "'")))
                        own, before = vown[:, j % 2, :, :, :], vown[:, 1 - j % 2, :, :, :]
                        for dst, k, rows, src, b in ((64, 0, 64, own[0:64], 1), (0, 0, 64, own[64:P], 1),
                                                     (32, 1, 96, own[0:96], 0), (0, 1, 32, before[96:P], 0),
                                                     (0, 2, 64, own[32:96], 1), (96, 2, 32, own[0:32], 1),
                                                     (64, 2, 32, before[96:P], 1)):
                            sp.dma_start(vmoved[dst:dst + rows, k, :, :], src[:, b, :, :]).then_inc(moved, 16)
            pipelined(sp, nc.sync, body)

        @block.tensor
        def _(pe):
            pe.wait_ge(zeroed, 6)

            def body(n, cur, prev):
                m = n - 1
                parity = (n // BATCH) % 2

                def begin(name):
                    need(pe, *free_before(n, name))
                    return ring[bank_of(name)]

                def split_product(bank, x_cols, w_cols):
                    nc.tensor.matmul(bank, xa_hi[:, x_cols], w_cols(w_hi), start=True, stop=False)
                    nc.tensor.matmul(bank, xa_hi[:, x_cols], w_cols(w_lo), start=False, stop=False)
                    return nc.tensor.matmul(bank, xa_lo[:, x_cols], w_cols(w_hi), start=False, stop=True)

                def project(j, q, c):
                    if j == 0 and c == 0:
                        pe.wait_ge(x_lo_done, 2 + q * 4)
                        pe.wait_ge(w_lo_done, BATCH + q)
                    if j == 2 and c == 0:
                        pe.wait_ge(x_lo_done, 4 + q * 4)
                    xcols = slice(WINDOW + j * P, WINDOW + (j + 1) * P)
                    par = (q // BATCH) % 2
                    need(pe, qkn_done, q * 8 + 2 * j + c - 1)
                    for k in range(2):
                        off = c * INNER + k * 512

                        def cols(w, off=off):
                            return w[:, bass.ds(par, 1), off:off + 512]
                        last = split_product(proj[c][:, k * 512:(k + 1) * 512], xcols, cols)
                    last.then_inc(proj_full, 1)

                def values(t, b):
                    start = WINDOW + t * P
                    bank = begin(f"V{t}{b}")

                    def cols(w):
                        return w[:, bass.ds(parity, 1), 2 * INNER:3 * INNER].rearrange(
                            "p o (q h d) -> p (o q) h d", h=2, d=HDIM)[:, :, b, :]
                    split_product(bank[:, :], slice(start, start + P), cols).then_inc(fill, 1)

                def transpose_probs(t, mark):
                    pe.wait_ge(prob_done, (m if mark else n) * 4 + t + 1)
                    for i in range(2):
                        bank = begin(f"P{t}{i}{mark}")
                        for p in range(4):
                            last = nc.tensor.transpose(bank[:, p * P:(p + 1) * P], prob[t % 2][:, 4 * i + p, :, :].rearrange("p s k -> p (s k)"), ident[:, :])
                        last.then_inc(fill, 1)

                def weigh(t, mark):
                    pe.wait_ge(act_free, ACT_FREE.at(n, f"P{t}1{mark}"))
                    pe.wait_ge(moved, ((m if mark else n) * 4 + t + 1) * 7 * 16)
                    for s in range(2):
                        bank = begin(f"O{t}{s}{mark}")[:, :].rearrange("p (q k) -> p q k", q=PAIRS)
                        pe.sem_inc(pe_passed, 1)
                        for p in range(PAIRS):
                            for w in range(4):
                                b = s ^ (w // 2)
                                k = (w % 2 == 0) * 2 + b - 1
                                v = vown[:, t % 2, 0, p, :] if k < 0 else vmoved[:, k, p, :]
                                last = nc.tensor.matmul(
                                    bank[32 * w:32 * w + 32, p, :], pT[64 * s:64 * s + 64, p, 32 * w:32 * w + 32],
                                    v[64 * s:64 * s + 64, :], start=True, stop=True)
                        last.then_inc(fill, 1)

                def turn(t, mark):
                    pe.wait_ge(act_free, ACT_FREE.at(n, f"O{t}1{mark}"))
                    for i in range(2):
                        bank = begin(f"Q{t}{i}{mark}")
                        for p in range(4):
                            last = nc.tensor.transpose(bank[:, p * P:(p + 1) * P],
                                                       otok[:, 4 * i + p, :, :].rearrange("p s d -> p (s d)"), ident[:, :])
                        last.then_inc(fill, 1)

                def feed_down():
                    pe.wait_ge(w2_in, n * 32)
                    pe.wait_ge(dve_free, DVE_FREE.at(n, "up5'"))
                    bank = begin("down'")
                    for i, (o, w) in enumerate(FFC):
                        last = nc.tensor.matmul(bank[:, :], w2[0:w, i, :], hid[0:w, i, :], start=(i == 0), stop=(i == 2))
                    last.then_inc(fill, 1)

                def transpose_qk(j, i):
                    k, c = divmod(i, 2)
                    if k == 0:
                        pe.wait_ge(add_done, n * 8 + 2 * j + c + 1)
                    bank = begin(f"T{j}{i}")
                    for p in range(4):
                        o = (4 * k + p) * P
                        last = nc.tensor.transpose(bank[:, p * P:(p + 1) * P], rc[:, c, o:o + P], ident[:, :])
                    last.then_inc(fill, 1)

                def score(j, k):
                    pe.wait_ge(act_free, ACT_FREE.at(n, f"T{j}{2 * k + 1}"))
                    if k == 0:
                        need(pe, sub_done, n * 4 + j)
                        for s in range(2):
                            mask = win_mask[j].rearrange("p (o k) -> p o k", o=1).broadcast_to([P, PAIRS, KEYS])
                            nc.tensor.matmul(scr[:, s, :, :], ident_bf, mask, start=True, stop=True)
                    else:
                        pe.sem_inc(pe_passed, 1)
                    for p in range(4 * k, 4 * k + 4):
                        for b in range(2):
                            for w in range(4):
                                s = b ^ (w // 2)
                                rows = slice(64 * b, 64 * b + 64)
                                last = nc.tensor.matmul(
                                    scr[32 * w:32 * w + 32, s, p, :], qT[rows, p, 32 * w:32 * w + 32],
                                    kT[rows, p, j * P + 32 * w:j * P + 32 * w + KEYS],
                                    start=False, stop=True, skip_group_check=True)
                    if k:
                        last.then_inc(scr_full, 1)

                if isinstance(n, int) and n == 0:
                    for c in range(2):
                        project(0, 0, c)

                def output(i):
                    pe.wait_ge(wo_in, n * 48)
                    pe.wait_ge(act_free, ACT_FREE.at(n, "Q31'"))
                    bank = begin(f"wo{i}'")
                    for p in range(PAIRS):
                        ot = oT[:, p, :].rearrange("p (t i k) -> p t i k", t=TILES, i=2)[:, :, i, :]
                        last = nc.tensor.matmul(bank[:, 0:TOKENS // 2], wo[:, i, p, :], ot, start=(p == 0),
                                                stop=(p == PAIRS - 1))
                    last.then_inc(fill, 1)

                def feed_up(pieces):
                    pe.wait_ge(w1_in, n * 16)
                    pe.wait_ge(h_done, m + 1)
                    for i in pieces:
                        o, w = FFC[i % 3]
                        o += FF if i < 3 else 0
                        bank = begin(f"up{i}'")
                        nc.tensor.matmul(bank[0:w, :], w1[:, o:o + w], xc[:, :], start=True, stop=True).then_inc(fill, 1)

                for j in range(TILES):
                    t, mark = (j - 1) % TILES, "'" if j == 0 else ""
                    on = prev if j == 0 else cur
                    ahead = (j + 1, n) if j < TILES - 1 else (0, n + 1)
                    if prev and j == 3:
                        feed_up((0, 1))
                    if cur:
                        project(*ahead, 0)
                    if prev and j == 3:
                        feed_up((2,))
                    if prev and j == 1:
                        output(0)
                    if cur:
                        transpose_qk(j, 0)
                        if j == 1:
                            project(*ahead, 1)
                            transpose_qk(j, 1)
                        else:
                            transpose_qk(j, 1)
                            project(*ahead, 1)
                        transpose_qk(j, 2)
                    if prev and j == 1:
                        output(1)
                    if cur:
                        transpose_qk(j, 3)
                    if cur:
                        score(j, 0)
                    if cur:
                        values(j, 0)
                    if prev and j == 2:
                        pe.wait_ge(xq_done, m + 1)
                        bank = begin("var'")
                        for i in range(TILES):
                            last = nc.tensor.matmul(bank[:, i:i + 1], xq[:, i * P:(i + 1) * P], mean_w[:, 0:1],
                                                    start=True, stop=True)
                        last.then_inc(fill, 1)
                    if cur:
                        score(j, 1)
                    if on:
                        transpose_probs(t, mark)
                    if cur and j == 0:
                        values(j, 1)
                    if prev and j == 3:
                        feed_up((3, 4, 5))
                    if prev and j == 1:
                        pe.wait_ge(xs_done, n * 2)
                        bank = begin("mean'")
                        nc.tensor.matmul(bank[:, :], mean_w[:, :], xs[:, :], start=True, stop=True).then_inc(fill, 1)
                    if prev and j == 2:
                        pe.wait_ge(spread_done, m + 1)
                        bank = begin("spread'")
                        for i in range(TILES):
                            last = nc.tensor.transpose(bank[:, i * P:(i + 1) * P], dev[:, i, :], ident[:, :])
                        last.then_inc(fill, 1)
                    if on:
                        weigh(t, mark)
                    if cur and j:
                        values(j, 1)
                    if on:
                        turn(t, mark)
                    if prev and j == 3:
                        feed_down()
            pipelined(pe, nc.tensor, body)

        @block.scalar
        def _(act):
            act.wait_ge(zeroed, 6)

            def stage_hi(seq, half):
                for rows, col, tok, width in stage[half]:
                    nc.scalar.activation(xa_hi[rows, col:col + width], resT[rows, seq, tok:tok + width],
                                         ACT.Copy).then_inc(x_hi_done, 1)

            def split_hi(parity, off, count, src=None):
                act.wait_ge(raw_in, count)
                nc.scalar.activation(w_hi[:, parity, off], w_raw[:, :].rearrange("p (o f) -> p o f", o=1) if src is None else src,
                                     ACT.Copy).then_inc(w_hi_done, 1)

            for s in range(BATCH):
                chunk = slice(s * WCHUNK, (s + 1) * WCHUNK)
                split_hi(slice(0, 1), chunk, BATCH * 16, first_raw[:, chunk].rearrange("p (o f) -> p o f", o=1))
            stage_hi(slice(0, 1), 0)

            def body(n, cur, prev):
                m = n - 1

                def empty(name, dst, src=None):
                    act.wait_ge(fill, FILL.at(n, name))
                    nc.scalar.activation(dst, ring[bank_of(name)][:, :] if src is None else src, ACT.Copy).then_inc(act_free, 1)

                def squares_of(j, q, c):
                    act.wait_ge(proj_full, q * 8 + 2 * j + c + 1)
                    need(act, ss_done, q * 8 + 2 * j + c)
                    nc.scalar.activation(squares[:, :], proj[c][:, :], ACT.Square).then_inc(sq_done, 1)

                if isinstance(n, int) and n == 0:
                    for c in range(2):
                        squares_of(0, 0, c)
                for j in range(TILES):
                    t, mark = (j - 1) % TILES, "'" if j == 0 else ""
                    on = prev if j == 0 else cur
                    ahead = (j + 1, n) if j < TILES - 1 else (0, n + 1)

                    def qk_out(k):
                        for c, dst in enumerate((qT[:, 4 * k:4 * k + 4, :],
                                                 kT[:, 4 * k:4 * k + 4, WINDOW + j * P:WINDOW + (j + 1) * P])):
                            name = f"T{j}{2 * k + c}"
                            empty(name, dst, ring[bank_of(name)][:, :].rearrange("p (q k) -> p q k", q=4))

                    def values_out(b):
                        name = f"V{j}{b}"
                        if b == 0:
                            need(act, moved, (n * 4 + j) * 7 * 16)
                        empty(name, vown[:, j % 2, b, :, :],
                              ring[bank_of(name)][:, :].rearrange("p (q d) -> p q d", q=PAIRS))

                    if prev and j == 3:
                        for i in range(3):
                            w = FFC[i][1]
                            act.wait_ge(fill, FILL.at(n, f"up{i}'"))
                            nc.scalar.activation(hid[0:w, i, :], ring[bank_of(f"up{i}'")][0:w, :], ACT.Gelu,
                                                 bias=vec[0:w, 6 + i:7 + i]).then_inc(act_free, 1)
                    if cur:
                        squares_of(*ahead, 0)
                        qk_out(0)
                        squares_of(*ahead, 1)
                    if cur:
                        qk_out(1)
                    if prev and j == 1:
                        act.wait_ge(dve_free, DVE_FREE.at(n, "wo1'"))
                        nc.scalar.activation(xs[0:64, :], x1[0:64, :], ACT.Copy).then_inc(xs_done, 1)
                        nc.scalar.activation(xs[64:P, 1:TOKENS], x1[64:P, 0:TOKENS - 1], ACT.Copy).then_inc(xs_done, 1)
                    if cur:
                        values_out(0)
                    if cur and j == 0:
                        stage_hi(bass.ds(n % BATCH, 1), 1)
                    if cur and j == 2:
                        stage_hi(bass.ds((n + 1) % BATCH, 1), 0)
                    if cur and j == 1:
                        split_hi(bass.ds((n // BATCH + 1) % 2, 1), bass.ds((n % BATCH) * WCHUNK, WCHUNK),
                                 (n + 1 + BATCH) * 16)
                    if on:
                        for i in range(2):
                            name = f"P{t}{i}{mark}"
                            empty(name, pT[:, 4 * i:4 * i + 4, :], ring[bank_of(name)][:, :].rearrange("p (q k) -> p q k", q=4))
                    if cur and j == 0:
                        values_out(1)
                    if cur:
                        act.wait_ge(sub_done, n * 4 + j + 1)
                        pr = prob[j % 2][:, :, :, :]
                        nc.scalar.activation(pr, pr, ACT.Exp).then_inc(exp_done, 1)
                    if prev and j == 2:
                        act.wait_ge(vec_done, n)
                        act.wait_ge(dve_free, DVE_FREE.at(n, "spread'"))
                        nc.scalar.activation(xc[:, :], xc[:, :], ACT.Identity, bias=vec[:, 1:2],
                                             scale=vec[:, 0:1]).then_inc(h_done, 1)
                    if on:
                        for s in range(2):
                            name = f"O{t}{s}{mark}"
                            empty(name, otok[:, :, s, :],
                                  ring[bank_of(name)][:, :].rearrange("p (q k) -> p q k", q=PAIRS))
                    if prev and j == 1:
                        act.wait_ge(dve_free, DVE_FREE.at(n, "mean'"))
                        nc.scalar.activation(xq, xc[:, :], ACT.Square).then_inc(xq_done, 1)
                    if cur and j:
                        values_out(1)
                    if on:
                        for i in range(2):
                            name = f"Q{t}{i}{mark}"
                            empty(name, oT[:, 4 * i:4 * i + 4, t * P:(t + 1) * P],
                                  ring[bank_of(name)][:, :].rearrange("p (q k) -> p q k", q=4))
                    if prev and j == 3:
                        act.wait_ge(fill, FILL.at(n, "down'"))
                        nc.scalar.activation(xc[:, :], ring[bank_of("down'")][:, :], ACT.Identity,
                                             bias=vec[:, 2:3]).then_inc(act_free, 1)
            pipelined(act, nc.scalar, body)

        @block.gpsimd
        def _(pool):
            nc.gpsimd.memset(xa_hi[:, 0:WINDOW + 1].bitcast(f32), 0.0).then_inc(zeroed, 1)
            nc.gpsimd.memset(xa_lo[:, 0:WINDOW + 1].bitcast(f32), 0.0).then_inc(zeroed, 1)
            nc.gpsimd.memset(kT[:, :, 0:WINDOW], 0.0).then_inc(zeroed, 1)
            nc.gpsimd.memset(xs[:, 0:1], 0.0).then_inc(zeroed, 1)
            nc.gpsimd.memset(mean_w[:, :], 1.0 / DIM).then_inc(zeroed, 1)
            nc.gpsimd.memset(vown[:, 1, :, :, :], 0.0).then_inc(zeroed, 1)
            pool.wait_ge(consts_in, 16)

            def split_lo(parity, off, count, src=None):
                pool.wait_ge(w_hi_done, count)
                nc.gpsimd.tensor_tensor(w_lo[:, parity, off], w_raw[:, :].rearrange("p (o f) -> p o f", o=1) if src is None else src,
                                        w_hi[:, parity, off].bitcast(f32), ALU.subtract).then_inc(w_lo_done, 1)

            def load_vec(layer):
                nc.gpsimd.tensor_copy(vec[:, :].rearrange("p (v o) -> p v o", o=1), vecs[:, :, layer]).then_inc(vec_done, 1)

            for s in range(BATCH):
                chunk = slice(s * WCHUNK, (s + 1) * WCHUNK)
                split_lo(slice(0, 1), chunk, s + 1, first_raw[:, chunk].rearrange("p (o f) -> p o f", o=1))
            load_vec(slice(0, 1))

            def body(n, cur, prev):
                def make_rope(q):
                    need(pool, rs_done, q * 8)
                    need(pool, rc_done, q * 8)
                    pool.wait_ge(qks_in, q * 32 + 32)
                    nc.gpsimd.tensor_tensor(rope[:, 0, :, :, :], rope0[:, 0, :, :, :],
                                            qks[:, :, :].rearrange("p (o c) d -> p o c d", o=1).broadcast_to([P, TILES, 2, HDIM]), ALU.mult).then_inc(rope_done, 1)
                    for s in range(2):
                        h, o = slice(32 * s, 32 * s + 32), slice(32 - 32 * s, 64 - 32 * s)
                        nc.gpsimd.tensor_tensor(rope[:, 1, :, :, h], rope0[:, 1, :, :, h],
                                                qks[:, :, o].rearrange("p (o c) d -> p o c d", o=1).broadcast_to([P, TILES, 2, HDIM // 2]), ALU.mult).then_inc(rope_done, 1)
                    pool.wait_ge(rope_done, q * 3 + 3)

                def turned_half(j, q):
                    for c in range(2):
                        u = 2 * j + c
                        pool.wait_ge(qkn_done, q * 8 + u + 1)
                        need(pool, add_done, q * 8 + u - 1)
                        src = qkn[:, c, :].rearrange("p (h s d) -> p h s d", h=HEADS, s=2)
                        dst = rs[:, c, :].rearrange("p (h s d) -> p h s d", h=HEADS, s=2)
                        tab = rope[:, 1, j, c, :].rearrange("p (o s d) -> p o s d", o=1, s=2)
                        for s in range(2):
                            ins = nc.gpsimd.tensor_tensor(dst[:, :, s, :], src[:, :, 1 - s, :],
                                                          tab[:, :, s, :].broadcast_to([P, HEADS, HDIM // 2]),
                                                          ALU.mult)
                        ins.then_inc(rs_done, 1)

                if isinstance(n, int) and n == 0:
                    make_rope(0)
                    turned_half(0, 0)
                if cur:
                    for j in range(TILES):
                        if j == 3:
                            make_rope(n + 1)
                        turned_half(*((j + 1, n) if j < TILES - 1 else (0, n + 1)))
                        pool.wait_ge(inv_done, n * 4 + j + 1)
                        pr = prob[j % 2][:, :, :, :]
                        nc.gpsimd.tensor_tensor(
                            pr, pr, rinv[:, :, :].rearrange("p q (s o) -> p q s o", o=1).broadcast_to([P, PAIRS, 2, KEYS]),
                            ALU.mult).then_inc(prob_done, 1)
                        if j == 1:
                            split_lo(bass.ds((n // BATCH + 1) % 2, 1), bass.ds((n % BATCH) * WCHUNK, WCHUNK), n + 1 + BATCH)
                if prev:
                    seq = bass.ds((n - 1) % BATCH, 1)
                    pool.wait_ge(act_free, ACT_FREE.at(n, "down'"))
                    nc.gpsimd.tensor_tensor(resT[:, seq, :], xc[:, :].rearrange("p (o t) -> p o t", o=1),
                                            x1[:, :].rearrange("p (o t) -> p o t", o=1), ALU.add).then_inc(res_done, 1)
                    if cur:
                        load_vec(bass.ds(n // BATCH, 1))
            pipelined(pool, nc.gpsimd, body)

        @block.vector
        def _(dve):
            dve.wait_ge(zeroed, 6)
            dve.wait_ge(consts_in, 16)

            def stage_lo(seq, half, count):
                for i, (rows, col, tok, width) in enumerate(stage[half]):
                    dve.wait_ge(x_hi_done, count + i + 1)
                    nc.vector.tensor_tensor(xa_lo[rows, col:col + width], resT[rows, seq, tok:tok + width],
                                            xa_hi[rows, col:col + width].bitcast(f32), ALU.subtract).then_inc(x_lo_done, 1)

            stage_lo(slice(0, 1), 0, 0)

            def body(n, cur, prev):
                m = n - 1
                def norms_of(j, q, layer_norm=False):
                    for c in range(2):
                        dve.wait_ge(sq_done, q * 8 + 2 * j + c + 1)
                        nc.vector.tensor_reduce(sums[:, c * HEADS:(c + 1) * HEADS],
                                                squares[:, :].rearrange("p (h d) -> p h d", h=HEADS),
                                                AX.X, ALU.add).then_inc(ss_done, 1)
                    dve.wait_ge(ss_done, q * 8 + 2 * j + 2)
                    ss = sums[:, 0:2 * HEADS]
                    nc.vector.tensor_scalar(ss, ss, 1e-24, None, ALU.max).then_inc(clamp_done, 1)
                    if layer_norm:
                        variance()
                    dve.wait_ge(clamp_done, q * 4 + j + 1)
                    w = 2 * HEADS + (TILES if layer_norm else 0)
                    rsqrt(nc, dve, sums[:, 0:w], rnorm[:, 0:w], rtmp[:, 0:w], rn_done, (q * 4 + j) * RSQRT_STEPS)
                    if layer_norm:
                        spread()

                def variance():
                    dve.wait_ge(fill, FILL.at(n, "var'"))
                    nc.vector.tensor_scalar(sums[:, 2 * HEADS:], ring[bank_of("var'")][:, 0:TILES], 1e-5, None, ALU.add)\
                      .then_inc(dve_free, 1)
                    dve.wait_ge(dve_free, DVE_FREE.at(n, "var'"))

                def spread():
                    nc.vector.tensor_copy(dev, rnorm[:, 2 * HEADS:].rearrange("p (t o) -> p t o", o=1).broadcast_to([P, TILES, P]))\
                      .then_inc(spread_done, 1)

                def r3(ap):
                    return ap.rearrange("p (o t) -> p o t", o=1)

                def normalise(c, j, q):
                    u = q * 8 + 2 * j + c
                    need(dve, rs_done, u - 1)
                    nc.vector.tensor_tensor(
                        qkn[:, c, :].rearrange("p (h d) -> p h d", h=HEADS),
                        proj[c][:, :].rearrange("p (h d) -> p h d", h=HEADS),
                        rnorm[:, c * HEADS:(c + 1) * HEADS].rearrange("p (h o) -> p h o", o=1).broadcast_to([P, HEADS, HDIM]),
                        ALU.mult).then_inc(qkn_done, 1)

                def straight_half(c, j, q):
                    if j == 0 and c == 0:
                        dve.wait_ge(rope_done, q * 3 + 3)
                    dve.wait_ge(qkn_done, q * 8 + 2 * j + c + 1)
                    nc.vector.tensor_tensor(
                        rc[:, c, :].rearrange("p (h d) -> p h d", h=HEADS),
                        qkn[:, c, :].rearrange("p (h d) -> p h d", h=HEADS),
                        rope[:, 0, j, c:c + 1, :].broadcast_to([P, HEADS, HDIM]), ALU.mult).then_inc(rc_done, 1)

                def add_halves(c, j, q):
                    dve.wait_ge(rs_done, q * 8 + 2 * j + c + 1)
                    dve.wait_ge(rc_done, q * 8 + 2 * j + c + 1)
                    nc.vector.tensor_tensor(rc[:, c, :], rc[:, c, :], rs[:, c, :], ALU.add).then_inc(add_done, 1)

                def add_attention(i):
                    dve.wait_ge(fill, FILL.at(n, f"wo{i}'"))

                    def part(ap):
                        return ap.rearrange("p o (t i k) -> p (o t) i k", t=TILES, i=2)[:, :, i, :]
                    nc.vector.tensor_tensor(part(r3(x1[:, :])),
                                            ring[bank_of(f"wo{i}'")][:, 0:TOKENS // 2].rearrange("p (t k) -> p t k", t=TILES),
                                            part(resT[:, seq, :]), ALU.add).then_inc(dve_free, 1)

                if isinstance(n, int) and n == 0:
                    norms_of(0, 0)
                    for c in range(2):
                        normalise(c, 0, 0)
                        straight_half(c, 0, 0)
                    for c in range(2):
                        add_halves(c, 0, 0)
                seq = bass.ds(m % BATCH, 1)
                for j in range(TILES):
                    ahead = (j + 1, n) if j < TILES - 1 else (0, n + 1)
                    if prev and j == 1 and not cur:
                        dve.wait_ge(res_done, n - 1)
                        add_attention(0)
                        add_attention(1)
                    if prev and cur and j == 1:
                        add_attention(0)
                    if cur:
                        norms_of(*ahead, j == 2 and prev)
                    if prev and cur and j == 1:
                        add_attention(1)
                    if cur and j == 0:
                        stage_lo(bass.ds(n % BATCH, 1), 1, 2 + n * 4)
                    if cur and j == 2:
                        stage_lo(bass.ds((n + 1) % BATCH, 1), 0, 4 + n * 4)
                    if prev and not cur and j == 2:
                        variance()
                        rsqrt(nc, dve, sums[:, 2 * HEADS:], rnorm[:, 2 * HEADS:], rtmp[:, 2 * HEADS:], rn_done,
                              (n * 4 + 1) * RSQRT_STEPS)
                        spread()
                    if cur:
                        dve.wait_ge(scr_full, n * 4 + j + 1)
                        nc.vector.tensor_reduce(rmax[:, :, :], scr[:, :, :, :], AX.X, ALU.max).then_inc(max_done, 1)
                        dve.wait_ge(max_done, n * 4 + j + 1)
                        nc.vector.tensor_tensor(
                            prob[j % 2][:, :, :, :].rearrange("p q s k -> p s q k"), scr[:, :, :, :],
                            rmax[:, :, :].rearrange("p s (q o) -> p s q o", o=1).broadcast_to([P, 2, PAIRS, KEYS]),
                            ALU.subtract).then_inc(sub_done, 1)
                    if prev and j == 1:
                        dve.wait_ge(fill, FILL.at(n, "mean'"))
                        nc.vector.tensor_tensor(xc[:, :], xs[:, :], ring[bank_of("mean'")][:, :], ALU.subtract).then_inc(dve_free, 1)
                    if prev and j == 2:
                        dve.wait_ge(fill, FILL.at(n, "spread'"))
                        nc.vector.tensor_tensor(xc[:, :], xc[:, :], ring[bank_of("spread'")][:, :], ALU.mult).then_inc(dve_free, 1)
                    if prev and j == 3:
                        for i in range(3):
                            w = FFC[i][1]
                            name = f"up{3 + i}'"
                            dve.wait_ge(act_free, ACT_FREE.at(n, f"up{i}'"))
                            dve.wait_ge(fill, FILL.at(n, name))
                            nc.vector.scalar_tensor_tensor(hid[0:w, i, :], ring[bank_of(name)][0:w, :], vec[0:w, 3 + i:4 + i],
                                                           hid[0:w, i, :], ALU.add, ALU.mult).then_inc(dve_free, 1)
                    if cur:
                        dve.wait_ge(rn_done, (ahead[1] * 4 + ahead[0] + 1) * RSQRT_STEPS)
                        normalise(0, *ahead)
                        dve.wait_ge(exp_done, n * 4 + j + 1)
                        nc.vector.tensor_reduce(rsum[:, :, :], prob[j % 2][:, :, :, :], AX.X, ALU.add).then_inc(sum_done, 1)
                    if cur:
                        normalise(1, *ahead)
                        dve.wait_ge(sum_done, n * 4 + j + 1)
                        need(dve, prob_done, n * 4 + j)
                        nc.vector.reciprocal(rinv[:, :, :], rsum[:, :, :]).then_inc(inv_done, 1)
                        for c in range(2):
                            dve.wait_ge(fill, FILL.at(n, f"T{j}{2 + c}"))
                            straight_half(c, *ahead)
                    if cur:
                        for c in range(2):
                            add_halves(c, *ahead)
            pipelined(dve, nc.vector, body)


def part_c(nc, out, alloc, need, x_attended, resT, ident, mod):
    f32 = mybir.dt.float32
    ALU, ACT = mybir.AluOpType, mybir.ActivationFunctionType
    ctx = ExitStack()
    with ctx:
        sb, ps, sem = alloc(ctx)
        yt = [ps(f"yt{i}", [P, TOKENS]) for i in range(2)]
        xtok = sb("xtok_c", [P, BATCH * TILES, DIM])
        x_back = sem("x_back"); scaled = sem("scaled"); turned = sem("turned"); added = sem("added"); stored = sem("stored")
        block = ctx.enter_context(nc.Block())
        ov = out.rearrange("b (t p) d -> p b t d", p=P)

        @block.scalar
        def _(act):
            for b in range(BATCH):
                nc.scalar.activation(resT[:, b, :], resT[:, b, :], ACT.Copy, scale=mod[:, 5, b:b + 1]).then_inc(scaled, 1)

        @block.tensor
        def _(pe):
            for b in range(BATCH):
                pe.wait_ge(scaled, b + 1)
                need(pe, added, b - 1)
                for j in range(TILES):
                    last = nc.tensor.transpose(yt[b % 2][:, j * P:(j + 1) * P], resT[:, b, j * P:(j + 1) * P], ident[:, :])
                last.then_inc(turned, 1)

        @block.vector
        def _(dve):
            for b in range(BATCH):
                dve.wait_ge(x_back, 16 * BATCH)
                dve.wait_ge(turned, b + 1)
                xb = xtok[:, b * TILES:(b + 1) * TILES, :]
                nc.vector.tensor_tensor(xb, yt[b % 2][:, :].rearrange("p (t f) -> p t f", t=TILES), xb, ALU.add).then_inc(added, 1)

        @block.sync
        def _(sp):
            for b in range(BATCH):
                tiles = slice(b * TILES, (b + 1) * TILES)
                sp.dma_start(xtok[:, tiles, :], x_attended[:, tiles, :]).then_inc(x_back, 16)
            for b in range(BATCH):
                sp.wait_ge(added, b + 1)
                sp.dma_start(ov[:, b, :, :], xtok[:, b * TILES:(b + 1) * TILES, :]).then_inc(stored, 16)
            sp.wait_ge(stored, 16 * BATCH)


_INS = ['L0_attn_x', 'L0_attn_Wq', 'L0_attn_Wk', 'L0_attn_Wv', 'L0_attn_Wo', 'L0_ffn_Wqkv', 'L0_ffn_q_scale',
        'L0_ffn_k_scale', 'L0_ffn_Wo', 'L0_ffn_ln_g', 'L0_ffn_ln_b', 'L0_ffn_W1', 'L0_ffn_b1', 'L0_ffn_W2',
        'L0_ffn_b2', 'L0_c', 'L0_wmod']


def kernel(**inputs):
    import numpy as _np
    import concourse.bacc as _bacc
    from concourse import mybir as _mybir
    from concourse.bass_utils import run_bass_kernel_spmd as _run

    nc = _bacc.Bacc("TRN2", target_bir_lowering=False, num_devices=1)
    arrays, args = {}, {}
    given = {name: _np.ascontiguousarray(inputs[name]) for name in _INS}
    given.update(constants())
    for name, a in given.items():
        arrays[f"in_{name}"] = a
        args[name] = nc.dram_tensor(f"in_{name}", a.shape, _mybir.dt.from_np(a.dtype), kind="ExternalInput").ap()
    o = nc.dram_tensor("out_0", (BATCH, TOKENS, DIM), _mybir.dt.float32, kind="ExternalOutput").ap()
    program(nc, args, o)
    r = _run(nc, [arrays], core_ids=[0])
    return r.results[0]["out_0"]
```
